# Optimizing a Trainium2 kernel written in Bass

```python
import numpy as np
import jax
import jax.numpy as jnp

def _softmax(x, axis=-1):
    return jax.nn.softmax(x, axis=axis)

def _gelu(x):
    return jax.nn.gelu(x, approximate=True)

def _silu(x):
    return jax.nn.silu(x)

def _sigmoid(x):
    return jax.nn.sigmoid(x)

def _layernorm(x, axis=-1, eps=1e-05):
    m = jnp.mean(x, axis=axis, keepdims=True)
    v = jnp.var(x, axis=axis, keepdims=True)
    return (x - m) / jnp.sqrt(v + eps)

def _scatter_add(tgt, idx, src, axis=0):
    return tgt.at[idx].add(src)

def _segment_sum(src, seg, n):
    return jax.ops.segment_sum(src, seg, n)
kernel_name = 'mk_macaron_d1_jaxref_r4_82be6f'

def setup_inputs(seed: int=0):
    np.random.seed(seed)
    _w = jnp.asarray

    def _L0_attn_setup():
        import jax, jax.numpy as jnp
        import numpy as np
        from math import sqrt
        EMBED = 256
        HEADS = 16
        key = jax.random.key(seed)
        k1, k2, k3, k4, k5 = jax.random.split(key, 5)
        x = jax.random.normal(k1, (2, 512, EMBED), dtype=jnp.float32)
        s = 1.0 / sqrt(EMBED)
        W_qkv = jax.random.normal(k2, (EMBED, 3 * EMBED), dtype=jnp.float32) * s
        b_qkv = jax.random.normal(k3, (3 * EMBED,), dtype=jnp.float32) * 0.01
        W_out = jax.random.normal(k4, (EMBED, EMBED), dtype=jnp.float32) * s
        b_out = jax.random.normal(k5, (EMBED,), dtype=jnp.float32) * 0.01
        return {'x': x, 'W_qkv': W_qkv, 'b_qkv': b_qkv, 'W_out': W_out, 'b_out': b_out}
    _L0_attn_in = _L0_attn_setup()

    def _L0_ffn_setup():
        import jax, jax.numpy as jnp
        import numpy as np
        B, T, D = (8, 1024, 256)
        NUM_SLOTS = 64
        TOP_K = 8
        DQ = D // 4
        DH = D // 2

        def _forward(x, slot_init, w1, b1, w2, b2, tau, Wih, Whh, bih, bhh, wq, bq, wk, bk, wv, bv, ln_g, ln_b, wvp, bvp, wo, bo):
            Bx, Tx, Dx = x.shape
            S = jnp.broadcast_to(slot_init[None], (Bx, NUM_SLOTS, Dx)).astype(x.dtype)
            slot_mean = jnp.broadcast_to(S.mean(axis=1, keepdims=True), (Bx, Tx, Dx))
            ctx = jnp.concatenate([x, slot_mean], axis=-1)
            h = jax.nn.gelu(ctx @ w1 + b1, approximate=False)
            route_logits = (h @ w2 + b2) / (jnp.abs(tau) + 0.1)
            topk_vals, topk_idx = jax.lax.top_k(route_logits, TOP_K)
            topk_w = jax.nn.softmax(topk_vals, axis=-1)
            alpha = (jax.nn.one_hot(topk_idx, NUM_SLOTS, dtype=x.dtype) * topk_w[..., None]).sum(axis=-2)
            slot_input = jnp.einsum('bts,btd->bsd', alpha, x)
            denom = alpha.sum(axis=1) + 1e-08
            si = slot_input / denom[..., None]
            gi = si @ Wih.T + bih
            gh = S @ Whh.T + bhh
            i_r, i_z, i_n = jnp.split(gi, 3, axis=-1)
            h_r, h_z, h_n = jnp.split(gh, 3, axis=-1)
            r = jax.nn.sigmoid(i_r + h_r)
            z = jax.nn.sigmoid(i_z + h_z)
            n = jnp.tanh(i_n + r * h_n)
            S_new = (1.0 - z) * n + z * S
            q = S_new @ wq + bq
            k = S_new @ wk + bk
            v = S_new @ wv + bv
            scale = DQ ** (-0.5)
            attn = jax.nn.softmax(jnp.einsum('bsq,btq->bst', q, k) * scale, axis=-1)
            S_comm = jnp.einsum('bst,btd->bsd', attn, v)
            y = S_new + S_comm
            mu = y.mean(axis=-1, keepdims=True)
            var = y.var(axis=-1, keepdims=True)
            y = (y - mu) * jax.lax.rsqrt(var + 1e-05) * ln_g + ln_b
            slot_values = y @ wvp + bvp
            out = jnp.einsum('bts,bsd->btd', alpha, slot_values)
            return out @ wo + bo
        key = jax.random.key(seed)
        ks = jax.random.split(key, 24)
        n = lambda k, shp, s=0.02: jax.random.normal(k, shp, dtype=jnp.float32) * s
        return {'x': jax.random.normal(ks[0], (B, T, D), dtype=jnp.float32), 'slot_init': n(ks[1], (NUM_SLOTS, D)), 'w1': n(ks[2], (2 * D, DH)), 'b1': jnp.zeros((DH,)), 'w2': n(ks[3], (DH, NUM_SLOTS)), 'b2': jnp.zeros((NUM_SLOTS,)), 'tau': jnp.ones((1,)), 'Wih': n(ks[4], (3 * D, D)), 'Whh': n(ks[5], (3 * D, D)), 'bih': jnp.zeros((3 * D,)), 'bhh': jnp.zeros((3 * D,)), 'wq': n(ks[6], (D, DQ)), 'bq': jnp.zeros((DQ,)), 'wk': n(ks[7], (D, DQ)), 'bk': jnp.zeros((DQ,)), 'wv': n(ks[8], (D, D)), 'bv': jnp.zeros((D,)), 'ln_g': jnp.ones((D,)), 'ln_b': jnp.zeros((D,)), 'wvp': n(ks[9], (D, D)), 'bvp': jnp.zeros((D,)), 'wo': n(ks[10], (D, D)), 'bo': jnp.zeros((D,))}
    _L0_ffn_in = _L0_ffn_setup()
    _d = {'L0_attn_x': _L0_attn_in['x'], 'L0_attn_W_qkv': _L0_attn_in['W_qkv'], 'L0_attn_b_qkv': _L0_attn_in['b_qkv'], 'L0_attn_W_out': _L0_attn_in['W_out'], 'L0_attn_b_out': _L0_attn_in['b_out'], 'L0_ffn_slot_init': _L0_ffn_in['slot_init'], 'L0_ffn_w1': _L0_ffn_in['w1'], 'L0_ffn_b1': _L0_ffn_in['b1'], 'L0_ffn_w2': _L0_ffn_in['w2'], 'L0_ffn_b2': _L0_ffn_in['b2'], 'L0_ffn_tau': _L0_ffn_in['tau'], 'L0_ffn_Wih': _L0_ffn_in['Wih'], 'L0_ffn_Whh': _L0_ffn_in['Whh'], 'L0_ffn_bih': _L0_ffn_in['bih'], 'L0_ffn_bhh': _L0_ffn_in['bhh'], 'L0_ffn_wq': _L0_ffn_in['wq'], 'L0_ffn_bq': _L0_ffn_in['bq'], 'L0_ffn_wk': _L0_ffn_in['wk'], 'L0_ffn_bk': _L0_ffn_in['bk'], 'L0_ffn_wv': _L0_ffn_in['wv'], 'L0_ffn_bv': _L0_ffn_in['bv'], 'L0_ffn_ln_g': _L0_ffn_in['ln_g'], 'L0_ffn_ln_b': _L0_ffn_in['ln_b'], 'L0_ffn_wvp': _L0_ffn_in['wvp'], 'L0_ffn_bvp': _L0_ffn_in['bvp'], 'L0_ffn_wo': _L0_ffn_in['wo'], 'L0_ffn_bo': _L0_ffn_in['bo']}
    _x0 = _d['L0_attn_x']
    _d['L0_attn_x'] = jax.random.normal(jax.random.fold_in(jax.random.key(seed), 1), (16, 1024, 256), dtype=_x0.dtype)
    del _x0
    return _d

def reference(L0_attn_x, L0_attn_W_qkv, L0_attn_b_qkv, L0_attn_W_out, L0_attn_b_out, L0_ffn_slot_init, L0_ffn_w1, L0_ffn_b1, L0_ffn_w2, L0_ffn_b2, L0_ffn_tau, L0_ffn_Wih, L0_ffn_Whh, L0_ffn_bih, L0_ffn_bhh, L0_ffn_wq, L0_ffn_bq, L0_ffn_wk, L0_ffn_bk, L0_ffn_wv, L0_ffn_bv, L0_ffn_ln_g, L0_ffn_ln_b, L0_ffn_wvp, L0_ffn_bvp, L0_ffn_wo, L0_ffn_bo):

    def _L0_attn_ref(x, W_qkv, b_qkv, W_out, b_out):
        import jax, jax.numpy as jnp
        import numpy as np
        from math import sqrt
        EMBED = 256
        HEADS = 16
        B, N, E = x.shape
        H = HEADS
        d = E // H
        qkv = x @ W_qkv + b_qkv
        q, k, v = jnp.split(qkv, 3, axis=2)
        q = q.reshape(B, N, H, d)
        k = k.reshape(B, N, H, d)
        v = v.reshape(B, N, H, d)
        energy = jnp.einsum('bqhe,bkhe->bqhk', q, k)
        attn = jax.nn.softmax(energy, axis=-1) / sqrt(E)
        out = jnp.einsum('bihv,bvhd->bihd', attn, v)
        out = out.reshape(B, N, E)
        return out @ W_out + b_out

    def _L0_ffn_ref(x, slot_init, w1, b1, w2, b2, tau, Wih, Whh, bih, bhh, wq, bq, wk, bk, wv, bv, ln_g, ln_b, wvp, bvp, wo, bo):
        import jax, jax.numpy as jnp
        import numpy as np
        B, T, D = (8, 1024, 256)
        NUM_SLOTS = 64
        TOP_K = 8
        DQ = D // 4
        DH = D // 2

        def _forward(x, slot_init, w1, b1, w2, b2, tau, Wih, Whh, bih, bhh, wq, bq, wk, bk, wv, bv, ln_g, ln_b, wvp, bvp, wo, bo):
            Bx, Tx, Dx = x.shape
            S = jnp.broadcast_to(slot_init[None], (Bx, NUM_SLOTS, Dx)).astype(x.dtype)
            slot_mean = jnp.broadcast_to(S.mean(axis=1, keepdims=True), (Bx, Tx, Dx))
            ctx = jnp.concatenate([x, slot_mean], axis=-1)
            h = jax.nn.gelu(ctx @ w1 + b1, approximate=False)
            route_logits = (h @ w2 + b2) / (jnp.abs(tau) + 0.1)
            topk_vals, topk_idx = jax.lax.top_k(route_logits, TOP_K)
            topk_w = jax.nn.softmax(topk_vals, axis=-1)
            alpha = (jax.nn.one_hot(topk_idx, NUM_SLOTS, dtype=x.dtype) * topk_w[..., None]).sum(axis=-2)
            slot_input = jnp.einsum('bts,btd->bsd', alpha, x)
            denom = alpha.sum(axis=1) + 1e-08
            si = slot_input / denom[..., None]
            gi = si @ Wih.T + bih
            gh = S @ Whh.T + bhh
            i_r, i_z, i_n = jnp.split(gi, 3, axis=-1)
            h_r, h_z, h_n = jnp.split(gh, 3, axis=-1)
            r = jax.nn.sigmoid(i_r + h_r)
            z = jax.nn.sigmoid(i_z + h_z)
            n = jnp.tanh(i_n + r * h_n)
            S_new = (1.0 - z) * n + z * S
            q = S_new @ wq + bq
            k = S_new @ wk + bk
            v = S_new @ wv + bv
            scale = DQ ** (-0.5)
            attn = jax.nn.softmax(jnp.einsum('bsq,btq->bst', q, k) * scale, axis=-1)
            S_comm = jnp.einsum('bst,btd->bsd', attn, v)
            y = S_new + S_comm
            mu = y.mean(axis=-1, keepdims=True)
            var = y.var(axis=-1, keepdims=True)
            y = (y - mu) * jax.lax.rsqrt(var + 1e-05) * ln_g + ln_b
            slot_values = y @ wvp + bvp
            out = jnp.einsum('bts,bsd->btd', alpha, slot_values)
            return out @ wo + bo
        return _forward(x, slot_init, w1, b1, w2, b2, tau, Wih, Whh, bih, bhh, wq, bq, wk, bk, wv, bv, ln_g, ln_b, wvp, bvp, wo, bo)
    x = L0_attn_x
    x = x + 0.5 * _L0_ffn_ref(_layernorm(x, axis=-1), L0_ffn_slot_init, L0_ffn_w1, L0_ffn_b1, L0_ffn_w2, L0_ffn_b2, L0_ffn_tau, L0_ffn_Wih, L0_ffn_Whh, L0_ffn_bih, L0_ffn_bhh, L0_ffn_wq, L0_ffn_bq, L0_ffn_wk, L0_ffn_bk, L0_ffn_wv, L0_ffn_bv, L0_ffn_ln_g, L0_ffn_ln_b, L0_ffn_wvp, L0_ffn_bvp, L0_ffn_wo, L0_ffn_bo)
    x = x + _L0_attn_ref(_layernorm(x, axis=-1), L0_attn_W_qkv, L0_attn_b_qkv, L0_attn_W_out, L0_attn_b_out)
    x = x + 0.5 * _L0_ffn_ref(_layernorm(x, axis=-1), L0_ffn_slot_init, L0_ffn_w1, L0_ffn_b1, L0_ffn_w2, L0_ffn_b2, L0_ffn_tau, L0_ffn_Wih, L0_ffn_Whh, L0_ffn_bih, L0_ffn_bhh, L0_ffn_wq, L0_ffn_bq, L0_ffn_wk, L0_ffn_bk, L0_ffn_wv, L0_ffn_bv, L0_ffn_ln_g, L0_ffn_ln_b, L0_ffn_wvp, L0_ffn_bvp, L0_ffn_wo, L0_ffn_bo)
    return x

_drawn_inputs = setup_inputs


def setup_inputs(seed=0):
    import zlib

    import numpy as np

    out = dict(_drawn_inputs(seed))
    spreads = {'L0_ffn_b1': (0.0, 0.8),
     'L0_ffn_b2': (0.0, 0.8),
     'L0_ffn_bih': (0.0, 0.1),
     'L0_ffn_bhh': (0.0, 0.432),
     'L0_ffn_bq': (0.0, 2.0),
     'L0_ffn_bk': (0.0, 2.0),
     'L0_ffn_bv': (0.0, 0.1),
     'L0_ffn_ln_g': (1.0, 0.6),
     'L0_ffn_ln_b': (0.0, 0.8),
     'L0_ffn_bvp': (0.0, 0.1),
     'L0_ffn_bo': (0.0, 0.1)}
    factors = {'L0_attn_b_qkv': 55.081,
     'L0_attn_b_out': 5.844,
     'L0_ffn_slot_init': 8.0,
     'L0_ffn_w1': 8.0,
     'L0_ffn_w2': 8.0,
     'L0_ffn_Wih': 7.372,
     'L0_ffn_Whh': 8.0,
     'L0_ffn_wq': 35.914,
     'L0_ffn_wk': 8.0,
     'L0_ffn_wv': 3.586}
    for name, (base, spread) in spreads.items():
        noise = np.random.default_rng([zlib.crc32(name.encode()), seed]).standard_normal(out[name].shape)
        drawn = base * np.exp(spread * noise) if base else spread * noise
        out[name] = jnp.asarray(drawn.astype(out[name].dtype))
    for name, factor in factors.items():
        out[name] = (out[name] * factor).astype(out[name].dtype)
    return out
```

```python
from contextlib import ExitStack

import concourse.bass as bass
from concourse import mybir

F32 = mybir.dt.float32
BF16 = mybir.dt.bfloat16
ALU = mybir.AluOpType
ACT = mybir.ActivationFunctionType
AX = mybir.AxisListType

P = 128
HALF = 512
EPS = 1e-5
NEG = -3.0e38


class Consts:
    pass


def clear(nc, sems):
    nums = sorted(s.num for s in sems)
    starts = [n for n in nums if n - 1 not in nums]
    with nc.Block() as block:
        @block.sync
        def _(sp):
            for n in starts:
                end = n
                while end in nums:
                    end += 1
                sp.sem_clear(range(n, end))


def build_setup(nc, ctx, d):
    D, F = d["L0_ffn_w1"].shape[0] // 2, d["L0_ffn_w1"].shape[1]
    S = d["L0_ffn_slot_init"].shape[0]
    G3 = d["L0_ffn_Wih"].shape[0]
    KT, MT = D // P, G3 // P
    c = Consts()
    c.D, c.F, c.S, c.G3, c.KT, c.MT = D, F, S, G3, KT, MT

    def sb(name, shape, dt=F32):
        return ctx.enter_context(nc.sbuf_tensor(name, shape, dt))

    c.ident = sb("ident", [P, P])
    c.ones = sb("ones", [P, P])
    c.neg_half = sb("neg_half", [P, 8])
    c.w1 = sb("w1", [P, KT, F])
    c.hid_bias = sb("hid_bias", [P, 1])
    c.w2 = sb("w2", [P, S])
    c.b2 = sb("b2", [P, S])
    c.wih_t = sb("wih_t", [P, KT, G3])
    c.gate_bias = sb("gate_bias", [P, MT])
    c.gh_t = sb("gh_t", [P, MT, S])
    c.slots_t = sb("slots_t", [P, KT, S])
    c.wq = sb("wq", [P, KT, S])
    c.wk = sb("wk", [P, KT, S])
    c.bq = sb("bq", [S, 1])
    c.bk = sb("bk", [S, 1])
    c.wv = sb("wv", [P, KT, D])
    c.bv = sb("bv", [P, D])
    c.ln_g = sb("ln_g", [P, KT])
    c.ln_b = sb("ln_b", [P, KT])
    c.wvp = sb("wvp", [P, KT, D])
    c.bvp = sb("bvp", [P, KT])
    c.wo = sb("wo", [P, KT, D])

    with ExitStack() as own:
        def tmp(name, shape, dt=F32):
            return own.enter_context(nc.sbuf_tensor(name, shape, dt))

        def sem(name):
            return ctx.enter_context(nc.semaphore(name))

        w1_mean = tmp("w1_mean", [P, KT, F])
        wih = tmp("wih", [P, MT, D])
        whh = tmp("whh", [P, MT, D])
        whh_t = tmp("whh_t", [P, KT, G3])
        hh_bias = tmp("hh_bias", [P, MT])
        both_bias = tmp("both_bias", [P, MT])
        slots = tmp("slots", [S, D])
        slot_sum = tmp("slot_sum", [P, KT])
        slot_mean = tmp("slot_mean", [P, KT])
        b1 = tmp("b1", [P, 1])
        tau = tmp("tau", [P, 1])
        tau_neg = tmp("tau_neg", [P, 1])
        tau_abs = tmp("tau_abs", [P, 1])
        tau_den = tmp("tau_den", [P, 1])
        tau_inv = tmp("tau_inv", [P, 1])
        w2_raw = tmp("w2_raw", [P, S])
        b2_raw = tmp("b2_raw", [P, S])
        ps = own.enter_context(nc.psum_tensor("ps_setup", [P, 8, HALF], F32))

        loaded = sem("setup_loaded")
        loaded_act = sem("setup_loaded_act")
        filled = sem("setup_filled")
        ident_ready = sem("ident_ready")
        turned = sem("setup_turned")
        copied = sem("setup_copied")
        slots_taken = sem("setup_slots_taken")
        mean_ready = sem("slot_mean_ready")
        product_ready = sem("setup_product_ready")
        tau_step = sem("tau_step")
        bias_step = sem("bias_step")

        block = own.enter_context(nc.Block())
        n_sync, n_act = [], []

        @block.sync
        def _(sp):
            def load(dst, src):
                sp.dma_start(dst, src).then_inc(loaded, 16)
                n_sync.append(1)
            load(wih[:, :, :], d["L0_ffn_Wih"].rearrange("(m p) d -> p m d", p=P))
            load(whh[:, :, :], d["L0_ffn_Whh"].rearrange("(m p) d -> p m d", p=P))
            load(slots[:, :], d["L0_ffn_slot_init"])
            load(c.w1[:, :, :], d["L0_ffn_w1"][0:D, :].rearrange("(k p) f -> p k f", p=P))
            load(w1_mean[:, :, :], d["L0_ffn_w1"][D:2 * D, :].rearrange("(k p) f -> p k f", p=P))
            load(w2_raw[:, :], d["L0_ffn_w2"])
            load(b2_raw[:, :], d["L0_ffn_b2"].partition_broadcast(P))
            load(tau[:, :], d["L0_ffn_tau"].partition_broadcast(P))
            load(b1[:, :], d["L0_ffn_b1"].rearrange("(p o) -> p o", o=1))
            load(c.gate_bias[:, :], d["L0_ffn_bih"].rearrange("(m p o) -> p m o", p=P, o=1))
            load(hh_bias[:, :], d["L0_ffn_bhh"].rearrange("(m p o) -> p m o", p=P, o=1))

        @block.scalar
        def _(act):
            def load(dst, src):
                act.dma_start(dst, src).then_inc(loaded_act, 16)
                n_act.append(1)
            load(c.wq[:, :, :], d["L0_ffn_wq"].rearrange("(k p) f -> p k f", p=P))
            load(c.wk[:, :, :], d["L0_ffn_wk"].rearrange("(k p) f -> p k f", p=P))
            load(c.wv[:, :, :], d["L0_ffn_wv"].rearrange("(k p) f -> p k f", p=P))
            load(c.wvp[:, :, :], d["L0_ffn_wvp"].rearrange("(k p) f -> p k f", p=P))
            load(c.wo[:, :, :], d["L0_ffn_wo"].rearrange("(k p) f -> p k f", p=P))
            load(c.bv[:, :], d["L0_ffn_bv"].partition_broadcast(P))
            load(c.bq[:, :], d["L0_ffn_bq"].rearrange("(p o) -> p o", o=1))
            load(c.bk[:, :], d["L0_ffn_bk"].rearrange("(p o) -> p o", o=1))
            load(c.ln_g[:, :], d["L0_ffn_ln_g"].rearrange("(m p o) -> p m o", p=P, o=1))
            load(c.ln_b[:, :], d["L0_ffn_ln_b"].rearrange("(m p o) -> p m o", p=P, o=1))
            load(c.bvp[:, :], d["L0_ffn_bvp"].rearrange("(m p o) -> p m o", p=P, o=1))
            act.wait_ge(loaded_act, 16 * len(n_act))

        @block.gpsimd
        def _(pool):
            nc.gpsimd.memset(c.ident[:, :], 0.0).then_inc(filled, 1)
            pool.wait_ge(filled, 1)
            nc.gpsimd.affine_select(out=c.ident[:, :], in_=c.ident[:, :], compare_op=ALU.not_equal, fill=1.0,
                                    base=0, pattern=[[-1, P]], channel_multiplier=1).then_inc(ident_ready, 1)
            nc.gpsimd.memset(c.ones[:, :], 1.0).then_inc(filled, 1)
            nc.gpsimd.memset(c.neg_half[:, :], -0.5).then_inc(filled, 1)
            pool.wait_ge(filled, 3)

        groups = KT * MT * P // HALF

        @block.tensor
        def _(pe):
            pe.wait_ge(loaded, 16 * len(n_sync))
            pe.wait_ge(ident_ready, 1)
            for n, w in enumerate((wih, whh)):
                for g in range(groups):
                    for j in range(4):
                        k, m = divmod(4 * g + j, MT)
                        last = pe.transpose(ps[:, 3 * n + g, j * P:(j + 1) * P], w[:, m, k * P:(k + 1) * P],
                                            c.ident[:, :])
                    last.then_inc(turned, 1)
            for k in range(KT):
                last = pe.transpose(ps[:, 6, k * S:(k + 1) * S], slots[:, k * P:(k + 1) * P], c.ident[0:S, 0:S])
            last.then_inc(turned, 1)
            pe.wait_ge(mean_ready, 1)
            for k in range(KT):
                last = pe.matmul(ps[:, 7, 0:1], w1_mean[:, k, :], slot_mean[:, k:k + 1],
                                 start=(k == 0), stop=(k == KT - 1))
            last.then_inc(product_ready, 1)
            pe.wait_ge(copied, 2 * groups)
            for m in range(MT):
                for k in range(KT):
                    last = pe.matmul(ps[:, 0, m * S:(m + 1) * S], whh_t[:, k, m * P:(m + 1) * P],
                                     c.slots_t[:, k, :], start=(k == 0), stop=(k == KT - 1))
            last.then_inc(product_ready, 1)

        @block.vector
        def _(dve):
            dve.wait_ge(loaded, 16 * len(n_sync))
            dve.tensor_scalar(tau_neg[:, :], tau[:, :], -1.0, None, ALU.mult).then_inc(tau_step, 1)
            dve.wait_ge(tau_step, 1)
            dve.tensor_tensor(tau_abs[:, :], tau[:, :], tau_neg[:, :], ALU.max).then_inc(tau_step, 1)
            dve.wait_ge(tau_step, 2)
            dve.tensor_scalar(tau_den[:, :], tau_abs[:, :], 0.1, None, ALU.add).then_inc(tau_step, 1)
            dve.wait_ge(tau_step, 3)
            dve.reciprocal(tau_inv[:, :], tau_den[:, :]).then_inc(tau_step, 1)
            dve.wait_ge(tau_step, 4)
            dve.tensor_scalar(c.w2[:, :], w2_raw[:, :], tau_inv[:, 0:1], None, ALU.mult).then_inc(tau_step, 1)
            dve.tensor_scalar(c.b2[:, :], b2_raw[:, :], tau_inv[:, 0:1], None, ALU.mult).then_inc(tau_step, 1)
            dve.tensor_tensor(both_bias[:, :], c.gate_bias[:, :], hh_bias[:, :], ALU.add).then_inc(bias_step, 1)
            for n, w_t in enumerate((c.wih_t, whh_t)):
                flat = w_t[:, :, :].rearrange("p k g -> p (k g)")
                for g in range(groups):
                    dve.wait_ge(turned, 3 * n + g + 1)
                    dve.tensor_copy(flat[:, g * HALF:(g + 1) * HALF], ps[:, 3 * n + g, :]).then_inc(copied, 1)
            dve.wait_ge(turned, 2 * groups + 1)
            src = ps[:, 6, 0:KT * S].rearrange("p (k s) -> p k s", k=KT)
            dve.tensor_copy(c.slots_t[:, :, :], src).then_inc(slots_taken, 1)
            dve.wait_ge(slots_taken, 1)
            dve.tensor_reduce(slot_sum[:, :], c.slots_t[:, :, :], AX.X, ALU.add).then_inc(slots_taken, 1)
            dve.wait_ge(slots_taken, 2)
            dve.tensor_scalar(slot_mean[:, :], slot_sum[:, :], 1.0 / S, None, ALU.mult).then_inc(mean_ready, 1)
            dve.wait_ge(product_ready, 1)
            dve.tensor_tensor(c.hid_bias[:, :], ps[:, 7, 0:1], b1[:, :], ALU.add).then_inc(bias_step, 1)
            dve.wait_ge(product_ready, 2)
            dve.wait_ge(bias_step, 1)
            for m in range(MT):
                bias = both_bias if m < 2 * KT else hh_bias
                dve.tensor_scalar(c.gh_t[:, m, :], ps[:, 0, m * S:(m + 1) * S], bias[:, m:m + 1], None,
                                  ALU.add).then_inc(bias_step, 1)
            dve.wait_ge(bias_step, 2 + MT)
            dve.wait_ge(tau_step, 6)
    return c


def build_ffn(nc, c, tag, x_in, x_out, bo):
    B, T, D = x_in.shape
    S, KT, MT, F = c.S, c.KT, c.MT, c.F
    TT = T // P
    NS = B * S
    PAIRS = B // 2
    R = 4

    def rows(t, b):
        return t[bass.ds(b, 1)].rearrange("a (p t) d -> (a p) t d", t=TT)

    with ExitStack() as ctx:
        def sb(name, shape, dt=F32, on=ctx):
            return on.enter_context(nc.sbuf_tensor(f"{tag}_{name}", shape, dt))

        def sem(name):
            sems.append(ctx.enter_context(nc.semaphore(f"{tag}_{name}")))
            return sems[-1]

        sems = []
        alpha_t = sb("alpha_t", [S, B, T])
        si_t = sb("si_t", [P, KT, NS])
        slot_out = sb("slot_out", [P, PAIRS, D])

        with ExitStack() as own:
            x_ring = sb("x_ring", [P, R, TT, D], F32, own)
            stats = sb("stats", [P, TT, 6], F32, own)
            mean_var = sb("mean_var", [P, TT, 2], F32, own)
            waited = sb("waited", [P, 1], F32, own)
            var_eps = sb("var_eps", [P, TT], F32, own)
            rstd = sb("rstd", [P, TT], F32, own)
            xn_t = sb("xn_t", [P, KT, T], F32, own)
            hid = sb("hid", [P, T], F32, own)
            logit = sb("logit", [P, TT, S], F32, own)
            top8 = sb("top8", [P, TT, 8], F32, own)
            rest = sb("rest", [P, TT, S], F32, own)
            shifted = sb("shifted", [P, TT, S], F32, own)
            expd = sb("expd", [P, TT, S], F32, own)
            picked = sb("picked", [P, TT, S], F32, own)
            total = sb("total", [P, TT], F32, own)
            inv_total = sb("inv_total", [P, TT], F32, own)
            alpha = sb("alpha", [P, 2, TT, S], F32, own)
            den_eps = sb("den_eps", [P, S], F32, own)
            den_inv = sb("den_inv", [P, S], F32, own)
            ps_turn = own.enter_context(nc.psum_tensor(f"{tag}_ps_turn", [P, 2, HALF], F32))
            ps_hid = own.enter_context(nc.psum_tensor(f"{tag}_ps_hid", [P, 2, HALF], F32))
            ps_logit = own.enter_context(nc.psum_tensor(f"{tag}_ps_logit", [P, TT, S], F32))
            ps_si = own.enter_context(nc.psum_tensor(f"{tag}_ps_si", [P, 8, S], F32))
            ps_at = own.enter_context(nc.psum_tensor(f"{tag}_ps_at", [P, 2, HALF], F32))

            x_loaded = [sem(f"x_loaded{r}") for r in range(R)]
            stat_step = sem("stat_step")
            var_ready = sem("var_ready")
            rstd_ready = sem("rstd_ready")
            xn_ready = sem("xn_ready")
            turned = sem("turned")
            turn_taken = sem("turn_taken")
            hid_ready = sem("hid_ready")
            gelu_done = sem("gelu_done")
            logit_ready = sem("logit_ready")
            logit_taken = sem("logit_taken")
            top_step = sem("top_step")
            shift_ready = sem("shift_ready")
            exp_done = sem("exp_done")
            pick_step = sem("pick_step")
            alpha_ready = sem("alpha_ready")
            si_ready = sem("si_ready")
            at_ready = sem("at_ready")
            at_taken = sem("at_taken")
            den_step = sem("den_step")
            si_taken = sem("si_taken")

            block = own.enter_context(nc.Block())
            FILLS = KT * T // HALF

            def over_batches(eng, step):
                for r in range(R):
                    step(r, r, front=True, back=r > 0, peeled=True)
                with eng.Fori(1, B // R, 1) as q:
                    for r in range(R):
                        step(q * R + r, r, front=True, back=True, peeled=False)
                step(B, 0, front=False, back=True, peeled=False)

            @block.sync
            def _(sp):
                for r in range(2):
                    sp.dma_start(x_ring[:, r], rows(x_in, r)).then_inc(x_loaded[r], 16)

                def load(b, r):
                    if not isinstance(b, int) or b >= 2:
                        sp.wait_ge(si_ready, b - 1)
                    q = (r + 2) % R
                    sp.dma_start(x_ring[:, q], rows(x_in, b + 2)).then_inc(x_loaded[q], 16)
                for r in range(R):
                    load(r, r)
                with sp.Fori(1, B // R - 1, 1) as q:
                    for r in range(R):
                        load(q * R + r, r)
                for r in range(R - 2):
                    load(B - R + r, r)

            @block.gpsimd
            def _(pool):
                def rsqrt(b, r, front, back, peeled):
                    if not front:
                        return
                    pool.wait_ge(var_ready, b + 1)
                    pool.tensor_tensor(rstd[:, :], var_eps[:, :], c.neg_half[:, 0:TT], ALU.pow).then_inc(rstd_ready, 1)
                over_batches(pool, rsqrt)

            @block.vector
            def _(dve):
                def normalise(b, r):
                    base = b * (2 * TT)
                    dve.wait_ge(x_loaded[r], b * (16 // R) + (16 - r * (16 // R)))
                    for t in range(TT):
                        dve.bn_stats(stats[:, t, :], x_ring[:, r, t, :]).then_inc(stat_step, 1)
                    dve.wait_ge(stat_step, base + TT)
                    dve.memset(waited[:, :], 0.0)
                    for t in range(TT):
                        dve.bn_aggr(mean_var[:, t, :], stats[:, t, :]).then_inc(stat_step, 1)
                    dve.wait_ge(stat_step, base + 2 * TT)
                    dve.tensor_scalar(var_eps[:, :], mean_var[:, :, 1], EPS, None, ALU.add).then_inc(var_ready, 1)
                    dve.wait_ge(rstd_ready, b + 1)
                    for t in range(TT):
                        last = dve.tensor_scalar(x_ring[:, r, t, :], x_ring[:, r, t, :], mean_var[:, t, 0:1],
                                                 rstd[:, t:t + 1], ALU.subtract, ALU.mult)
                    last.then_inc(xn_ready, 1)

                def route(b, r):
                    dve.wait_ge(logit_ready, b + 1)
                    dve.tensor_tensor(logit[:, :, :], ps_logit[:, :, :], c.b2[:, :].unsqueeze(1).to_broadcast([P, TT, S]),
                                      ALU.add).then_inc(logit_taken, 1)
                    dve.wait_ge(logit_taken, b + 1)
                    n = b * (2 * TT)
                    dve.memset(waited[:, :], 0.0)
                    for t in range(TT):
                        dve.max(top8[:, t, :], logit[:, t, :]).then_inc(top_step, 1)
                    dve.wait_ge(top_step, n + TT)
                    dve.tensor_tensor(shifted[:, :, :], logit[:, :, :], top8[:, :, 0:1].to_broadcast([P, TT, S]),
                                      ALU.subtract).then_inc(shift_ready, 1)
                    for t in range(TT):
                        dve.match_replace(out=rest[:, t, :], in_to_replace=top8[:, t, :], in_values=logit[:, t, :],
                                          imm_value=NEG).then_inc(top_step, 1)
                    dve.wait_ge(top_step, n + 2 * TT)
                    dve.wait_ge(exp_done, b + 1)
                    dve.scalar_tensor_tensor(picked[:, :, :], rest[:, :, :], NEG, expd[:, :, :], ALU.is_equal,
                                             ALU.mult).then_inc(pick_step, 1)
                    dve.wait_ge(pick_step, b * 3 + 1)
                    dve.tensor_reduce(total[:, :], picked[:, :, :], AX.X, ALU.add).then_inc(pick_step, 1)
                    dve.wait_ge(pick_step, b * 3 + 2)
                    dve.reciprocal(inv_total[:, :], total[:, :]).then_inc(pick_step, 1)
                    dve.wait_ge(pick_step, b * 3 + 3)
                    if not isinstance(b, int) or b >= 2:
                        dve.wait_ge(at_ready, b - 1)
                    dve.tensor_tensor(alpha[:, r % 2], picked[:, :, :], inv_total[:, :].unsqueeze(2).to_broadcast([P, TT, S]),
                                      ALU.mult).then_inc(alpha_ready, 1)

                def slot_inputs(b):
                    dve.wait_ge(si_ready, b + 1)
                    dve.tensor_scalar(den_eps[:, :], ps_si[:, KT, :], 1e-8, None, ALU.add).then_inc(den_step, 1)
                    dve.wait_ge(den_step, b * 2 + 1)
                    dve.reciprocal(den_inv[:, :], den_eps[:, :]).then_inc(den_step, 1)
                    dve.wait_ge(den_step, b * 2 + 2)
                    dve.tensor_tensor(si_t[:, :, bass.ds(b * S, S)], ps_si[:, 0:KT, :],
                                      den_inv[:, :].unsqueeze(1).to_broadcast([P, KT, S]), ALU.mult).then_inc(si_taken, 1)

                normalise(0, 0)

                def step(b, r, front, back):
                    if back:
                        route(b - 1, (r - 1) % R)
                    if front:
                        normalise(b + 1, (r + 1) % R)
                    if back:
                        slot_inputs(b - 1)
                for r in range(R):
                    step(r, r, True, r > 0)
                with dve.Fori(1, B // R - 1, 1) as q:
                    for r in range(R):
                        step(q * R + r, r, True, True)
                for r in range(R):
                    step(B - R + r, r, r < R - 1, True)
                step(B, 0, False, True)

            @block.tensor
            def _(pe):
                def step(b, r, front, back, peeled):
                    if front:
                        pe.wait_ge(xn_ready, b + 1)
                        for f in range(FILLS):
                            if not (peeled and r == 0 and f < 2):
                                pe.wait_ge(turn_taken, b * FILLS + (f - 1))
                            for j in range(4):
                                k, t = divmod(4 * f + j, TT)
                                last = pe.transpose(ps_turn[:, f % 2, j * P:(j + 1) * P],
                                                    x_ring[:, r, t, k * P:(k + 1) * P], c.ident[:, :])
                            last.then_inc(turned, 1)
                        pe.wait_ge(turn_taken, b * FILLS + FILLS)
                        if not (peeled and r == 0):
                            pe.wait_ge(gelu_done, b)
                        for n in range(T // HALF):
                            for k in range(KT):
                                last = pe.matmul(ps_hid[:, n, :], c.w1[:, k, :], xn_t[:, k, n * HALF:(n + 1) * HALF],
                                                 start=(k == 0), stop=(k == KT - 1))
                        last.then_inc(hid_ready, 1)
                    if back:
                        pe.wait_ge(alpha_ready, b)
                        if not (peeled and r == 1):
                            pe.wait_ge(si_taken, b - 1)
                            pe.wait_ge(at_taken, b - 1)
                        q = (r - 1) % R
                        for k in range(KT):
                            for t in range(TT):
                                pe.matmul(ps_si[:, k, :], x_ring[:, q, t, k * P:(k + 1) * P], alpha[:, q % 2, t, :],
                                          start=(t == 0), stop=(t == TT - 1))
                        for t in range(TT):
                            last = pe.matmul(ps_si[:, KT, :], c.ones[:, :], alpha[:, q % 2, t, :],
                                             start=(t == 0), stop=(t == TT - 1))
                        last.then_inc(si_ready, 1)
                        for t in range(TT):
                            last = pe.transpose(ps_at[0:S, t // 4, (t % 4) * P:(t % 4 + 1) * P], alpha[:, q % 2, t, :],
                                                c.ident[:, :])
                        last.then_inc(at_ready, 1)
                    if front:
                        pe.wait_ge(gelu_done, b + 1)
                        if not (peeled and r == 0):
                            pe.wait_ge(logit_taken, b)
                        for t in range(TT):
                            last = pe.matmul(ps_logit[:, t, :], hid[:, t * P:(t + 1) * P], c.w2[:, :],
                                             start=True, stop=True)
                        last.then_inc(logit_ready, 1)
                over_batches(pe, step)

            @block.scalar
            def _(act):
                def step(b, r, front, back, peeled):
                    if back:
                        act.wait_ge(shift_ready, b)
                        act.activation(expd[:, :, :], shifted[:, :, :], ACT.Exp).then_inc(exp_done, 1)
                    if front:
                        flat = xn_t[:, :, :].rearrange("p k t -> p (k t)")
                        for f in range(FILLS):
                            act.wait_ge(turned, b * FILLS + (f + 1))
                            act.activation(flat[:, f * HALF:(f + 1) * HALF], ps_turn[:, f % 2, :],
                                           ACT.Identity).then_inc(turn_taken, 1)
                        act.wait_ge(hid_ready, b + 1)
                        if not (peeled and r == 0):
                            act.wait_ge(logit_ready, b)
                        act.activation(hid[:, :].rearrange("p (n h) -> p n h", n=2), ps_hid[:, :, :], ACT.Gelu,
                                       bias=c.hid_bias[:, 0:1]).then_inc(gelu_done, 1)
                    if back:
                        act.wait_ge(at_ready, b)
                        act.activation(alpha_t[:, bass.ds(b - 1, 1), :].rearrange("p a (n h) -> p (a n) h", n=2),
                                       ps_at[0:S, :, :], ACT.Identity).then_inc(at_taken, 1)
                over_batches(act, step)

        with ExitStack() as own:
            gates = sb("gates", [P, 2 * KT, NS], F32, own)
            pre = sb("pre", [P, KT, NS], F32, own)
            cand = sb("cand", [P, KT, NS], F32, own)
            mix = sb("mix", [P, KT, NS], F32, own)
            mix_z = sb("mix_z", [P, KT, NS], F32, own)
            new_t = sb("new_t", [P, KT, NS], F32, own)
            q_t = sb("q_t", [S, NS], F32, own)
            k_t = sb("k_t", [S, NS], F32, own)
            v_sb = sb("v_sb", [P, PAIRS, D], F32, own)
            s_max = sb("s_max", [P, PAIRS], F32, own)
            s_shift = sb("s_shift", [P, PAIRS, S], F32, own)
            s_exp = sb("s_exp", [P, PAIRS, S], F32, own)
            s_sum = sb("s_sum", [P, PAIRS], F32, own)
            s_inv = sb("s_inv", [P, PAIRS], F32, own)
            attn = sb("attn", [P, PAIRS, P], F32, own)
            attn_t = sb("attn_t", [P, PAIRS, P], F32, own)
            stats = sb("y_stats", [P, PAIRS, 6], F32, own)
            mean_var = sb("y_mean_var", [P, PAIRS, 2], F32, own)
            var_eps = sb("y_var_eps", [P, PAIRS], F32, own)
            rstd = sb("y_rstd", [P, PAIRS], F32, own)
            y_hat = sb("y_hat", [P, PAIRS, D], F32, own)
            y_t, val_t = pre, mix
            ps = own.enter_context(nc.psum_tensor(f"{tag}_ps_slot", [P, 8, HALF], F32))

            gi_ready, gate_sum = sem("gi_ready"), sem("gate_sum")
            tanh_done, gate_ready = sem("tanh_done"), sem("gate_ready")
            cand_step, cand_ready, mix_step = sem("cand_step"), sem("cand_ready"), sem("mix_step")
            qk_ready, qk_taken = sem("qk_ready"), sem("qk_taken")
            v_ready, v_taken = sem("v_ready"), sem("v_taken")
            score_ready, soft_step, soft_exp = sem("score_ready"), sem("soft_step"), sem("soft_exp")
            attn_zero, attn_ready = sem("attn_zero"), sem("attn_ready")
            attn_turned, attn_taken = sem("attn_turned"), sem("attn_taken")
            y_ready, y_step = sem("y_ready"), sem("y_step")
            y_var, y_rstd, yhat_ready = sem("y_var"), sem("y_rstd"), sem("yhat_ready")
            y_turned, yt_ready = sem("y_turned"), sem("yt_ready")
            val_ready, val_taken = sem("val_ready"), sem("val_taken")
            out_ready, out_taken = sem("out_ready"), sem("out_taken")

            block = own.enter_context(nc.Block())
            NH = NS // HALF

            def pair_banks(n):
                return ps[:, 2 * (n % 4):2 * (n % 4) + NH, :]

            def cols(ap):
                return ap.rearrange("p (n h) -> p n h", h=HALF)

            @block.tensor
            def _(pe):
                def project(n, weights, moving, rows_out=P):
                    for h in range(NH):
                        for k in range(KT):
                            last = pe.matmul(ps[0:rows_out, 2 * (n % 4) + h, :], weights(k),
                                             moving[:, k, h * HALF:(h + 1) * HALF], start=(k == 0), stop=(k == KT - 1))
                    return last
                for m in range(MT):
                    if m >= 4:
                        pe.wait_ge(gate_sum, m - 3)
                    project(m, lambda k: c.wih_t[:, k, m * P:(m + 1) * P], si_t).then_inc(gi_ready, 1)
                pe.wait_ge(mix_step, 3 * KT)
                project(2, lambda k: c.wq[:, k, :], new_t, S).then_inc(qk_ready, 1)
                project(3, lambda k: c.wk[:, k, :], new_t, S).then_inc(qk_ready, 1)
                for pair in range(PAIRS):
                    for k in range(KT):
                        last = pe.matmul(ps[:, pair // 2, (pair % 2) * D:(pair % 2 + 1) * D],
                                         new_t[:, k, pair * P:(pair + 1) * P], c.wv[:, k, :],
                                         start=(k == 0), stop=(k == KT - 1))
                    if pair % 2:
                        last.then_inc(v_ready, 1)
                pe.wait_ge(qk_taken, 2)
                for b in range(B):
                    half = b % 2 * S
                    last = pe.matmul(ps[half:half + S, 4, b // 2 * S:(b // 2 + 1) * S], q_t[:, b * S:(b + 1) * S],
                                     k_t[:, b * S:(b + 1) * S], start=True, stop=True)
                last.then_inc(score_ready, 1)
                pe.wait_ge(attn_ready, 2)
                for pair in range(PAIRS):
                    last = pe.transpose(ps[:, 6 + pair // 4, (pair % 4) * P:(pair % 4 + 1) * P], attn[:, pair, :],
                                        c.ident[:, :])
                last.then_inc(attn_turned, 1)
                pe.wait_ge(attn_taken, 1)
                pe.wait_ge(v_taken, PAIRS // 2)
                for pair in range(PAIRS):
                    y = ps[:, pair // 2, (pair % 2) * D:(pair % 2 + 1) * D]
                    pe.matmul(y, attn_t[:, pair, :], v_sb[:, pair, :], start=True, stop=True)
                    for k in range(KT):
                        last = pe.matmul(y[:, k * P:(k + 1) * P], new_t[:, k, pair * P:(pair + 1) * P], c.ident[:, :],
                                         start=False, stop=True, skip_group_check=True)
                    last.then_inc(y_ready, 1)
                pe.wait_ge(yhat_ready, 1)
                for k in range(KT):
                    for pair in range(PAIRS):
                        last = pe.transpose(ps[:, 4 + 2 * k + pair // 4, (pair % 4) * P:(pair % 4 + 1) * P],
                                            y_hat[:, pair, k * P:(k + 1) * P], c.ident[:, :])
                    last.then_inc(y_turned, 1)
                pe.wait_ge(yt_ready, KT)
                for m in range(KT):
                    project(m, lambda k: c.wvp[:, k, m * P:(m + 1) * P], y_t).then_inc(val_ready, 1)
                pe.wait_ge(val_taken, KT)
                for pair in range(PAIRS):
                    for k in range(KT):
                        last = pe.matmul(ps[:, 4 + pair // 2, (pair % 2) * D:(pair % 2 + 1) * D],
                                         val_t[:, k, pair * P:(pair + 1) * P], c.wo[:, k, :],
                                         start=(k == 0), stop=(k == KT - 1))
                    if pair % 2:
                        last.then_inc(out_ready, 1)

            @block.vector
            def _(dve):
                def per_batch(ap):
                    return ap.unsqueeze(1).to_broadcast([P, B, S])

                def by_batch(ap):
                    return ap.rearrange("p (b s) -> p b s", s=S)

                def banks_by_batch(n):
                    return pair_banks(n).rearrange("p n (b s) -> p (n b) s", s=S)

                dve.memset(attn[:, :, :], 0.0).then_inc(attn_zero, 1)
                for m in range(2 * KT):
                    dve.wait_ge(gi_ready, m + 1)
                    dve.tensor_tensor(by_batch(gates[:, m, :]), banks_by_batch(m), per_batch(c.gh_t[:, m, :]),
                                      ALU.add).then_inc(gate_sum, 1)
                for m in range(2 * KT):
                    dve.wait_ge(tanh_done, m + 1)
                    dve.tensor_scalar(gates[:, m, :], gates[:, m, :], 0.5, 0.5, ALU.mult, ALU.add).then_inc(gate_ready, 1)
                for k in range(KT):
                    m = 2 * KT + k
                    dve.wait_ge(gate_ready, k + 1)
                    dve.tensor_tensor(by_batch(pre[:, k, :]), by_batch(gates[:, k, :]), per_batch(c.gh_t[:, m, :]),
                                      ALU.mult).then_inc(cand_step, 1)
                    dve.wait_ge(gi_ready, m + 1)
                    dve.wait_ge(cand_step, 2 * k + 1)
                    dve.scalar_tensor_tensor(cols(pre[:, k, :]), pair_banks(m), c.gate_bias[:, m:m + 1],
                                             cols(pre[:, k, :]), ALU.add, ALU.add).then_inc(cand_step, 1)
                dve.wait_ge(gate_ready, 2 * KT)
                for k in range(KT):
                    old = per_batch(c.slots_t[:, k, :])
                    dve.wait_ge(cand_ready, k + 1)
                    dve.tensor_tensor(by_batch(mix[:, k, :]), old, by_batch(cand[:, k, :]), ALU.subtract).then_inc(mix_step, 1)
                    dve.wait_ge(mix_step, 3 * k + 1)
                    dve.tensor_tensor(mix_z[:, k, :], mix[:, k, :], gates[:, KT + k, :], ALU.mult).then_inc(mix_step, 1)
                    dve.wait_ge(mix_step, 3 * k + 2)
                    dve.tensor_tensor(new_t[:, k, :], mix_z[:, k, :], cand[:, k, :], ALU.add).then_inc(mix_step, 1)
                for g in range(PAIRS // 2):
                    dve.wait_ge(v_ready, g + 1)
                    dve.tensor_tensor(v_sb[:, 2 * g:2 * g + 2, :], ps[:, g, :].rearrange("p (a d) -> p a d", d=D),
                                      c.bv[:, :].unsqueeze(1).to_broadcast([P, 2, D]), ALU.add).then_inc(v_taken, 1)
                scores = ps[:, 4, :].rearrange("p (a s) -> p a s", s=S)
                dve.wait_ge(score_ready, 1)
                dve.tensor_reduce(s_max[:, :], scores, AX.X, ALU.max).then_inc(soft_step, 1)
                dve.wait_ge(soft_step, 1)
                dve.tensor_tensor(s_shift[:, :, :], scores, s_max[:, :].unsqueeze(2).to_broadcast([P, PAIRS, S]),
                                  ALU.subtract).then_inc(soft_step, 1)
                dve.wait_ge(soft_exp, 1)
                dve.tensor_reduce(s_sum[:, :], s_exp[:, :, :], AX.X, ALU.add).then_inc(soft_step, 1)
                dve.wait_ge(soft_step, 3)
                dve.reciprocal(s_inv[:, :], s_sum[:, :]).then_inc(soft_step, 1)
                dve.wait_ge(soft_step, 4)
                dve.wait_ge(attn_zero, 1)
                for h in range(2):
                    rows_h = slice(h * S, (h + 1) * S)
                    dve.tensor_tensor(attn[rows_h, :, rows_h], s_exp[rows_h, :, :],
                                      s_inv[rows_h, :].unsqueeze(2).to_broadcast([S, PAIRS, S]),
                                      ALU.mult).then_inc(attn_ready, 1)
                dve.wait_ge(attn_turned, 1)
                dve.tensor_copy(attn_t[:, :, :].rearrange("p a s -> p (a s)").rearrange("p (n h) -> p n h", h=HALF),
                                ps[:, 6:8, :]).then_inc(attn_taken, 1)
                dve.wait_ge(y_ready, PAIRS)
                y_rows = ps[:, 0:PAIRS // 2, :].rearrange("p n (a d) -> p (n a) d", d=D)
                for a in range(PAIRS):
                    dve.bn_stats(stats[:, a, :], y_rows[:, a, :]).then_inc(y_step, 1)
                dve.wait_ge(y_step, PAIRS)
                for a in range(PAIRS):
                    dve.bn_aggr(mean_var[:, a, :], stats[:, a, :]).then_inc(y_step, 1)
                dve.wait_ge(y_step, 2 * PAIRS)
                dve.tensor_scalar(var_eps[:, :], mean_var[:, :, 1], EPS, None, ALU.add).then_inc(y_var, 1)
                dve.wait_ge(y_rstd, 1)
                for a in range(PAIRS):
                    last = dve.tensor_scalar(y_hat[:, a, :], y_rows[:, a, :], mean_var[:, a, 0:1], rstd[:, a:a + 1],
                                             ALU.subtract, ALU.mult)
                last.then_inc(yhat_ready, 1)
                for g in range(PAIRS // 2):
                    dve.wait_ge(out_ready, g + 1)
                    dve.tensor_copy(slot_out[:, 2 * g:2 * g + 2, :], ps[:, 4 + g, :].rearrange("p (a d) -> p a d", d=D)
                                    ).then_inc(out_taken, 1)
                dve.wait_ge(out_taken, PAIRS // 2)

            @block.gpsimd
            def _(pool):
                pool.wait_ge(y_var, 1)
                pool.tensor_tensor(rstd[:, :], var_eps[:, :], c.neg_half[:, 0:PAIRS], ALU.pow).then_inc(y_rstd, 1)

            @block.scalar
            def _(act):
                for m in range(2 * KT):
                    act.wait_ge(gate_sum, m + 1)
                    act.activation(gates[:, m, :], gates[:, m, :], ACT.Tanh, scale=0.5).then_inc(tanh_done, 1)
                for k in range(KT):
                    act.wait_ge(cand_step, 2 * k + 2)
                    act.activation(cand[:, k, :], pre[:, k, :], ACT.Tanh).then_inc(cand_ready, 1)
                for n, (dst, bias) in enumerate(((q_t, c.bq), (k_t, c.bk))):
                    act.wait_ge(qk_ready, n + 1)
                    act.activation(cols(dst[:, :]), ps[0:S, 4 + 2 * n:6 + 2 * n, :], ACT.Identity,
                                   bias=bias[:, 0:1]).then_inc(qk_taken, 1)
                act.wait_ge(soft_step, 2)
                act.activation(s_exp[:, :, :], s_shift[:, :, :], ACT.Exp, scale=float(S) ** -0.5).then_inc(soft_exp, 1)
                for k in range(KT):
                    act.wait_ge(y_turned, k + 1)
                    act.activation(cols(y_t[:, k, :]), ps[:, 4 + 2 * k:6 + 2 * k, :], ACT.Identity,
                                   bias=c.ln_b[:, k:k + 1], scale=c.ln_g[:, k:k + 1]).then_inc(yt_ready, 1)
                for m in range(KT):
                    act.wait_ge(val_ready, m + 1)
                    act.activation(cols(val_t[:, m, :]), pair_banks(m), ACT.Identity,
                                   bias=c.bvp[:, m:m + 1]).then_inc(val_taken, 1)

        with ExitStack() as own:
            xc = sb("xc", [P, R, TT, D], F32, own)
            at_cur = sb("at_cur", [S + 1, 2, T], F32, own)
            so_cur = sb("so_cur", [S + 1, 2, D], F32, own)
            ps = own.enter_context(nc.psum_tensor(f"{tag}_ps_back", [P, 8, HALF], F32))
            back_loaded = [sem(f"back_loaded{r}") for r in range(R)]
            cur_loaded = [sem(f"cur_loaded{r}") for r in range(2)]
            bo_loaded, ones_set = sem("bo_loaded"), sem("ones_set")
            mixed, added = sem("mixed"), sem("added")
            stored = [sem(f"stored{r}") for r in range(R)]
            block = own.enter_context(nc.Block())
            BANKS = TT * D // HALF

            def over_quads(eng, step, steps=B // R):
                step(0, True)
                with eng.Fori(1, steps, 1) as q:
                    step(q, False)

            @block.gpsimd
            def _(pool):
                pool.memset(at_cur[S:S + 1, :, :], 1.0).then_inc(ones_set, 1)

            @block.sync
            def _(sp):
                for r in range(2):
                    sp.dma_start(so_cur[S:S + 1, r, :], bo.rearrange("(o d) -> o d", o=1)).then_inc(bo_loaded, 16)

                def step(q, first):
                    for r in range(R):
                        if not first:
                            sp.wait_ge(stored[r], q * 16)
                        sp.dma_start(xc[:, r], rows(x_in, q * R + r)).then_inc(back_loaded[r], 16)
                        if not (first and r < 2):
                            sp.wait_ge(mixed, (q * R + (r - 1)) * BANKS)
                        h = r % 2
                        sp.dma_start(at_cur[0:S, h, :], alpha_t[:, bass.ds(q * R + r, 1), :]).then_inc(cur_loaded[h], 16)
                        sp.dma_start(so_cur[0:S, h, :],
                                     slot_out[h * S:(h + 1) * S, bass.ds(q * (R // 2) + r // 2, 1), :]).then_inc(cur_loaded[h], 16)
                over_quads(sp, step)

            @block.tensor
            def _(pe):
                pe.wait_ge(bo_loaded, 32)
                pe.wait_ge(ones_set, 1)

                def step(q, first):
                    for r in range(R):
                        h = r % 2
                        pe.wait_ge(cur_loaded[h], q * (R // 2 * 32) + (r // 2 + 1) * 32)
                        for n in range(BANKS):
                            if not (first and r < 2):
                                pe.wait_ge(added, q * (R * BANKS) + ((r - 2) * BANKS + n + 1))
                            for j in range(2):
                                t = 2 * n + j
                                last = pe.matmul(ps[:, h * BANKS + n, j * D:(j + 1) * D], at_cur[:, h, t * P:(t + 1) * P],
                                                 so_cur[:, h, :], start=True, stop=True)
                            last.then_inc(mixed, 1)
                over_quads(pe, step)

            @block.vector
            def _(dve):
                def step(q, first):
                    for r in range(R):
                        dve.wait_ge(back_loaded[r], q * 16 + 16)
                        for n in range(BANKS):
                            dve.wait_ge(mixed, q * (R * BANKS) + (r * BANKS + n + 1))
                            x2 = xc[:, r, 2 * n:2 * n + 2, :].rearrange("p t d -> p (t d)")
                            dve.scalar_tensor_tensor(x2, ps[:, r % 2 * BANKS + n, :], 0.5, x2, ALU.mult,
                                                     ALU.add).then_inc(added, 1)
                over_quads(dve, step)

            @block.scalar
            def _(act):
                def step(q, first):
                    for r in range(R):
                        act.wait_ge(added, q * (R * BANKS) + (r + 1) * BANKS)
                        act.dma_start(rows(x_out, q * R + r), xc[:, r]).then_inc(stored[r], 16)
                over_quads(act, step)
                for r in range(R):
                    act.wait_ge(stored[r], B // R * 16)

        clear(nc, sems)


def build_attention(nc, c, x_in, x_out, w_qkv, b_qkv, w_out, b_out):
    B, T, D = x_in.shape
    KT, TT = D // P, T // P
    H, DH = 16, D // 16
    GH = 4
    NG = H // GH
    CHUNKS = T // HALF
    GU = GH * TT * CHUNKS
    BU = NG * GU
    AHEAD = GU + 16
    NQ = 4
    Q_PARTS, K_PARTS = (0, 0, 1, 0, 2, 1), (0, 1, 0, 2, 0, 1)
    SR = len(Q_PARTS) * DH
    PREP = 3
    B0 = 2

    QK_AT = [76, GU + 37, 2 * GU + 37, 3 * GU + 37]
    X_AT = 88
    V_AT = [70, 83, 2 * GU + 8, 2 * GU + 14]
    RATE = {"turn_x": 4, "qk": 2 * NG, "v": NG, "turn_max": NG, "turn_o": TT, "turn_ctx": TT, "project": TT}

    def jobs(b):
        out = []
        for qt in range(TT):
            out += [(6 + 8 * qt, "turn_o", TT * (b - 1) + qt), (11 + 8 * qt, "turn_ctx", TT * (b - 1) + qt),
                    (16 + 8 * qt, "project", TT * (b - 1) + qt)]
        for g in range(NG):
            u, G = g * GU, NG * b + g
            out += [(u + 49, "turn_max", G + 1)] + [(QK_AT[g] + 3 * i, "qk", 2 * (G + PREP) + i) for i in range(2)]
        out += [(X_AT + 3 * f, "turn_x", 4 * (b + 1) + f) for f in range(4)]
        out += [(at, "v", NG * b + 2 + i) for i, at in enumerate(V_AT)]
        return sorted(out)

    LIMIT = {k: r * B for k, r in RATE.items()}

    def body_jobs(b):
        return [j for j in jobs(b) if 0 <= j[2] < LIMIT[j[1]]]

    bank_of = {(kind, n % RATE[kind]): 6 + i % 2 for i, (_, kind, n) in enumerate(jobs(B0))}
    opening = [(0, "turn_x", f) for f in range(4)]
    for G in range(PREP):
        opening += [(0, "qk", 2 * G), (0, "qk", 2 * G + 1)] + [(0, "v", G)] * (G < 2)
    opening += [(66, "turn_max", 0)]
    closing = []
    for s in range(TT + 2):
        closing += [(s, kind, TT * (B - 1) + s - lag) for lag, kind in enumerate(("turn_o", "turn_ctx", "project"))
                    if 0 <= s - lag < TT]
    before = {}
    holder = {}
    for _, kind, n in opening + [j for b in range(B) for j in body_jobs(b)] + closing:
        bank = bank_of[kind, n % RATE[kind]]
        before[kind, n] = holder.get(bank)
        holder[bank] = (kind, n)

    with ExitStack() as ctx:
        def sb(name, shape, dt=F32):
            return ctx.enter_context(nc.sbuf_tensor(f"attn_{name}", shape, dt))

        def sem(name):
            sems.append(ctx.enter_context(nc.semaphore(f"attn_{name}")))
            return sems[-1]

        sems = []
        blocks = ExitStack()
        w_qk = sb("w_qk", [P, KT, NG, P])
        b_qk = sb("b_qk", [P, NG])
        w_v = sb("w_v", [P, KT, D])
        b_v = sb("b_v", [P, D])
        w_o = sb("w_o", [P, KT, D])
        b_o = sb("b_o", [P, D])
        x_ln = sb("x_ln", [P, TT, D])
        x_res = sb("x_res", [P, TT, D])
        stats = sb("stats", [P, TT, 6])
        mean_var = sb("mean_var", [P, TT, 2])
        waited = sb("waited", [P, 1])
        var_eps = sb("var_eps", [P, TT])
        rstd = sb("rstd", [P, TT])
        xn_t = sb("xn_t", [P, KT, T])
        qk = sb("qk", [P, T])
        qk_rest = sb("qk_rest", [P, T])
        parts = sb("parts", [P, 3, T], BF16)
        q_rows = sb("q_rows", [SR + 3, NG, GH, T], BF16)
        k_rows = sb("k_rows", [SR + 3, NG, GH, T], BF16)
        v_ones = sb("v_ones", [P, NG, TT, GH, 2 * DH])
        probs = sb("probs", [P, NQ, GH, HALF])
        o_sb = sb("o_sb", [P, NG, T])
        part_max = sb("part_max", [P, 2, GU])
        neg_max = sb("neg_max", [P, 2, GU // 2])
        max_rest = sb("max_rest", [GU // 2, P])
        max_parts = sb("max_parts", [GU // 2, 3, P], BF16)
        sum_inv = sb("sum_inv", [P, 2, H])
        ctx_rows = sb("ctx_rows", [P, 2, D])
        ctx_t = sb("ctx_t", [P, 2, KT, P])
        w_raw = o_sb[:, 0, :].rearrange("p (k n) -> p k n", k=KT)
        ps = ctx.enter_context(nc.psum_tensor("attn_ps", [P, 8, HALF], F32))

        weights_loaded, w_raw_loaded = sem("weights_loaded"), sem("w_raw_loaded")
        w_qk_ready, ones_ready = sem("w_qk_ready"), sem("ones_ready")
        x_loaded, res_loaded, res_ready = sem("x_loaded"), sem("res_loaded"), sem("res_ready")
        stat_step, var_ready, rstd_ready, xn_ready = sem("stat_step"), sem("var_ready"), sem("rstd_ready"), sem("xn_ready")
        ready = {k: sem(f"{k}_ready") for k in RATE}
        taken = {k: sem(f"{k}_taken") for k in RATE if k != "qk"}
        qk_whole, part1_ready = sem("qk_whole"), sem("part1_ready")
        taken["qk"] = part1_ready
        rest_ready, part2_ready, part3_ready = sem("rest_ready"), sem("part2_ready"), sem("part3_ready")
        rows_loaded = [sem(f"rows_loaded{g}") for g in range(NG)]
        max_tile_ready, max_tile_taken = sem("max_tile_ready"), sem("max_tile_taken")
        neg_max_ready, max_split, max_parts_ready = sem("neg_max_ready"), sem("max_split"), sem("max_parts_ready")
        max_loaded = [sem(f"max_loaded{g}") for g in range(NG)]
        scores_ready, exp_done, pv_done, o_taken = sem("scores_ready"), sem("exp_done"), sem("pv_done"), sem("o_taken")
        inv_ready = sem("inv_ready")
        stored = sem("stored")

        block = blocks.enter_context(nc.Block())

        def over_batches(eng, body):
            body(0, 0)
            with eng.Fori(1, B - 1, 1) as b:
                body({1: b, "eng": eng}, B0)
            body(B - 1, B - 1)

        def value(b, rate, n):
            if isinstance(b, int):
                return n
            if rate not in b:
                b[rate] = b["eng"].snap(b[1] * rate)
            return b[rate] + (n - B0 * rate)

        def wait(eng, sem_, b, rate, n):
            if n <= 0:
                assert isinstance(b, int)
                return
            assert isinstance(b, int) or n > rate, (rate, n)
            eng.wait_ge(sem_, value(b, rate, n))

        def rows(t, b, b0, ahead=0):
            at = b if isinstance(b, int) else b[1]
            return t[bass.ds(at + ahead, 1)].rearrange("a (p t) d -> (a p) t d", t=TT)

        @block.sync
        def _(sp):
            sp.dma_start(w_raw, w_qkv[:, 0:2 * D].rearrange("(k p) n -> p k n", p=P)).then_inc(w_raw_loaded, 16)
            sp.dma_start(x_ln[:, :, :], rows(x_in, 0, 0)).then_inc(x_loaded, 16)
            sp.dma_start(w_v[:, :, :], w_qkv[:, 2 * D:3 * D].rearrange("(k p) n -> p k n", p=P)).then_inc(weights_loaded, 16)
            sp.dma_start(w_o[:, :, :], w_out.rearrange("(k p) n -> p k n", p=P)).then_inc(weights_loaded, 16)
            sp.dma_start(b_v[:, :], b_qkv[2 * D:3 * D].partition_broadcast(P)).then_inc(weights_loaded, 16)
            sp.dma_start(b_o[:, :], b_out.partition_broadcast(P)).then_inc(weights_loaded, 16)
            for i in range(2):
                for g in range(NG):
                    src = b_qkv[i * D + g * GH * DH:i * D + (g + 1) * GH * DH].rearrange("(h d o) -> d h o", h=GH, o=1)
                    sp.dma_start(b_qk[i * 64:i * 64 + 64, g:g + 1], src).then_inc(weights_loaded, 16)

            def lay_out(b, b0, G):
                g = G % NG
                wait(sp, part3_ready, b, NG, G + 1)
                wait(sp, part1_ready, b, 2 * NG, 2 * G + 2)
                for dst, order, half in ((q_rows, Q_PARTS, 0), (k_rows, K_PARTS, 1)):
                    for i, part in enumerate(order):
                        sp.dma_start(dst[i * DH:(i + 1) * DH, g, :, :],
                                     parts[half * 64:half * 64 + 64, part, :]).then_inc(rows_loaded[g], 16)

            def max_rows(b, b0, G):
                wait(sp, max_parts_ready, b, NG, G + 1)
                for i in range(3):
                    sp.dma_start(q_rows[SR + i:SR + i + 1, G % NG, :, :],
                                 max_parts[:, i, :]).then_inc(max_loaded[G % NG], 16)

            for G in range(PREP):
                lay_out(0, 0, G)
            max_rows(0, 0, 0)

            def body(b, b0):
                if b0 < B - 1:
                    wait(sp, ready["turn_x"], b, 4, 4 * (b0 + 1))
                    sp.dma_start(x_ln[:, :, :], rows(x_in, b, b0, 1)).then_inc(x_loaded, 16)
                for g in range(NG):
                    G = NG * b0 + g
                    if G + 1 < NG * B:
                        max_rows(b, b0, G + 1)
                    if g == 0:
                        if b0 > 0:
                            wait(sp, taken["project"], b, TT, TT * b0)
                            sp.dma_start(rows(x_out, b, b0, -1), x_res[:, :, :]).then_inc(stored, 16)
                            wait(sp, stored, b, 16, 16 * b0)
                        sp.dma_start(x_res[:, :, :], rows(x_in, b, b0)).then_inc(res_loaded, 16)
                    if G + PREP < NG * B:
                        lay_out(b, b0, G + PREP)
            over_batches(sp, body)
            sp.wait_ge(taken["project"], TT * B)
            sp.dma_start(rows(x_out, B - 1, B - 1), x_res[:, :, :]).then_inc(stored, 16)
            sp.wait_ge(stored, 16 * B)

        @block.gpsimd
        def _(pool):
            pool.memset(v_ones[:, :, :, :, :], 1.0).then_inc(ones_ready, 1)

            def split(b, b0, G):
                wait(pool, qk_whole, b, 2 * NG, 2 * G + 2)
                wait(pool, part1_ready, b, 2 * NG, 2 * G + 2)
                pool.tensor_tensor(qk_rest[:, :], qk[:, :], parts[:, 0, :], ALU.subtract).then_inc(rest_ready, 1)
                wait(pool, part2_ready, b, NG, G + 1)
                pool.tensor_tensor(parts[:, 2, :], qk_rest[:, :], parts[:, 1, :], ALU.subtract).then_inc(part3_ready, 1)

            def rsqrt(b, b0, n):
                wait(pool, var_ready, b, 1, n + 1)
                pool.tensor_tensor(rstd[:, :], var_eps[:, :], c.neg_half[:, 0:TT], ALU.pow).then_inc(rstd_ready, 1)
            rsqrt(0, 0, 0)
            for G in range(PREP):
                split(0, 0, G)
            pool.wait_ge(weights_loaded, 16 * (4 + 2 * NG))

            def body(b, b0):
                if b0 < B - 1:
                    rsqrt(b, b0, b0 + 1)
                for g in range(NG):
                    if NG * b0 + g + PREP < NG * B:
                        split(b, b0, NG * b0 + g + PREP)
                    if g == 1:
                        wait(pool, res_loaded, b, 16, 16 * (b0 + 1))
                        pool.tensor_tensor(x_res[:, :, :], x_res[:, :, :],
                                           b_o[:, :].unsqueeze(1).to_broadcast([P, TT, D]), ALU.add).then_inc(res_ready, 1)
            over_batches(pool, body)

        @block.vector
        def _(dve):
            dve.memset(k_rows[SR:SR + 3, :, :, :], 1.0).then_inc(ones_ready, 1)
            dve.wait_ge(w_raw_loaded, 16)
            for k in range(KT):
                for i in range(2):
                    for g in range(NG):
                        src = w_raw[:, k, i * D + g * 64:i * D + (g + 1) * 64].rearrange("p (h d) -> p d h", h=GH)
                        dst = w_qk[:, k, g, i * 64:(i + 1) * 64].rearrange("p (d h) -> p d h", h=GH)
                        dve.tensor_copy(dst, src).then_inc(w_qk_ready, 1)

            def stat(b, b0, n, t):
                if t == 0:
                    wait(dve, x_loaded, b, 16, 16 * (n + 1))
                dve.bn_stats(stats[:, t, :], x_ln[:, t, :]).then_inc(stat_step, 1)

            def moments(b, b0, n):
                wait(dve, stat_step, b, 2 * TT, 2 * TT * n + TT)
                dve.memset(waited[:, :], 0.0)
                for t in range(TT):
                    dve.bn_aggr(mean_var[:, t, :], stats[:, t, :]).then_inc(stat_step, 1)
                wait(dve, stat_step, b, 2 * TT, 2 * TT * (n + 1))
                dve.tensor_scalar(var_eps[:, :], mean_var[:, :, 1], EPS, None, ALU.add).then_inc(var_ready, 1)

            def normalise(b, b0, n, t):
                if t == 0:
                    wait(dve, rstd_ready, b, 1, n + 1)
                ins = dve.tensor_scalar(x_ln[:, t, :], x_ln[:, t, :], mean_var[:, t, 0:1], rstd[:, t:t + 1],
                                        ALU.subtract, ALU.mult)
                if t == TT - 1:
                    ins.then_inc(xn_ready, 1)

            def values(b, b0, n):
                pair, half = n % NG // 2, n % 2
                bank = ps[:, bank_of["v", n % NG], :].rearrange("p (t g h d) -> p t g h d", t=TT // 2, g=2, h=GH)
                wait(dve, ready["v"], b, NG, n + 1)
                for i in range(2):
                    g = 2 * pair + i
                    bias = b_v[:, g * 64:(g + 1) * 64].rearrange("p (h d) -> p h d", h=GH)
                    last = dve.tensor_tensor(v_ones[:, g, half * (TT // 2):(half + 1) * (TT // 2), :, 0:DH], bank[:, :, i],
                                             bias.unsqueeze(1).to_broadcast([P, TT // 2, GH, DH]), ALU.add)
                last.then_inc(taken["v"], 1)

            def reduce_tile(b, b0, v):
                G, w = divmod(v, GU)
                wait(dve, max_tile_ready, b, BU, v + 1)
                dve.tensor_reduce(part_max[:, G % 2, w:w + 1], ps[:, v % 2, :], AX.X, ALU.max).then_inc(max_tile_taken, 1)
                if w == GU - 1:
                    wait(dve, max_tile_taken, b, BU, v + 1)
                    dve.tensor_reduce(neg_max[:, G % 2, :], part_max[:, G % 2, :].rearrange("p (n h) -> p n h", h=CHUNKS),
                                      AX.X, ALU.max, negate=True).then_inc(neg_max_ready, 1)

            def split_max(b, b0, G):
                bank = ps[0:GU // 2, bank_of["turn_max", G % NG], 0:P]
                wait(dve, ready["turn_max"], b, NG, G + 1)
                if G > 0:
                    wait(dve, max_loaded[(G - 1) % NG], b, 48, 48 * ((G - 1) // NG + 1))
                dve.tensor_copy(max_parts[:, 0, :], bank).then_inc(max_split, 1)
                wait(dve, max_split, b, 2 * NG, 2 * G + 1)
                dve.tensor_tensor(max_rest[:, :], bank, max_parts[:, 0, :], ALU.subtract).then_inc(taken["turn_max"], 1)
                wait(dve, taken["turn_max"], b, NG, G + 1)
                dve.tensor_copy(max_parts[:, 1, :], max_rest[:, :]).then_inc(max_split, 1)
                wait(dve, max_split, b, 2 * NG, 2 * G + 2)
                dve.tensor_tensor(max_parts[:, 2, :], max_rest[:, :], max_parts[:, 1, :], ALU.subtract).then_inc(max_parts_ready, 1)

            def normalise_out(b, b0, n):
                qt = n % TT
                bank = ps[:, bank_of["turn_o", qt], :].rearrange("p (h d) -> p h d", h=H)
                wait(dve, ready["turn_o"], b, TT, n + 1)
                dve.reciprocal(sum_inv[:, qt % 2, :], bank[:, :, DH]).then_inc(inv_ready, 1)
                wait(dve, inv_ready, b, TT, n + 1)
                dve.tensor_tensor(ctx_rows[:, qt % 2, :].rearrange("p (h d) -> p h d", h=H), bank[:, :, 0:DH],
                                  sum_inv[:, qt % 2, :].unsqueeze(2).to_broadcast([P, H, DH]), ALU.mult).then_inc(taken["turn_o"], 1)

            def add_out(b, b0, n):
                qt = n % TT
                wait(dve, ready["project"], b, TT, n + 1)
                if qt == 0:
                    wait(dve, res_ready, b, 1, n // TT + 1)
                dve.tensor_tensor(x_res[:, qt, :], ps[:, bank_of["project", qt], 0:D], x_res[:, qt, :],
                                  ALU.add).then_inc(taken["project"], 1)

            uses = {"v": values, "turn_max": split_max, "turn_o": normalise_out, "project": add_out}
            for t in range(TT):
                stat(0, 0, 0, t)
            moments(0, 0, 0)
            for t in range(TT):
                normalise(0, 0, 0, t)
            dve.wait_ge(weights_loaded, 16 * (4 + 2 * NG))
            dve.wait_ge(ones_ready, 2)
            for n in range(2):
                values(0, 0, n)
            for v in range(AHEAD):
                reduce_tile(0, 0, v)
                if v == 67:
                    split_max(0, 0, 0)

            def body(b, b0):
                todo = body_jobs(b0)
                for u in range(BU):
                    v = BU * b0 + u + AHEAD
                    if v < BU * B:
                        reduce_tile(b, b0, v)
                    for at, kind, n in todo:
                        if at == u - 1 and kind in uses:
                            uses[kind](b, b0, n)
                    if b0 < B - 1:
                        for t in range(TT):
                            if u == 30 + 3 * t:
                                stat(b, b0, b0 + 1, t)
                            if u == 69 + 2 * t:
                                normalise(b, b0, b0 + 1, t)
                        if u == 60:
                            moments(b, b0, b0 + 1)
            over_batches(dve, body)
            for _, kind, n in closing:
                if kind in uses:
                    uses[kind](B - 1, B - 1, n)

        @block.tensor
        def _(pe):
            def small(b, b0, kind, n):
                key = n % RATE[kind]
                bank = bank_of[kind, key]
                if before[kind, n]:
                    prev, m = before[kind, n]
                    wait(pe, taken[prev], b, RATE[prev], m + 1)
                if kind == "turn_x":
                    if key == 0:
                        wait(pe, xn_ready, b, 1, n // 4 + 1)
                    for j in range(4):
                        k, t = divmod(4 * key + j, TT)
                        last = pe.transpose(ps[:, bank, j * P:(j + 1) * P], x_ln[:, t, k * P:(k + 1) * P], c.ident[:, :])
                elif kind == "qk":
                    G, half = divmod(n, 2)
                    wait(pe, taken["turn_x"], b, 4, 4 * (G // NG + 1))
                    for k in range(KT):
                        last = pe.matmul(ps[:, bank, :], w_qk[:, k, G % NG, :], xn_t[:, k, half * HALF:(half + 1) * HALF],
                                         start=(k == 0), stop=(k == KT - 1))
                elif kind == "v":
                    pair, half = n % NG // 2, n % 2
                    wait(pe, taken["turn_x"], b, 4, 4 * (n // NG + 1))
                    for t in range(TT // 2):
                        for k in range(KT):
                            last = pe.matmul(ps[:, bank, t * P:(t + 1) * P],
                                             xn_t[:, k, (half * (TT // 2) + t) * P:(half * (TT // 2) + t + 1) * P],
                                             w_v[:, k, pair * P:(pair + 1) * P], start=(k == 0), stop=(k == KT - 1))
                elif kind == "turn_max":
                    wait(pe, neg_max_ready, b, NG, n + 1)
                    last = pe.transpose(ps[0:GU // 2, bank, 0:P], neg_max[:, n % 2, :], c.ident[:, :])
                elif kind == "turn_o":
                    if key == 0:
                        wait(pe, o_taken, b, 2 * NG, 2 * NG * (n // TT + 1))
                    for g in range(NG):
                        last = pe.transpose(ps[:, bank, g * P:(g + 1) * P], o_sb[:, g, key * P:(key + 1) * P], c.ident[:, :])
                elif kind == "turn_ctx":
                    wait(pe, taken["turn_o"], b, TT, n + 1)
                    for k in range(KT):
                        last = pe.transpose(ps[:, bank, k * P:(k + 1) * P], ctx_rows[:, key % 2, k * P:(k + 1) * P], c.ident[:, :])
                else:
                    wait(pe, taken["turn_ctx"], b, TT, n + 1)
                    for k in range(KT):
                        last = pe.matmul(ps[:, bank, 0:D], ctx_t[:, key % 2, k, :], w_o[:, k, :],
                                         start=(k == 0), stop=(k == KT - 1))
                last.then_inc(ready[kind], 1)

            def max_tile(b, b0, v):
                G, w = divmod(v, GU)
                h, t, half = w // (TT * CHUNKS), w // CHUNKS % TT, w % CHUNKS
                g = G % NG
                if w == 0:
                    wait(pe, rows_loaded[g], b, 192, 192 * (G // NG + 1))
                wait(pe, max_tile_taken, b, BU, v - 1)
                pe.matmul(ps[:, v % 2, :], q_rows[0:SR, g, h, t * P:(t + 1) * P],
                          k_rows[0:SR, g, h, half * HALF:(half + 1) * HALF], start=True, stop=True).then_inc(max_tile_ready, 1)

            def score_tile(b, b0, u):
                G, w = divmod(u, GU)
                half, kt, h = w // (TT * GH), w // GH % TT, w % GH
                g = G % NG
                if w == 0:
                    wait(pe, max_loaded[g], b, 48, 48 * (G // NG + 1))
                wait(pe, exp_done, b, BU, u - 1)
                pe.matmul(ps[:, 2 + u % 2, :], k_rows[:, g, h, kt * P:(kt + 1) * P],
                          q_rows[:, g, h, half * HALF:(half + 1) * HALF], start=True, stop=True).then_inc(scores_ready, 1)

            def pv(b, b0, quad, piece):
                window, kt = divmod(quad, TT)
                G = window // CHUNKS
                if piece == 0:
                    wait(pe, exp_done, b, BU, 4 * (quad + 1))
                    if kt == 0:
                        wait(pe, o_taken, b, 2 * NG, window - 1)
                        if window % (2 * CHUNKS) == 0:
                            wait(pe, taken["v"], b, NG, G + 2)
                cols = slice(piece * HALF // 2, (piece + 1) * HALF // 2)
                for h in range(GH):
                    last = pe.matmul(ps[32 * h:32 * h + 32, 4 + window % 2, cols], v_ones[:, G % NG, kt, h, :],
                                     probs[:, quad % NQ, h, cols], start=(kt == 0 and piece == 0), stop=(kt == TT - 1),
                                     skip_group_check=True)
                if piece == 1:
                    last.then_inc(pv_done, 1)

            pe.wait_ge(w_qk_ready, 2 * KT * NG)
            pe.wait_ge(weights_loaded, 16 * (4 + 2 * NG))
            for _, kind, n in opening[:-1]:
                small(0, 0, kind, n)
            pe.wait_ge(ones_ready, 2)
            for v in range(AHEAD):
                if v == opening[-1][0]:
                    small(0, 0, "turn_max", 0)
                max_tile(0, 0, v)

            def body(b, b0):
                todo = body_jobs(b0)
                for u in range(BU):
                    for at, kind, n in todo:
                        if at == u:
                            small(b, b0, kind, n)
                    if BU * b0 + u + AHEAD < BU * B:
                        max_tile(b, b0, BU * b0 + u + AHEAD)
                    score_tile(b, b0, BU * b0 + u)
                    quad = (BU * b0 + u) // 4 - 1
                    if u % 2 == 1 and quad >= 0:
                        pv(b, b0, quad, u % 4 // 2)
            over_batches(pe, body)
            for piece in range(2):
                pv(B - 1, B - 1, BU * B // 4 - 1, piece)
            for _, kind, n in closing:
                small(B - 1, B - 1, kind, n)

        @block.scalar
        def _(act):
            def turned_x(b, b0, n):
                f = n % 4
                wait(act, ready["turn_x"], b, 4, n + 1)
                act.activation(xn_t[:, :, :].rearrange("p k t -> p (k t)")[:, f * HALF:(f + 1) * HALF],
                               ps[:, bank_of["turn_x", f], :], ACT.Identity).then_inc(taken["turn_x"], 1)

            def take_qk(b, b0, n):
                G, half = divmod(n, 2)
                g = G % NG
                cols = slice(half * HALF, (half + 1) * HALF)
                bank = ps[:, bank_of["qk", n % RATE["qk"]], :]
                wait(act, ready["qk"], b, 2 * NG, n + 1)
                wait(act, rest_ready, b, NG, G)
                act.activation(qk[:, cols], bank, ACT.Identity, bias=b_qk[:, g:g + 1]).then_inc(qk_whole, 1)
                if G > 0:
                    wait(act, rows_loaded[(G - 1) % NG], b, 192, 192 * ((G - 1) // NG + 1))
                act.activation(parts[:, 0, cols], bank, ACT.Identity, bias=b_qk[:, g:g + 1]).then_inc(part1_ready, 1)

            def second_part(b, b0, G):
                wait(act, rest_ready, b, NG, G + 1)
                act.activation(parts[:, 1, :], qk_rest[:, :], ACT.Identity).then_inc(part2_ready, 1)

            def take_ctx(b, b0, n):
                qt = n % TT
                wait(act, ready["turn_ctx"], b, TT, n + 1)
                act.activation(ctx_t[:, qt % 2, :, :], ps[:, bank_of["turn_ctx", qt], 0:D].rearrange("p (k q) -> p k q", k=KT),
                               ACT.Identity, scale=float(D) ** -0.5).then_inc(taken["turn_ctx"], 1)

            def take_o(b, b0, window):
                wait(act, pv_done, b, BU // 4, TT * (window + 1))
                g, half = window // CHUNKS % NG, window % CHUNKS
                if g == 0 and window >= 2 * NG:
                    wait(act, ready["turn_o"], b, TT, window // (2 * NG) * TT - TT // 2 * (1 - half))
                act.activation(o_sb[:, g, half * HALF:(half + 1) * HALF], ps[:, 4 + window % 2, :],
                               ACT.Identity).then_inc(o_taken, 1)

            uses = {"turn_x": turned_x, "qk": take_qk, "turn_ctx": take_ctx}
            act.wait_ge(weights_loaded, 16 * (4 + 2 * NG))
            for _, kind, n in opening:
                if kind in uses:
                    uses[kind](0, 0, n)
                if kind == "qk" and n % 2:
                    second_part(0, 0, n // 2)

            def body(b, b0):
                todo = body_jobs(b0)
                for u in range(BU):
                    U = BU * b0 + u
                    if u % GH == 0:
                        wait(act, pv_done, b, BU // 4, U // GH - NQ + 1)
                    wait(act, scores_ready, b, BU, U + 1)
                    act.activation(probs[:, U // GH % NQ, u % GH, :], ps[:, 2 + u % 2, :], ACT.Exp).then_inc(exp_done, 1)
                    if u % (TT * GH) == 5 and U >= TT * GH:
                        take_o(b, b0, U // (TT * GH) - 1)
                    for at, kind, n in todo:
                        if at == u - 1 and kind in uses:
                            uses[kind](b, b0, n)
                    for g in range(NG):
                        if u == QK_AT[g] + 9 and NG * b0 + g + PREP < NG * B:
                            second_part(b, b0, NG * b0 + g + PREP)
            over_batches(act, body)
            take_o(B - 1, B - 1, 2 * NG * B - 1)
            for _, kind, n in closing:
                if kind in uses:
                    uses[kind](B - 1, B - 1, n)

        blocks.close()
        clear(nc, sems)


def build_program(nc, d, out):
    x = d["L0_attn_x"]
    x1 = nc.dram_tensor("after_first_ffn", x.shape, F32, kind="Internal").ap()
    x2 = nc.dram_tensor("after_attention", x.shape, F32, kind="Internal").ap()
    with ExitStack() as ctx:
        ctx.enter_context(nc.allow_non_contiguous_dma(reason="bias vectors, a few hundred elements each, loaded once"))
        c = build_setup(nc, ctx, d)
        build_ffn(nc, c, "ffn1", x, x1, d["L0_ffn_bo"])
        nc.disable_value_cache = True
        build_attention(nc, c, x1, x2, d["L0_attn_W_qkv"], d["L0_attn_b_qkv"], d["L0_attn_W_out"], d["L0_attn_b_out"])
        build_ffn(nc, c, "ffn2", x2, out, d["L0_ffn_bo"])


_INS = ["L0_attn_x", "L0_attn_W_qkv", "L0_attn_b_qkv", "L0_attn_W_out", "L0_attn_b_out", "L0_ffn_slot_init", "L0_ffn_w1",
        "L0_ffn_b1", "L0_ffn_w2", "L0_ffn_b2", "L0_ffn_tau", "L0_ffn_Wih", "L0_ffn_Whh", "L0_ffn_bih", "L0_ffn_bhh",
        "L0_ffn_wq", "L0_ffn_bq", "L0_ffn_wk", "L0_ffn_bk", "L0_ffn_wv", "L0_ffn_bv", "L0_ffn_ln_g", "L0_ffn_ln_b",
        "L0_ffn_wvp", "L0_ffn_bvp", "L0_ffn_wo", "L0_ffn_bo"]


def kernel(**inputs):
    import numpy as np
    import concourse.bacc as bacc
    from concourse.bass_utils import run_bass_kernel_spmd

    nc = bacc.Bacc("TRN2", target_bir_lowering=False, num_devices=1)
    arrays, d = {}, {}
    for name in _INS:
        a = np.ascontiguousarray(inputs[name])
        arrays[f"in_{name}"] = a
        d[name] = nc.dram_tensor(f"in_{name}", a.shape, mybir.dt.from_np(a.dtype), kind="ExternalInput").ap()
    out = nc.dram_tensor("out", inputs["L0_attn_x"].shape, F32, kind="ExternalOutput").ap()
    build_program(nc, d, out)
    r = run_bass_kernel_spmd(nc, [arrays], core_ids=[0])
    return r.results[0]["out"]
```

```python
from contextlib import ExitStack

import concourse.bass as bass
from concourse import mybir

F32 = mybir.dt.float32
BF16 = mybir.dt.bfloat16
ALU = mybir.AluOpType
ACT = mybir.ActivationFunctionType
AX = mybir.AxisListType

P = 128
HALF = 512
EPS = 1e-5
NEG = -3.0e38


class Consts:
    pass


def clear(nc, sems):
    nums = sorted(s.num for s in sems)
    starts = [n for n in nums if n - 1 not in nums]
    with nc.Block() as block:
        @block.sync
        def _(sp):
            for n in starts:
                end = n
                while end in nums:
                    end += 1
                sp.sem_clear(range(n, end))


def build_setup(nc, ctx, d):
    D, F = d["L0_ffn_w1"].shape[0] // 2, d["L0_ffn_w1"].shape[1]
    S = d["L0_ffn_slot_init"].shape[0]
    G3 = d["L0_ffn_Wih"].shape[0]
    KT, MT = D // P, G3 // P
    c = Consts()
    c.D, c.F, c.S, c.G3, c.KT, c.MT = D, F, S, G3, KT, MT

    def sb(name, shape, dt=F32):
        return ctx.enter_context(nc.sbuf_tensor(name, shape, dt))

    c.ident = sb("ident", [P, P])
    c.ones = sb("ones", [P, P])
    c.neg_half = sb("neg_half", [P, 8])
    c.w1 = sb("w1", [P, KT, F])
    c.hid_bias = sb("hid_bias", [P, 1])
    c.w2 = sb("w2", [P, S])
    c.b2 = sb("b2", [P, S])
    c.wih_t = sb("wih_t", [P, KT, G3])
    c.gate_bias = sb("gate_bias", [P, MT])
    c.gh_t = sb("gh_t", [P, MT, S])
    c.slots_t = sb("slots_t", [P, KT, S])
    c.wq = sb("wq", [P, KT, S])
    c.wk = sb("wk", [P, KT, S])
    c.bq = sb("bq", [S, 1])
    c.bk = sb("bk", [S, 1])
    c.wv = sb("wv", [P, KT, D])
    c.bv = sb("bv", [P, D])
    c.ln_g = sb("ln_g", [P, KT])
    c.ln_b = sb("ln_b", [P, KT])
    c.wvp = sb("wvp", [P, KT, D])
    c.bvp = sb("bvp", [P, KT])
    c.wo = sb("wo", [P, KT, D])

    with ExitStack() as own:
        def tmp(name, shape, dt=F32):
            return own.enter_context(nc.sbuf_tensor(name, shape, dt))

        def sem(name):
            return ctx.enter_context(nc.semaphore(name))

        w1_mean = tmp("w1_mean", [P, KT, F])
        wih = tmp("wih", [P, MT, D])
        whh = tmp("whh", [P, MT, D])
        whh_t = tmp("whh_t", [P, KT, G3])
        hh_bias = tmp("hh_bias", [P, MT])
        both_bias = tmp("both_bias", [P, MT])
        slots = tmp("slots", [S, D])
        slot_sum = tmp("slot_sum", [P, KT])
        slot_mean = tmp("slot_mean", [P, KT])
        b1 = tmp("b1", [P, 1])
        tau = tmp("tau", [P, 1])
        tau_neg = tmp("tau_neg", [P, 1])
        tau_abs = tmp("tau_abs", [P, 1])
        tau_den = tmp("tau_den", [P, 1])
        tau_inv = tmp("tau_inv", [P, 1])
        w2_raw = tmp("w2_raw", [P, S])
        b2_raw = tmp("b2_raw", [P, S])
        ps = own.enter_context(nc.psum_tensor("ps_setup", [P, 8, HALF], F32))

        loaded = sem("setup_loaded")
        loaded_act = sem("setup_loaded_act")
        filled = sem("setup_filled")
        ident_ready = sem("ident_ready")
        turned = sem("setup_turned")
        copied = sem("setup_copied")
        slots_taken = sem("setup_slots_taken")
        mean_ready = sem("slot_mean_ready")
        product_ready = sem("setup_product_ready")
        tau_step = sem("tau_step")
        bias_step = sem("bias_step")

        block = own.enter_context(nc.Block())
        n_sync, n_act = [], []

        @block.sync
        def _(sp):
            def load(dst, src):
                sp.dma_start(dst, src).then_inc(loaded, 16)
                n_sync.append(1)
            load(wih[:, :, :], d["L0_ffn_Wih"].rearrange("(m p) d -> p m d", p=P))
            load(whh[:, :, :], d["L0_ffn_Whh"].rearrange("(m p) d -> p m d", p=P))
            load(slots[:, :], d["L0_ffn_slot_init"])
            load(c.w1[:, :, :], d["L0_ffn_w1"][0:D, :].rearrange("(k p) f -> p k f", p=P))
            load(w1_mean[:, :, :], d["L0_ffn_w1"][D:2 * D, :].rearrange("(k p) f -> p k f", p=P))
            load(w2_raw[:, :], d["L0_ffn_w2"])
            load(b2_raw[:, :], d["L0_ffn_b2"].partition_broadcast(P))
            load(tau[:, :], d["L0_ffn_tau"].partition_broadcast(P))
            load(b1[:, :], d["L0_ffn_b1"].rearrange("(p o) -> p o", o=1))
            load(c.gate_bias[:, :], d["L0_ffn_bih"].rearrange("(m p o) -> p m o", p=P, o=1))
            load(hh_bias[:, :], d["L0_ffn_bhh"].rearrange("(m p o) -> p m o", p=P, o=1))

        @block.scalar
        def _(act):
            def load(dst, src):
                act.dma_start(dst, src).then_inc(loaded_act, 16)
                n_act.append(1)
            load(c.wq[:, :, :], d["L0_ffn_wq"].rearrange("(k p) f -> p k f", p=P))
            load(c.wk[:, :, :], d["L0_ffn_wk"].rearrange("(k p) f -> p k f", p=P))
            load(c.wv[:, :, :], d["L0_ffn_wv"].rearrange("(k p) f -> p k f", p=P))
            load(c.wvp[:, :, :], d["L0_ffn_wvp"].rearrange("(k p) f -> p k f", p=P))
            load(c.wo[:, :, :], d["L0_ffn_wo"].rearrange("(k p) f -> p k f", p=P))
            load(c.bv[:, :], d["L0_ffn_bv"].partition_broadcast(P))
            load(c.bq[:, :], d["L0_ffn_bq"].rearrange("(p o) -> p o", o=1))
            load(c.bk[:, :], d["L0_ffn_bk"].rearrange("(p o) -> p o", o=1))
            load(c.ln_g[:, :], d["L0_ffn_ln_g"].rearrange("(m p o) -> p m o", p=P, o=1))
            load(c.ln_b[:, :], d["L0_ffn_ln_b"].rearrange("(m p o) -> p m o", p=P, o=1))
            load(c.bvp[:, :], d["L0_ffn_bvp"].rearrange("(m p o) -> p m o", p=P, o=1))
            act.wait_ge(loaded_act, 16 * len(n_act))

        @block.gpsimd
        def _(pool):
            nc.gpsimd.memset(c.ident[:, :], 0.0).then_inc(filled, 1)
            pool.wait_ge(filled, 1)
            nc.gpsimd.affine_select(out=c.ident[:, :], in_=c.ident[:, :], compare_op=ALU.not_equal, fill=1.0,
                                    base=0, pattern=[[-1, P]], channel_multiplier=1).then_inc(ident_ready, 1)
            nc.gpsimd.memset(c.ones[:, :], 1.0).then_inc(filled, 1)
            nc.gpsimd.memset(c.neg_half[:, :], -0.5).then_inc(filled, 1)
            pool.wait_ge(filled, 3)

        groups = KT * MT * P // HALF

        @block.tensor
        def _(pe):
            pe.wait_ge(loaded, 16 * len(n_sync))
            pe.wait_ge(ident_ready, 1)
            for n, w in enumerate((wih, whh)):
                for g in range(groups):
                    for j in range(4):
                        k, m = divmod(4 * g + j, MT)
                        last = pe.transpose(ps[:, 3 * n + g, j * P:(j + 1) * P], w[:, m, k * P:(k + 1) * P],
                                            c.ident[:, :])
                    last.then_inc(turned, 1)
            for k in range(KT):
                last = pe.transpose(ps[:, 6, k * S:(k + 1) * S], slots[:, k * P:(k + 1) * P], c.ident[0:S, 0:S])
            last.then_inc(turned, 1)
            pe.wait_ge(mean_ready, 1)
            for k in range(KT):
                last = pe.matmul(ps[:, 7, 0:1], w1_mean[:, k, :], slot_mean[:, k:k + 1],
                                 start=(k == 0), stop=(k == KT - 1))
            last.then_inc(product_ready, 1)
            pe.wait_ge(copied, 2 * groups)
            for m in range(MT):
                for k in range(KT):
                    last = pe.matmul(ps[:, 0, m * S:(m + 1) * S], whh_t[:, k, m * P:(m + 1) * P],
                                     c.slots_t[:, k, :], start=(k == 0), stop=(k == KT - 1))
            last.then_inc(product_ready, 1)

        @block.vector
        def _(dve):
            dve.wait_ge(loaded, 16 * len(n_sync))
            dve.tensor_scalar(tau_neg[:, :], tau[:, :], -1.0, None, ALU.mult).then_inc(tau_step, 1)
            dve.wait_ge(tau_step, 1)
            dve.tensor_tensor(tau_abs[:, :], tau[:, :], tau_neg[:, :], ALU.max).then_inc(tau_step, 1)
            dve.wait_ge(tau_step, 2)
            dve.tensor_scalar(tau_den[:, :], tau_abs[:, :], 0.1, None, ALU.add).then_inc(tau_step, 1)
            dve.wait_ge(tau_step, 3)
            dve.reciprocal(tau_inv[:, :], tau_den[:, :]).then_inc(tau_step, 1)
            dve.wait_ge(tau_step, 4)
            dve.tensor_scalar(c.w2[:, :], w2_raw[:, :], tau_inv[:, 0:1], None, ALU.mult).then_inc(tau_step, 1)
            dve.tensor_scalar(c.b2[:, :], b2_raw[:, :], tau_inv[:, 0:1], None, ALU.mult).then_inc(tau_step, 1)
            dve.tensor_tensor(both_bias[:, :], c.gate_bias[:, :], hh_bias[:, :], ALU.add).then_inc(bias_step, 1)
            for n, w_t in enumerate((c.wih_t, whh_t)):
                flat = w_t[:, :, :].rearrange("p k g -> p (k g)")
                for g in range(groups):
                    dve.wait_ge(turned, 3 * n + g + 1)
                    dve.tensor_copy(flat[:, g * HALF:(g + 1) * HALF], ps[:, 3 * n + g, :]).then_inc(copied, 1)
            dve.wait_ge(turned, 2 * groups + 1)
            src = ps[:, 6, 0:KT * S].rearrange("p (k s) -> p k s", k=KT)
            dve.tensor_copy(c.slots_t[:, :, :], src).then_inc(slots_taken, 1)
            dve.wait_ge(slots_taken, 1)
            dve.tensor_reduce(slot_sum[:, :], c.slots_t[:, :, :], AX.X, ALU.add).then_inc(slots_taken, 1)
            dve.wait_ge(slots_taken, 2)
            dve.tensor_scalar(slot_mean[:, :], slot_sum[:, :], 1.0 / S, None, ALU.mult).then_inc(mean_ready, 1)
            dve.wait_ge(product_ready, 1)
            dve.tensor_tensor(c.hid_bias[:, :], ps[:, 7, 0:1], b1[:, :], ALU.add).then_inc(bias_step, 1)
            dve.wait_ge(product_ready, 2)
            dve.wait_ge(bias_step, 1)
            for m in range(MT):
                bias = both_bias if m < 2 * KT else hh_bias
                dve.tensor_scalar(c.gh_t[:, m, :], ps[:, 0, m * S:(m + 1) * S], bias[:, m:m + 1], None,
                                  ALU.add).then_inc(bias_step, 1)
            dve.wait_ge(bias_step, 2 + MT)
            dve.wait_ge(tau_step, 6)
    return c


def build_ffn(nc, c, tag, x_in, x_out, bo):
    B, T, D = x_in.shape
    S, KT, MT, F = c.S, c.KT, c.MT, c.F
    TT = T // P
    NS = B * S
    PAIRS = B // 2
    R = 4

    def rows(t, b):
        return t[bass.ds(b, 1)].rearrange("a (p t) d -> (a p) t d", t=TT)

    with ExitStack() as ctx:
        def sb(name, shape, dt=F32, on=ctx):
            return on.enter_context(nc.sbuf_tensor(f"{tag}_{name}", shape, dt))

        def sem(name):
            sems.append(ctx.enter_context(nc.semaphore(f"{tag}_{name}")))
            return sems[-1]

        sems = []
        alpha_t = sb("alpha_t", [P, PAIRS, T])
        si_t = sb("si_t", [P, KT, NS])
        slot_out = sb("slot_out", [P, PAIRS, 2, D])

        with ExitStack() as own:
            x_ring = sb("x_ring", [P, R, TT, D + 1], F32, own)
            stats = sb("stats", [P, TT, 6], F32, own)
            mean_var = sb("mean_var", [P, TT, 2], F32, own)
            waited = sb("waited", [P, 1], F32, own)
            var_eps = sb("var_eps", [P, TT], F32, own)
            rstd = sb("rstd", [P, TT], F32, own)
            shift = sb("shift", [P, TT], F32, own)
            xn_t = sb("xn_t", [P, KT, T], F32, own)
            hid = sb("hid", [P, T], F32, own)
            logit = sb("logit", [P, TT, S], F32, own)
            top8 = sb("top8", [P, TT, 8], F32, own)
            rest = sb("rest", [P, TT, S], F32, own)
            shifted = sb("shifted", [P, TT, S], F32, own)
            expd = sb("expd", [P, TT, S], F32, own)
            picked = sb("picked", [P, TT, S], F32, own)
            total = sb("total", [P, TT], F32, own)
            inv_total = sb("inv_total", [P, TT], F32, own)
            alpha = sb("alpha", [P, 2, TT, 2, S], F32, own)
            den_eps = sb("den_eps", [P, 1], F32, own)
            den_inv = sb("den_inv", [P, 1], F32, own)
            si_rows = sb("si_rows", [P, D], F32, own)
            ps_turn = own.enter_context(nc.psum_tensor(f"{tag}_ps_turn", [P, 2, HALF], F32))
            ps_hid = own.enter_context(nc.psum_tensor(f"{tag}_ps_hid", [P, 2, HALF], F32))
            ps_logit = own.enter_context(nc.psum_tensor(f"{tag}_ps_logit", [P, TT, S], F32))
            ps_si = own.enter_context(nc.psum_tensor(f"{tag}_ps_si", [P, HALF], F32))
            ps_at = own.enter_context(nc.psum_tensor(f"{tag}_ps_at", [P, 2, HALF], F32))

            x_loaded = [sem(f"x_loaded{r}") for r in range(R)]
            ones_set = sem("ones_set")
            stat_step = sem("stat_step")
            var_ready = sem("var_ready")
            rstd_ready = sem("rstd_ready")
            shift_set = sem("shift_set")
            xn_low, xn_high = sem("xn_low"), sem("xn_high")
            turned = sem("turned")
            turn_taken = sem("turn_taken")
            hid_ready = sem("hid_ready")
            gelu_done = sem("gelu_done")
            logit_ready = sem("logit_ready")
            logit_taken = sem("logit_taken")
            top_step = sem("top_step")
            shift_ready = sem("shift_ready")
            exp_done = sem("exp_done")
            pick_step = sem("pick_step")
            alpha_ready = sem("alpha_ready")
            si_ready = sem("si_ready")
            den_step = sem("den_step")
            si_taken = sem("si_taken")
            at_ready, at_taken = sem("at_ready"), sem("at_taken")
            si_turned, si_t_ready = sem("si_turned"), sem("si_t_ready")

            block = own.enter_context(nc.Block())
            FILLS = KT * T // HALF
            assert FILLS == 4 and TT == 8
            LOW = TT // 2

            def over_batches(eng, step):
                for b in range(R):
                    step(b, 0, b, b)
                with eng.Fori(1, B // R - 1, 1) as q:
                    for r in range(R):
                        step(q * R + r, q, r, R + r)
                for b in range(B - R, B + 3):
                    step(b, b // R, b % R, b)

            def pairs_of(q, r):
                return q * (R // 2) + r // 2

            @block.sync
            def _(sp):
                for r in range(R):
                    sp.dma_start(x_ring[:, r, :, 0:D], rows(x_in, r)).then_inc(x_loaded[r], 16)

                def load(b, q, r, n):
                    if 2 <= n < B - 2:
                        sp.wait_ge(si_ready, b - 1)
                        sp.dma_start(x_ring[:, (r + 2) % R, :, 0:D], rows(x_in, b + 2)).then_inc(x_loaded[(r + 2) % R], 16)
                over_batches(sp, load)

            @block.gpsimd
            def _(pool):
                pool.memset(x_ring[:, :, :, D:D + 1], 1.0).then_inc(ones_set, 1)

                def rsqrt(b):
                    pool.wait_ge(var_ready, b + 1)
                    pool.tensor_tensor(rstd[:, :], var_eps[:, :], c.neg_half[:, 0:TT], ALU.pow).then_inc(rstd_ready, 1)

                rsqrt(0)

                def step(b, q, r, n):
                    if n + 1 < B:
                        pool.wait_ge(xn_high, b + 1)
                        rsqrt(b + 1)
                over_batches(pool, step)

            @block.vector
            def _(dve):
                def statistics(b, r):
                    base = b * (2 * TT)
                    dve.wait_ge(x_loaded[r], b * (16 // R) + (16 - r * (16 // R)))
                    for t in range(TT):
                        dve.bn_stats(stats[:, t, :], x_ring[:, r, t, 0:D]).then_inc(stat_step, 1)
                    dve.wait_ge(stat_step, base + TT)
                    dve.memset(waited[:, :], 0.0)
                    for t in range(TT):
                        dve.bn_aggr(mean_var[:, t, :], stats[:, t, :]).then_inc(stat_step, 1)
                    dve.wait_ge(stat_step, base + 2 * TT)
                    dve.tensor_scalar(var_eps[:, :], mean_var[:, :, 1], EPS, None, ALU.add).then_inc(var_ready, 1)

                def normalise(b, r):
                    dve.wait_ge(rstd_ready, b + 1)
                    dve.scalar_tensor_tensor(shift[:, :], mean_var[:, :, 0], -1.0, rstd[:, :], ALU.mult,
                                             ALU.mult).then_inc(shift_set, 1)
                    for t in range(LOW):
                        last = dve.tensor_scalar(x_ring[:, r, t, 0:D], x_ring[:, r, t, 0:D], mean_var[:, t, 0:1],
                                                 rstd[:, t:t + 1], ALU.subtract, ALU.mult)
                    last.then_inc(xn_low, 1)

                def find_top(b):
                    dve.wait_ge(logit_ready, b + 1)
                    dve.tensor_tensor(logit[:, :, :], ps_logit[:, :, :], c.b2[:, :].unsqueeze(1).to_broadcast([P, TT, S]),
                                      ALU.add).then_inc(logit_taken, 1)
                    dve.wait_ge(logit_taken, b + 1)
                    dve.memset(waited[:, :], 0.0)
                    for t in range(TT):
                        dve.max(top8[:, t, :], logit[:, t, :]).then_inc(top_step, 1)
                    dve.wait_ge(top_step, b * (2 * TT) + TT)
                    dve.tensor_tensor(shifted[:, :, :], logit[:, :, :], top8[:, :, 0:1].to_broadcast([P, TT, S]),
                                      ALU.subtract).then_inc(shift_ready, 1)
                    for t in range(TT):
                        dve.match_replace(out=rest[:, t, :], in_to_replace=top8[:, t, :], in_values=logit[:, t, :],
                                          imm_value=NEG).then_inc(top_step, 1)

                def weigh(b, pair, r, n):
                    dve.wait_ge(top_step, b * (2 * TT) + 2 * TT)
                    dve.wait_ge(exp_done, b + 1)
                    dve.scalar_tensor_tensor(picked[:, :, :], rest[:, :, :], NEG, expd[:, :, :], ALU.is_equal,
                                             ALU.mult).then_inc(pick_step, 1)
                    dve.wait_ge(pick_step, b * 3 + 1)
                    dve.tensor_reduce(total[:, :], picked[:, :, :], AX.X, ALU.add).then_inc(pick_step, 1)
                    dve.wait_ge(pick_step, b * 3 + 2)
                    dve.reciprocal(inv_total[:, :], total[:, :]).then_inc(pick_step, 1)
                    dve.wait_ge(pick_step, b * 3 + 3)
                    if n >= R:
                        dve.wait_ge(at_ready, pair - 1)
                    dve.tensor_tensor(alpha[:, r // 2, :, r % 2, :], picked[:, :, :],
                                      inv_total[:, :].unsqueeze(2).to_broadcast([P, TT, S]),
                                      ALU.mult).then_inc(alpha_ready, 1)

                def divide(pairs, n):
                    dve.wait_ge(si_ready, pairs * 2)
                    dve.tensor_scalar(den_eps[:, :], ps_si[:, D:D + 1], 1e-8, None, ALU.add).then_inc(den_step, 1)
                    dve.wait_ge(den_step, pairs * 2 - 1)
                    dve.reciprocal(den_inv[:, :], den_eps[:, :]).then_inc(den_step, 1)
                    dve.wait_ge(den_step, pairs * 2)
                    if n >= 5:
                        dve.wait_ge(si_turned, pairs - 1)
                    dve.tensor_scalar(si_rows[:, :], ps_si[:, 0:D], den_inv[:, 0:1], None, ALU.mult).then_inc(si_taken, 1)

                statistics(0, 0)
                normalise(0, 0)

                def step(b, q, r, n):
                    if 1 <= n <= B:
                        find_top(b - 1)
                    if n + 1 < B:
                        statistics(b + 1, (r + 1) % R)
                    if 1 <= n <= B:
                        weigh(b - 1, q * (R // 2) + (r - 1) // 2, (r - 1) % R, n - 1)
                    if n + 1 < B:
                        normalise(b + 1, (r + 1) % R)
                    if n % 2 and 3 <= n <= B + 1:
                        divide(pairs_of(q, r), n)
                over_batches(dve, step)

            @block.tensor
            def _(pe):
                def turn_rows(b, r, n, fills):
                    for f in fills:
                        if f < 2:
                            pe.wait_ge((xn_low, xn_high)[f], b + 1)
                        if n * FILLS + f >= 2:
                            pe.wait_ge(turn_taken, b * FILLS + (f - 1))
                        for j in range(4):
                            k, t = divmod(4 * f + j, TT)
                            last = pe.transpose(ps_turn[:, f % 2, j * P:(j + 1) * P],
                                                x_ring[:, r, t, k * P:(k + 1) * P], c.ident[:, :])
                        last.then_inc(turned, 1)

                def hidden(b, n):
                    pe.wait_ge(turn_taken, b * FILLS + FILLS)
                    if n >= 1:
                        pe.wait_ge(gelu_done, b)
                    for h in range(T // HALF):
                        for k in range(KT):
                            last = pe.matmul(ps_hid[:, h, :], c.w1[:, k, :], xn_t[:, k, h * HALF:(h + 1) * HALF],
                                             start=(k == 0), stop=(k == KT - 1))
                    last.then_inc(hid_ready, 1)

                def logits(b, n):
                    pe.wait_ge(gelu_done, b + 1)
                    if n >= 1:
                        pe.wait_ge(logit_taken, b)
                    for t in range(TT):
                        last = pe.matmul(ps_logit[:, t, :], hid[:, t * P:(t + 1) * P], c.w2[:, :], start=True, stop=True)
                    last.then_inc(logit_ready, 1)

                def sum_tokens(b, pair, r, n, tiles):
                    e = r % 2
                    if tiles[0] == 0:
                        pe.wait_ge(alpha_ready, b + 1)
                        if n >= 2 and e == 0:
                            pe.wait_ge(si_taken, pair)
                    for t in tiles:
                        last = pe.matmul(ps_si[e * S:(e + 1) * S, 0:D + 1], alpha[:, r // 2, t, e, :], x_ring[:, r, t, :],
                                         start=(t == 0), stop=(t == TT - 1), skip_group_check=True)
                    if t == TT - 1:
                        last.then_inc(si_ready, 1)

                def turn_weights(pairs, r, n):
                    if n >= 5:
                        pe.wait_ge(si_t_ready, pairs - 1)
                    for t in range(TT):
                        last = pe.transpose(ps_at[:, t // 4, (t % 4) * P:(t % 4 + 1) * P],
                                            alpha[:, (r - 3) % R // 2, t].rearrange("p e s -> p (e s)"), c.ident[:, :])
                    last.then_inc(at_ready, 1)

                def turn_sums(pairs):
                    pe.wait_ge(at_taken, pairs - 1)
                    pe.wait_ge(si_taken, pairs - 1)
                    for k in range(KT):
                        last = pe.transpose(ps_at[:, 0, k * P:(k + 1) * P], si_rows[:, k * P:(k + 1) * P], c.ident[:, :])
                    last.then_inc(si_turned, 1)

                pe.wait_ge(ones_set, 1)

                def step(b, q, r, n):
                    def sums(*tiles):
                        if 2 <= n <= B + 1:
                            sum_tokens(b - 2, q * (R // 2) + (r - 2) // 2, (r - 2) % R, n - 2, tiles)
                    if n < B:
                        turn_rows(b, r, n, (0, 1))
                    sums(0)
                    if n < B:
                        turn_rows(b, r, n, (2, 3))
                    sums(1, 2, 3)
                    if n < B:
                        hidden(b, n)
                    if n % 2 == 0 and n >= 4:
                        turn_sums(pairs_of(q, r))
                    sums(4, 5, 6, 7)
                    if n % 2 and 3 <= n <= B + 1:
                        turn_weights(pairs_of(q, r), r, n)
                    if n < B:
                        logits(b, n)
                over_batches(pe, step)

            @block.scalar
            def _(act):
                def normalise(b, r):
                    act.wait_ge(shift_set, b + 1)
                    for t in range(LOW, TT):
                        last = act.activation(x_ring[:, r, t, 0:D], x_ring[:, r, t, 0:D], ACT.Identity,
                                              bias=shift[:, t:t + 1], scale=rstd[:, t:t + 1])
                    last.then_inc(xn_high, 1)

                normalise(0, 0)

                def step(b, q, r, n):
                    flat = xn_t[:, :, :].rearrange("p k t -> p (k t)")
                    if n < B:
                        for f in range(FILLS):
                            act.wait_ge(turned, b * FILLS + (f + 1))
                            act.activation(flat[:, f * HALF:(f + 1) * HALF], ps_turn[:, f % 2, :],
                                           ACT.Identity).then_inc(turn_taken, 1)
                    if 1 <= n <= B:
                        act.wait_ge(shift_ready, b)
                        act.activation(expd[:, :, :], shifted[:, :, :], ACT.Exp).then_inc(exp_done, 1)
                    if n < B:
                        act.wait_ge(hid_ready, b + 1)
                        if n >= 1:
                            act.wait_ge(logit_ready, b)
                        act.activation(hid[:, :].rearrange("p (n h) -> p n h", n=2), ps_hid[:, :, :], ACT.Gelu,
                                       bias=c.hid_bias[:, 0:1]).then_inc(gelu_done, 1)
                    if n + 1 < B:
                        normalise(b + 1, (r + 1) % R)
                    pairs = pairs_of(q, r)
                    if n % 2 and 3 <= n <= B + 1:
                        act.wait_ge(at_ready, pairs)
                        act.activation(alpha_t[:, bass.ds(pairs - 1, 1), :].rearrange("p a (n h) -> p (a n) h", n=2),
                                       ps_at[:, :, :], ACT.Identity).then_inc(at_taken, 1)
                    if n % 2 == 0 and n >= 4:
                        act.wait_ge(si_turned, pairs - 1)
                        act.activation(si_t[:, :, bass.ds((pairs - 2) * P, P)],
                                       ps_at[:, 0, 0:D].rearrange("p (k s) -> p k s", k=KT),
                                       ACT.Identity).then_inc(si_t_ready, 1)
                over_batches(act, step)

        with ExitStack() as own:
            gates = sb("gates", [P, 2 * KT, NS], F32, own)
            pre = sb("pre", [P, KT, NS], F32, own)
            cand = sb("cand", [P, KT, NS], F32, own)
            mix = sb("mix", [P, KT, NS], F32, own)
            mix_z = sb("mix_z", [P, KT, NS], F32, own)
            new_t = sb("new_t", [P, KT, NS], F32, own)
            q_t = sb("q_t", [S, NS], F32, own)
            k_t = sb("k_t", [S, NS], F32, own)
            v_sb = sb("v_sb", [P, PAIRS, D], F32, own)
            s_max = sb("s_max", [P, PAIRS], F32, own)
            s_shift = sb("s_shift", [P, PAIRS, S], F32, own)
            s_exp = sb("s_exp", [P, PAIRS, S], F32, own)
            s_sum = sb("s_sum", [P, PAIRS], F32, own)
            s_inv = sb("s_inv", [P, PAIRS], F32, own)
            attn = sb("attn", [P, PAIRS, P], F32, own)
            attn_t = sb("attn_t", [P, PAIRS, P], F32, own)
            stats = sb("y_stats", [P, PAIRS, 6], F32, own)
            mean_var = sb("y_mean_var", [P, PAIRS, 2], F32, own)
            var_eps = sb("y_var_eps", [P, PAIRS], F32, own)
            rstd = sb("y_rstd", [P, PAIRS], F32, own)
            y_hat = sb("y_hat", [P, PAIRS, D], F32, own)
            b_out = sb("b_out", [P, D], F32, own)
            y_t, val_t = pre, mix
            ps = own.enter_context(nc.psum_tensor(f"{tag}_ps_slot", [P, 8, HALF], F32))

            gi_ready, gate_sum = sem("gi_ready"), sem("gate_sum")
            tanh_done, gate_ready = sem("tanh_done"), sem("gate_ready")
            cand_step, cand_ready, mix_step = sem("cand_step"), sem("cand_ready"), sem("mix_step")
            qk_ready, qk_taken = sem("qk_ready"), sem("qk_taken")
            v_ready, v_taken = sem("v_ready"), sem("v_taken")
            score_ready, soft_step, soft_exp = sem("score_ready"), sem("soft_step"), sem("soft_exp")
            attn_zero, attn_ready = sem("attn_zero"), sem("attn_ready")
            attn_turned, attn_taken = sem("attn_turned"), sem("attn_taken")
            y_ready, y_step = sem("y_ready"), sem("y_step")
            y_var, y_rstd, yhat_ready = sem("y_var"), sem("y_rstd"), sem("yhat_ready")
            y_turned, yt_ready = sem("y_turned"), sem("yt_ready")
            val_ready, val_taken = sem("val_ready"), sem("val_taken")
            out_ready, out_taken = sem("out_ready"), sem("out_taken")
            b_out_loaded, out_zero = sem("b_out_loaded"), sem("out_zero")

            block = own.enter_context(nc.Block())
            NH = NS // HALF

            def pair_banks(n):
                return ps[:, 2 * (n % 4):2 * (n % 4) + NH, :]

            def cols(ap):
                return ap.rearrange("p (n h) -> p n h", h=HALF)

            @block.tensor
            def _(pe):
                def project(n, weights, moving, rows_out=P):
                    for h in range(NH):
                        for k in range(KT):
                            last = pe.matmul(ps[0:rows_out, 2 * (n % 4) + h, :], weights(k),
                                             moving[:, k, h * HALF:(h + 1) * HALF], start=(k == 0), stop=(k == KT - 1))
                    return last
                for m in range(MT):
                    if m >= 4:
                        pe.wait_ge(gate_sum, m - 3)
                    project(m, lambda k: c.wih_t[:, k, m * P:(m + 1) * P], si_t).then_inc(gi_ready, 1)
                pe.wait_ge(mix_step, 3 * KT)
                project(2, lambda k: c.wq[:, k, :], new_t, S).then_inc(qk_ready, 1)
                project(3, lambda k: c.wk[:, k, :], new_t, S).then_inc(qk_ready, 1)
                for pair in range(PAIRS):
                    for k in range(KT):
                        last = pe.matmul(ps[:, pair // 2, (pair % 2) * D:(pair % 2 + 1) * D],
                                         new_t[:, k, pair * P:(pair + 1) * P], c.wv[:, k, :],
                                         start=(k == 0), stop=(k == KT - 1))
                    if pair % 2:
                        last.then_inc(v_ready, 1)
                pe.wait_ge(qk_taken, 2)
                for b in range(B):
                    half = b % 2 * S
                    last = pe.matmul(ps[half:half + S, 4, b // 2 * S:(b // 2 + 1) * S], q_t[:, b * S:(b + 1) * S],
                                     k_t[:, b * S:(b + 1) * S], start=True, stop=True)
                last.then_inc(score_ready, 1)
                pe.wait_ge(attn_ready, 2)
                for pair in range(PAIRS):
                    last = pe.transpose(ps[:, 6 + pair // 4, (pair % 4) * P:(pair % 4 + 1) * P], attn[:, pair, :],
                                        c.ident[:, :])
                last.then_inc(attn_turned, 1)
                pe.wait_ge(attn_taken, 1)
                pe.wait_ge(v_taken, PAIRS // 2)
                for pair in range(PAIRS):
                    y = ps[:, pair // 2, (pair % 2) * D:(pair % 2 + 1) * D]
                    pe.matmul(y, attn_t[:, pair, :], v_sb[:, pair, :], start=True, stop=True)
                    for k in range(KT):
                        last = pe.matmul(y[:, k * P:(k + 1) * P], new_t[:, k, pair * P:(pair + 1) * P], c.ident[:, :],
                                         start=False, stop=True, skip_group_check=True)
                    last.then_inc(y_ready, 1)
                pe.wait_ge(yhat_ready, 1)
                for k in range(KT):
                    for pair in range(PAIRS):
                        last = pe.transpose(ps[:, 4 + 2 * k + pair // 4, (pair % 4) * P:(pair % 4 + 1) * P],
                                            y_hat[:, pair, k * P:(k + 1) * P], c.ident[:, :])
                    last.then_inc(y_turned, 1)
                pe.wait_ge(yt_ready, KT)
                for m in range(KT):
                    project(m, lambda k: c.wvp[:, k, m * P:(m + 1) * P], y_t).then_inc(val_ready, 1)
                pe.wait_ge(val_taken, KT)
                for pair in range(PAIRS):
                    for k in range(KT):
                        last = pe.matmul(ps[:, 4 + pair // 2, (pair % 2) * D:(pair % 2 + 1) * D],
                                         val_t[:, k, pair * P:(pair + 1) * P], c.wo[:, k, :],
                                         start=(k == 0), stop=(k == KT - 1))
                    if pair % 2:
                        last.then_inc(out_ready, 1)

            @block.vector
            def _(dve):
                def per_batch(ap):
                    return ap.unsqueeze(1).to_broadcast([P, B, S])

                def by_batch(ap):
                    return ap.rearrange("p (b s) -> p b s", s=S)

                def banks_by_batch(n):
                    return pair_banks(n).rearrange("p n (b s) -> p (n b) s", s=S)

                dve.memset(attn[:, :, :], 0.0).then_inc(attn_zero, 1)
                for m in range(2 * KT):
                    dve.wait_ge(gi_ready, m + 1)
                    dve.tensor_tensor(by_batch(gates[:, m, :]), banks_by_batch(m), per_batch(c.gh_t[:, m, :]),
                                      ALU.add).then_inc(gate_sum, 1)
                for m in range(2 * KT):
                    dve.wait_ge(tanh_done, m + 1)
                    dve.tensor_scalar(gates[:, m, :], gates[:, m, :], 0.5, 0.5, ALU.mult, ALU.add).then_inc(gate_ready, 1)
                for k in range(KT):
                    m = 2 * KT + k
                    dve.wait_ge(gate_ready, k + 1)
                    dve.tensor_tensor(by_batch(pre[:, k, :]), by_batch(gates[:, k, :]), per_batch(c.gh_t[:, m, :]),
                                      ALU.mult).then_inc(cand_step, 1)
                    dve.wait_ge(gi_ready, m + 1)
                    dve.wait_ge(cand_step, 2 * k + 1)
                    dve.scalar_tensor_tensor(cols(pre[:, k, :]), pair_banks(m), c.gate_bias[:, m:m + 1],
                                             cols(pre[:, k, :]), ALU.add, ALU.add).then_inc(cand_step, 1)
                dve.wait_ge(gate_ready, 2 * KT)
                for k in range(KT):
                    old = per_batch(c.slots_t[:, k, :])
                    dve.wait_ge(cand_ready, k + 1)
                    dve.tensor_tensor(by_batch(mix[:, k, :]), old, by_batch(cand[:, k, :]), ALU.subtract).then_inc(mix_step, 1)
                    dve.wait_ge(mix_step, 3 * k + 1)
                    dve.tensor_tensor(mix_z[:, k, :], mix[:, k, :], gates[:, KT + k, :], ALU.mult).then_inc(mix_step, 1)
                    dve.wait_ge(mix_step, 3 * k + 2)
                    dve.tensor_tensor(new_t[:, k, :], mix_z[:, k, :], cand[:, k, :], ALU.add).then_inc(mix_step, 1)
                for g in range(PAIRS // 2):
                    dve.wait_ge(v_ready, g + 1)
                    dve.tensor_tensor(v_sb[:, 2 * g:2 * g + 2, :], ps[:, g, :].rearrange("p (a d) -> p a d", d=D),
                                      c.bv[:, :].unsqueeze(1).to_broadcast([P, 2, D]), ALU.add).then_inc(v_taken, 1)
                scores = ps[:, 4, :].rearrange("p (a s) -> p a s", s=S)
                dve.wait_ge(score_ready, 1)
                dve.tensor_reduce(s_max[:, :], scores, AX.X, ALU.max).then_inc(soft_step, 1)
                dve.wait_ge(soft_step, 1)
                dve.tensor_tensor(s_shift[:, :, :], scores, s_max[:, :].unsqueeze(2).to_broadcast([P, PAIRS, S]),
                                  ALU.subtract).then_inc(soft_step, 1)
                dve.wait_ge(soft_exp, 1)
                dve.tensor_reduce(s_sum[:, :], s_exp[:, :, :], AX.X, ALU.add).then_inc(soft_step, 1)
                dve.wait_ge(soft_step, 3)
                dve.reciprocal(s_inv[:, :], s_sum[:, :]).then_inc(soft_step, 1)
                dve.wait_ge(soft_step, 4)
                dve.wait_ge(attn_zero, 1)
                for h in range(2):
                    rows_h = slice(h * S, (h + 1) * S)
                    dve.tensor_tensor(attn[rows_h, :, rows_h], s_exp[rows_h, :, :],
                                      s_inv[rows_h, :].unsqueeze(2).to_broadcast([S, PAIRS, S]),
                                      ALU.mult).then_inc(attn_ready, 1)
                dve.wait_ge(attn_turned, 1)
                dve.tensor_copy(attn_t[:, :, :].rearrange("p a s -> p (a s)").rearrange("p (n h) -> p n h", h=HALF),
                                ps[:, 6:8, :]).then_inc(attn_taken, 1)
                dve.wait_ge(y_ready, PAIRS)
                y_rows = ps[:, 0:PAIRS // 2, :].rearrange("p n (a d) -> p (n a) d", d=D)
                for a in range(PAIRS):
                    dve.bn_stats(stats[:, a, :], y_rows[:, a, :]).then_inc(y_step, 1)
                dve.wait_ge(y_step, PAIRS)
                for a in range(PAIRS):
                    dve.bn_aggr(mean_var[:, a, :], stats[:, a, :]).then_inc(y_step, 1)
                dve.wait_ge(y_step, 2 * PAIRS)
                dve.tensor_scalar(var_eps[:, :], mean_var[:, :, 1], EPS, None, ALU.add).then_inc(y_var, 1)
                dve.wait_ge(y_rstd, 1)
                for a in range(PAIRS):
                    last = dve.tensor_scalar(y_hat[:, a, :], y_rows[:, a, :], mean_var[:, a, 0:1], rstd[:, a:a + 1],
                                             ALU.subtract, ALU.mult)
                last.then_inc(yhat_ready, 1)
                dve.wait_ge(b_out_loaded, 16)
                dve.wait_ge(out_zero, 1)
                for g in range(PAIRS // 2):
                    dve.wait_ge(out_ready, g + 1)
                    for h in range(2):
                        rows_h = slice(h * S, (h + 1) * S)
                        dve.tensor_tensor(slot_out[rows_h, 2 * g:2 * g + 2, h, :],
                                          ps[rows_h, 4 + g, :].rearrange("p (a d) -> p a d", d=D),
                                          b_out[rows_h, :].unsqueeze(1).to_broadcast([S, 2, D]),
                                          ALU.add).then_inc(out_taken, 1)
                dve.wait_ge(out_taken, PAIRS)

            @block.sync
            def _(sp):
                sp.dma_start(b_out[:, :], bo.partition_broadcast(P)).then_inc(b_out_loaded, 16)

            @block.gpsimd
            def _(pool):
                pool.memset(slot_out[:, :, :, :], 0.0).then_inc(out_zero, 1)
                pool.wait_ge(y_var, 1)
                pool.tensor_tensor(rstd[:, :], var_eps[:, :], c.neg_half[:, 0:PAIRS], ALU.pow).then_inc(y_rstd, 1)

            @block.scalar
            def _(act):
                for m in range(2 * KT):
                    act.wait_ge(gate_sum, m + 1)
                    act.activation(gates[:, m, :], gates[:, m, :], ACT.Tanh, scale=0.5).then_inc(tanh_done, 1)
                for k in range(KT):
                    act.wait_ge(cand_step, 2 * k + 2)
                    act.activation(cand[:, k, :], pre[:, k, :], ACT.Tanh).then_inc(cand_ready, 1)
                for n, (dst, bias) in enumerate(((q_t, c.bq), (k_t, c.bk))):
                    act.wait_ge(qk_ready, n + 1)
                    act.activation(cols(dst[:, :]), ps[0:S, 4 + 2 * n:6 + 2 * n, :], ACT.Identity,
                                   bias=bias[:, 0:1]).then_inc(qk_taken, 1)
                act.wait_ge(soft_step, 2)
                act.activation(s_exp[:, :, :], s_shift[:, :, :], ACT.Exp, scale=float(S) ** -0.5).then_inc(soft_exp, 1)
                for k in range(KT):
                    act.wait_ge(y_turned, k + 1)
                    act.activation(cols(y_t[:, k, :]), ps[:, 4 + 2 * k:6 + 2 * k, :], ACT.Identity,
                                   bias=c.ln_b[:, k:k + 1], scale=c.ln_g[:, k:k + 1]).then_inc(yt_ready, 1)
                for m in range(KT):
                    act.wait_ge(val_ready, m + 1)
                    act.activation(cols(val_t[:, m, :]), pair_banks(m), ACT.Identity,
                                   bias=c.bvp[:, m:m + 1]).then_inc(val_taken, 1)

        with ExitStack() as own:
            RP = 4
            xc = sb("xc", [P, RP, 2, TT, D], F32, own)
            ps = own.enter_context(nc.psum_tensor(f"{tag}_ps_back", [P, TT, 2, D], F32))
            back_loaded = [sem(f"back_loaded{r}") for r in range(RP)]
            stored = [sem(f"stored{r}") for r in range(RP)]
            mixed, added = sem("mixed"), sem("added")
            block = own.enter_context(nc.Block())

            def over_pairs(eng, step):
                step(0, True)
                with eng.Fori(1, PAIRS // RP, 1) as q:
                    step(q, False)

            @block.sync
            def _(sp):
                def step(q, first):
                    for r in range(RP):
                        if not first:
                            sp.wait_ge(stored[r], q * 32)
                        for e in range(2):
                            sp.dma_start(xc[:, r, e], rows(x_in, q * (2 * RP) + (2 * r + e))).then_inc(back_loaded[r], 16)
                over_pairs(sp, step)

            @block.tensor
            def _(pe):
                def step(q, first):
                    for r in range(RP):
                        for t in range(TT):
                            if not (first and r == 0):
                                pe.wait_ge(added, q * (RP * TT) + ((r - 1) * TT + t + 1))
                            pe.matmul(ps[:, t].rearrange("p e d -> p (e d)"),
                                      alpha_t[:, bass.ds(q * RP + r, 1), t * P:(t + 1) * P].rearrange("p a n -> p (a n)"),
                                      slot_out[:, bass.ds(q * RP + r, 1), :, :].rearrange("p a e d -> p (a e d)"),
                                      start=True, stop=True).then_inc(mixed, 1)
                over_pairs(pe, step)

            @block.vector
            def _(dve):
                def step(q, first):
                    for r in range(RP):
                        dve.wait_ge(back_loaded[r], q * 32 + 32)
                        for t in range(TT):
                            dve.wait_ge(mixed, q * (RP * TT) + (r * TT + t + 1))
                            dve.scalar_tensor_tensor(xc[:, r, :, t, :], ps[:, t], 0.5, xc[:, r, :, t, :], ALU.mult,
                                                     ALU.add).then_inc(added, 1)
                over_pairs(dve, step)

            @block.scalar
            def _(act):
                def step(q, first):
                    for r in range(RP):
                        act.wait_ge(added, q * (RP * TT) + (r + 1) * TT)
                        for e in range(2):
                            act.dma_start(rows(x_out, q * (2 * RP) + (2 * r + e)), xc[:, r, e]).then_inc(stored[r], 16)
                over_pairs(act, step)
                for r in range(RP):
                    act.wait_ge(stored[r], PAIRS // RP * 32)

        clear(nc, sems)


def build_attention(nc, c, x_in, x_out, w_qkv, b_qkv, w_out, b_out):
    B, T, D = x_in.shape
    KT, TT = D // P, T // P
    H, DH = 16, D // 16
    GH = 4
    NG = H // GH
    CHUNKS = T // HALF
    GU = GH * TT * CHUNKS
    BU = NG * GU
    AHEAD = GU + 16
    NQ = 4
    Q_PARTS, K_PARTS = (0, 0, 1, 0, 2, 1), (0, 1, 0, 2, 0, 1)
    SR = len(Q_PARTS) * DH
    PREP = 3
    B0 = 2

    QK_AT = [76, GU + 37, 2 * GU + 37, 3 * GU + 37]
    X_AT = 88
    V_AT = [70, 83, 2 * GU + 8, 2 * GU + 14]
    RATE = {"turn_x": 4, "qk": 2 * NG, "v": NG, "turn_max": NG, "turn_o": TT, "turn_ctx": TT, "project": TT}

    def jobs(b):
        out = []
        for qt in range(TT):
            out += [(6 + 8 * qt, "turn_o", TT * (b - 1) + qt), (11 + 8 * qt, "turn_ctx", TT * (b - 1) + qt),
                    (16 + 8 * qt, "project", TT * (b - 1) + qt)]
        for g in range(NG):
            u, G = g * GU, NG * b + g
            out += [(u + 49, "turn_max", G + 1)] + [(QK_AT[g] + 3 * i, "qk", 2 * (G + PREP) + i) for i in range(2)]
        out += [(X_AT + 3 * f, "turn_x", 4 * (b + 1) + f) for f in range(4)]
        out += [(at, "v", NG * b + 2 + i) for i, at in enumerate(V_AT)]
        return sorted(out)

    LIMIT = {k: r * B for k, r in RATE.items()}

    def body_jobs(b):
        return [j for j in jobs(b) if 0 <= j[2] < LIMIT[j[1]]]

    bank_of = {(kind, n % RATE[kind]): 6 + i % 2 for i, (_, kind, n) in enumerate(jobs(B0))}
    opening = [(0, "turn_x", f) for f in range(4)] + [(0, "qk", 0), (0, "qk", 1), (0, "v", 0), (1, "v", 1),
               (3, "qk", 2), (6, "qk", 3), (30, "qk", 4), (33, "qk", 5), (66, "turn_max", 0)]
    assert PREP == 3 and AHEAD > 66
    closing = []
    for s in range(TT + 2):
        closing += [(s, kind, TT * (B - 1) + s - lag) for lag, kind in enumerate(("turn_o", "turn_ctx", "project"))
                    if 0 <= s - lag < TT]
    before = {}
    holder = {}
    for _, kind, n in opening + [j for b in range(B) for j in body_jobs(b)] + closing:
        bank = bank_of[kind, n % RATE[kind]]
        before[kind, n] = holder.get(bank)
        holder[bank] = (kind, n)

    with ExitStack() as ctx:
        def sb(name, shape, dt=F32):
            return ctx.enter_context(nc.sbuf_tensor(f"attn_{name}", shape, dt))

        def sem(name):
            sems.append(ctx.enter_context(nc.semaphore(f"attn_{name}")))
            return sems[-1]

        sems = []
        blocks = ExitStack()
        w_qk = sb("w_qk", [P, KT, NG, P])
        b_qk = sb("b_qk", [P, NG])
        w_v = sb("w_v", [P, KT, D])
        b_v = sb("b_v", [P, D])
        w_o = sb("w_o", [P, KT, D])
        b_o = sb("b_o", [P, D])
        x_ln = sb("x_ln", [P, TT, D])
        x_res = sb("x_res", [P, TT, D])
        stats = sb("stats", [P, TT, 6])
        mean_var = sb("mean_var", [P, TT, 2])
        waited = sb("waited", [P, 1])
        var_eps = sb("var_eps", [P, TT])
        rstd = sb("rstd", [P, TT])
        xn_t = sb("xn_t", [P, KT, T])
        qk = sb("qk", [P, T])
        qk_rest = sb("qk_rest", [P, T])
        parts = sb("parts", [P, 3, T], BF16)
        q_rows = sb("q_rows", [SR + 3, NG, GH, T], BF16)
        k_rows = sb("k_rows", [SR + 3, NG, GH, T], BF16)
        v_ones = sb("v_ones", [P, NG, TT, GH, 2 * DH])
        probs = sb("probs", [P, NQ, GH, HALF])
        o_sb = sb("o_sb", [P, NG, T])
        part_max = sb("part_max", [P, 2, GU])
        neg_max = sb("neg_max", [P, 2, GU // 2])
        max_rest = sb("max_rest", [GU // 2, P])
        max_parts = sb("max_parts", [GU // 2, 3, P], BF16)
        sum_inv = sb("sum_inv", [P, 2, H])
        ctx_rows = sb("ctx_rows", [P, 2, D])
        ctx_t = sb("ctx_t", [P, 2, KT, P])
        w_raw = o_sb[:, 0, :].rearrange("p (k n) -> p k n", k=KT)
        ps = ctx.enter_context(nc.psum_tensor("attn_ps", [P, 8, HALF], F32))

        weights_loaded, w_raw_loaded = sem("weights_loaded"), sem("w_raw_loaded")
        w_qk_ready, ones_ready, v_filled = sem("w_qk_ready"), sem("ones_ready"), sem("v_filled")
        x_loaded, res_loaded, res_ready = sem("x_loaded"), sem("res_loaded"), sem("res_ready")
        stat_step, var_ready, rstd_ready, xn_ready = sem("stat_step"), sem("var_ready"), sem("rstd_ready"), sem("xn_ready")
        ready = {k: sem(f"{k}_ready") for k in RATE}
        taken = {k: sem(f"{k}_taken") for k in RATE if k != "qk"}
        qk_whole, part1_ready = sem("qk_whole"), sem("part1_ready")
        taken["qk"] = part1_ready
        rest_ready, part2_ready, part3_ready = sem("rest_ready"), sem("part2_ready"), sem("part3_ready")
        rows_loaded = [sem(f"rows_loaded{g}") for g in range(NG)]
        max_tile_ready, max_tile_taken = sem("max_tile_ready"), sem("max_tile_taken")
        neg_max_ready, max_split, max_parts_ready = sem("neg_max_ready"), sem("max_split"), sem("max_parts_ready")
        max_loaded = [sem(f"max_loaded{g}") for g in range(NG)]
        scores_ready, exp_done, pv_done, o_taken = sem("scores_ready"), sem("exp_done"), sem("pv_done"), sem("o_taken")
        inv_ready = sem("inv_ready")
        stored = sem("stored")

        block = blocks.enter_context(nc.Block())

        def over_batches(eng, body):
            body(0, 0)
            with eng.Fori(1, B - 1, 1) as b:
                body({1: b, "eng": eng}, B0)
            body(B - 1, B - 1)

        def value(b, rate, n):
            if isinstance(b, int):
                return n
            if rate not in b:
                b[rate] = b["eng"].snap(b[1] * rate)
            return b[rate] + (n - B0 * rate)

        def wait(eng, sem_, b, rate, n):
            if n <= 0:
                assert isinstance(b, int)
                return
            assert isinstance(b, int) or n > rate, (rate, n)
            eng.wait_ge(sem_, value(b, rate, n))

        def rows(t, b, b0, ahead=0):
            at = b if isinstance(b, int) else b[1]
            return t[bass.ds(at + ahead, 1)].rearrange("a (p t) d -> (a p) t d", t=TT)

        @block.sync
        def _(sp):
            sp.dma_start(x_ln[:, :, :], rows(x_in, 0, 0)).then_inc(x_loaded, 16)
            sp.dma_start(w_raw, w_qkv[:, 0:2 * D].rearrange("(k p) n -> p k n", p=P)).then_inc(w_raw_loaded, 16)
            sp.dma_start(w_v[:, :, :], w_qkv[:, 2 * D:3 * D].rearrange("(k p) n -> p k n", p=P)).then_inc(weights_loaded, 16)
            sp.dma_start(w_o[:, :, :], w_out.rearrange("(k p) n -> p k n", p=P)).then_inc(weights_loaded, 16)
            sp.dma_start(b_v[:, :], b_qkv[2 * D:3 * D].partition_broadcast(P)).then_inc(weights_loaded, 16)
            sp.dma_start(b_o[:, :], b_out.partition_broadcast(P)).then_inc(weights_loaded, 16)
            for i in range(2):
                for g in range(NG):
                    src = b_qkv[i * D + g * GH * DH:i * D + (g + 1) * GH * DH].rearrange("(h d o) -> d h o", h=GH, o=1)
                    sp.dma_start(b_qk[i * 64:i * 64 + 64, g:g + 1], src).then_inc(weights_loaded, 16)

            def lay_out(b, b0, G):
                g = G % NG
                wait(sp, part3_ready, b, NG, G + 1)
                wait(sp, part1_ready, b, 2 * NG, 2 * G + 2)
                for dst, order, half in ((q_rows, Q_PARTS, 0), (k_rows, K_PARTS, 1)):
                    for i, part in enumerate(order):
                        sp.dma_start(dst[i * DH:(i + 1) * DH, g, :, :],
                                     parts[half * 64:half * 64 + 64, part, :]).then_inc(rows_loaded[g], 16)

            def max_rows(b, b0, G):
                wait(sp, max_parts_ready, b, NG, G + 1)
                for i in range(3):
                    sp.dma_start(q_rows[SR + i:SR + i + 1, G % NG, :, :],
                                 max_parts[:, i, :]).then_inc(max_loaded[G % NG], 16)

            for G in range(PREP):
                lay_out(0, 0, G)
            max_rows(0, 0, 0)

            def body(b, b0):
                if b0 < B - 1:
                    wait(sp, ready["turn_x"], b, 4, 4 * (b0 + 1))
                    sp.dma_start(x_ln[:, :, :], rows(x_in, b, b0, 1)).then_inc(x_loaded, 16)
                for g in range(NG):
                    G = NG * b0 + g
                    if G + 1 < NG * B:
                        max_rows(b, b0, G + 1)
                    if g == 0:
                        if b0 > 0:
                            wait(sp, taken["project"], b, TT, TT * b0)
                            sp.dma_start(rows(x_out, b, b0, -1), x_res[:, :, :]).then_inc(stored, 16)
                            wait(sp, stored, b, 16, 16 * b0)
                        sp.dma_start(x_res[:, :, :], rows(x_in, b, b0)).then_inc(res_loaded, 16)
                    if G + PREP < NG * B:
                        lay_out(b, b0, G + PREP)
            over_batches(sp, body)
            sp.wait_ge(taken["project"], TT * B)
            sp.dma_start(rows(x_out, B - 1, B - 1), x_res[:, :, :]).then_inc(stored, 16)
            sp.wait_ge(stored, 16 * B)

        @block.gpsimd
        def _(pool):
            pool.memset(v_ones[:, :, :, :, :], 1.0).then_inc(v_filled, 1)

            def split(b, b0, G):
                wait(pool, qk_whole, b, 2 * NG, 2 * G + 2)
                wait(pool, part1_ready, b, 2 * NG, 2 * G + 2)
                pool.tensor_tensor(qk_rest[:, :], qk[:, :], parts[:, 0, :], ALU.subtract).then_inc(rest_ready, 1)
                wait(pool, part2_ready, b, NG, G + 1)
                pool.tensor_tensor(parts[:, 2, :], qk_rest[:, :], parts[:, 1, :], ALU.subtract).then_inc(part3_ready, 1)

            def rsqrt(b, b0, n):
                wait(pool, var_ready, b, 1, n + 1)
                pool.tensor_tensor(rstd[:, :], var_eps[:, :], c.neg_half[:, 0:TT], ALU.pow).then_inc(rstd_ready, 1)
            rsqrt(0, 0, 0)
            for G in range(PREP):
                split(0, 0, G)
            pool.wait_ge(weights_loaded, 16 * (4 + 2 * NG))

            def body(b, b0):
                if b0 < B - 1:
                    rsqrt(b, b0, b0 + 1)
                for g in range(NG):
                    if NG * b0 + g + PREP < NG * B:
                        split(b, b0, NG * b0 + g + PREP)
                    if g == 1:
                        wait(pool, res_loaded, b, 16, 16 * (b0 + 1))
                        pool.tensor_tensor(x_res[:, :, :], x_res[:, :, :],
                                           b_o[:, :].unsqueeze(1).to_broadcast([P, TT, D]), ALU.add).then_inc(res_ready, 1)
            over_batches(pool, body)

        @block.vector
        def _(dve):
            def stat(b, b0, n, t):
                if t == 0:
                    wait(dve, x_loaded, b, 16, 16 * (n + 1))
                dve.bn_stats(stats[:, t, :], x_ln[:, t, :]).then_inc(stat_step, 1)

            def moments(b, b0, n):
                wait(dve, stat_step, b, 2 * TT, 2 * TT * n + TT)
                dve.memset(waited[:, :], 0.0)
                for t in range(TT):
                    dve.bn_aggr(mean_var[:, t, :], stats[:, t, :]).then_inc(stat_step, 1)
                wait(dve, stat_step, b, 2 * TT, 2 * TT * (n + 1))
                dve.tensor_scalar(var_eps[:, :], mean_var[:, :, 1], EPS, None, ALU.add).then_inc(var_ready, 1)

            def normalise(b, b0, n, t):
                if t == 0:
                    wait(dve, rstd_ready, b, 1, n + 1)
                ins = dve.tensor_scalar(x_ln[:, t, :], x_ln[:, t, :], mean_var[:, t, 0:1], rstd[:, t:t + 1],
                                        ALU.subtract, ALU.mult)
                if t == TT - 1:
                    ins.then_inc(xn_ready, 1)

            def values(b, b0, n):
                pair, half = n % NG // 2, n % 2
                bank = ps[:, bank_of["v", n % NG], :].rearrange("p (t g h d) -> p t g h d", t=TT // 2, g=2, h=GH)
                wait(dve, ready["v"], b, NG, n + 1)
                for i in range(2):
                    g = 2 * pair + i
                    bias = b_v[:, g * 64:(g + 1) * 64].rearrange("p (h d) -> p h d", h=GH)
                    last = dve.tensor_tensor(v_ones[:, g, half * (TT // 2):(half + 1) * (TT // 2), :, 0:DH], bank[:, :, i],
                                             bias.unsqueeze(1).to_broadcast([P, TT // 2, GH, DH]), ALU.add)
                last.then_inc(taken["v"], 1)

            def reduce_tile(b, b0, v):
                G, w = divmod(v, GU)
                wait(dve, max_tile_ready, b, BU, v + 1)
                dve.tensor_reduce(part_max[:, G % 2, w:w + 1], ps[:, v % 2, :], AX.X, ALU.max).then_inc(max_tile_taken, 1)
                if w == GU - 1:
                    wait(dve, max_tile_taken, b, BU, v + 1)
                    dve.tensor_reduce(neg_max[:, G % 2, :], part_max[:, G % 2, :].rearrange("p (n h) -> p n h", h=CHUNKS),
                                      AX.X, ALU.max, negate=True).then_inc(neg_max_ready, 1)

            def split_max(b, b0, G):
                bank = ps[0:GU // 2, bank_of["turn_max", G % NG], 0:P]
                wait(dve, ready["turn_max"], b, NG, G + 1)
                if G > 0:
                    wait(dve, max_loaded[(G - 1) % NG], b, 48, 48 * ((G - 1) // NG + 1))
                dve.tensor_copy(max_parts[:, 0, :], bank).then_inc(max_split, 1)
                wait(dve, max_split, b, 2 * NG, 2 * G + 1)
                dve.tensor_tensor(max_rest[:, :], bank, max_parts[:, 0, :], ALU.subtract).then_inc(taken["turn_max"], 1)
                wait(dve, taken["turn_max"], b, NG, G + 1)
                dve.tensor_copy(max_parts[:, 1, :], max_rest[:, :]).then_inc(max_split, 1)
                wait(dve, max_split, b, 2 * NG, 2 * G + 2)
                dve.tensor_tensor(max_parts[:, 2, :], max_rest[:, :], max_parts[:, 1, :], ALU.subtract).then_inc(max_parts_ready, 1)

            def normalise_out(b, b0, n):
                qt = n % TT
                bank = ps[:, bank_of["turn_o", qt], :].rearrange("p (h d) -> p h d", h=H)
                wait(dve, ready["turn_o"], b, TT, n + 1)
                dve.reciprocal(sum_inv[:, qt % 2, :], bank[:, :, DH]).then_inc(inv_ready, 1)
                wait(dve, inv_ready, b, TT, n + 1)
                dve.tensor_tensor(ctx_rows[:, qt % 2, :].rearrange("p (h d) -> p h d", h=H), bank[:, :, 0:DH],
                                  sum_inv[:, qt % 2, :].unsqueeze(2).to_broadcast([P, H, DH]), ALU.mult).then_inc(taken["turn_o"], 1)

            def add_out(b, b0, n):
                qt = n % TT
                wait(dve, ready["project"], b, TT, n + 1)
                if qt == 0:
                    wait(dve, res_ready, b, 1, n // TT + 1)
                dve.tensor_tensor(x_res[:, qt, :], ps[:, bank_of["project", qt], 0:D], x_res[:, qt, :],
                                  ALU.add).then_inc(taken["project"], 1)

            uses = {"v": values, "turn_max": split_max, "turn_o": normalise_out, "project": add_out}
            for t in range(TT):
                stat(0, 0, 0, t)
            moments(0, 0, 0)
            dve.wait_ge(w_raw_loaded, 16)
            for k in range(KT):
                for i in range(2):
                    for g in range(NG):
                        src = w_raw[:, k, i * D + g * 64:i * D + (g + 1) * 64].rearrange("p (h d) -> p d h", h=GH)
                        dst = w_qk[:, k, g, i * 64:(i + 1) * 64].rearrange("p (d h) -> p d h", h=GH)
                        dve.tensor_copy(dst, src).then_inc(w_qk_ready, 1)
            for t in range(TT):
                normalise(0, 0, 0, t)
            dve.memset(k_rows[SR:SR + 3, 0:2, :, :], 1.0).then_inc(ones_ready, 1)
            dve.wait_ge(weights_loaded, 16 * (4 + 2 * NG))
            dve.wait_ge(v_filled, 1)
            values(0, 0, 0)
            dve.memset(k_rows[SR:SR + 3, 2:NG, :, :], 1.0).then_inc(ones_ready, 1)
            for v in range(AHEAD):
                reduce_tile(0, 0, v)
                if v == 2:
                    values(0, 0, 1)
                if v == 67:
                    split_max(0, 0, 0)

            def body(b, b0):
                todo = body_jobs(b0)
                for u in range(BU):
                    v = BU * b0 + u + AHEAD
                    if v < BU * B:
                        reduce_tile(b, b0, v)
                    for at, kind, n in todo:
                        if at == u - 1 and kind in uses:
                            uses[kind](b, b0, n)
                    if b0 < B - 1:
                        for t in range(TT):
                            if u == 30 + 3 * t:
                                stat(b, b0, b0 + 1, t)
                            if u == 69 + 2 * t:
                                normalise(b, b0, b0 + 1, t)
                        if u == 60:
                            moments(b, b0, b0 + 1)
            over_batches(dve, body)
            for _, kind, n in closing:
                if kind in uses:
                    uses[kind](B - 1, B - 1, n)

        @block.tensor
        def _(pe):
            def small(b, b0, kind, n):
                key = n % RATE[kind]
                bank = bank_of[kind, key]
                if before[kind, n]:
                    prev, m = before[kind, n]
                    wait(pe, taken[prev], b, RATE[prev], m + 1)
                if kind == "turn_x":
                    if key == 0:
                        wait(pe, xn_ready, b, 1, n // 4 + 1)
                    for j in range(4):
                        k, t = divmod(4 * key + j, TT)
                        last = pe.transpose(ps[:, bank, j * P:(j + 1) * P], x_ln[:, t, k * P:(k + 1) * P], c.ident[:, :])
                elif kind == "qk":
                    G, half = divmod(n, 2)
                    wait(pe, taken["turn_x"], b, 4, 4 * (G // NG + 1))
                    for k in range(KT):
                        last = pe.matmul(ps[:, bank, :], w_qk[:, k, G % NG, :], xn_t[:, k, half * HALF:(half + 1) * HALF],
                                         start=(k == 0), stop=(k == KT - 1))
                elif kind == "v":
                    pair, half = n % NG // 2, n % 2
                    wait(pe, taken["turn_x"], b, 4, 4 * (n // NG + 1))
                    for t in range(TT // 2):
                        for k in range(KT):
                            last = pe.matmul(ps[:, bank, t * P:(t + 1) * P],
                                             xn_t[:, k, (half * (TT // 2) + t) * P:(half * (TT // 2) + t + 1) * P],
                                             w_v[:, k, pair * P:(pair + 1) * P], start=(k == 0), stop=(k == KT - 1))
                elif kind == "turn_max":
                    wait(pe, neg_max_ready, b, NG, n + 1)
                    last = pe.transpose(ps[0:GU // 2, bank, 0:P], neg_max[:, n % 2, :], c.ident[:, :])
                elif kind == "turn_o":
                    if key == 0:
                        wait(pe, o_taken, b, 2 * NG, 2 * NG * (n // TT + 1))
                    for g in range(NG):
                        last = pe.transpose(ps[:, bank, g * P:(g + 1) * P], o_sb[:, g, key * P:(key + 1) * P], c.ident[:, :])
                elif kind == "turn_ctx":
                    wait(pe, taken["turn_o"], b, TT, n + 1)
                    for k in range(KT):
                        last = pe.transpose(ps[:, bank, k * P:(k + 1) * P], ctx_rows[:, key % 2, k * P:(k + 1) * P], c.ident[:, :])
                else:
                    wait(pe, taken["turn_ctx"], b, TT, n + 1)
                    for k in range(KT):
                        last = pe.matmul(ps[:, bank, 0:D], ctx_t[:, key % 2, k, :], w_o[:, k, :],
                                         start=(k == 0), stop=(k == KT - 1))
                last.then_inc(ready[kind], 1)

            def max_tile(b, b0, v):
                G, w = divmod(v, GU)
                h, t, half = w // (TT * CHUNKS), w // CHUNKS % TT, w % CHUNKS
                g = G % NG
                if w == 0:
                    wait(pe, rows_loaded[g], b, 192, 192 * (G // NG + 1))
                wait(pe, max_tile_taken, b, BU, v - 1)
                pe.matmul(ps[:, v % 2, :], q_rows[0:SR, g, h, t * P:(t + 1) * P],
                          k_rows[0:SR, g, h, half * HALF:(half + 1) * HALF], start=True, stop=True).then_inc(max_tile_ready, 1)

            def score_tile(b, b0, u):
                G, w = divmod(u, GU)
                half, kt, h = w // (TT * GH), w // GH % TT, w % GH
                g = G % NG
                if w == 0:
                    wait(pe, max_loaded[g], b, 48, 48 * (G // NG + 1))
                wait(pe, exp_done, b, BU, u - 1)
                pe.matmul(ps[:, 2 + u % 2, :], k_rows[:, g, h, kt * P:(kt + 1) * P],
                          q_rows[:, g, h, half * HALF:(half + 1) * HALF], start=True, stop=True).then_inc(scores_ready, 1)

            def pv(b, b0, quad, piece):
                window, kt = divmod(quad, TT)
                G = window // CHUNKS
                if piece == 0:
                    wait(pe, exp_done, b, BU, 4 * (quad + 1))
                    if kt == 0:
                        wait(pe, o_taken, b, 2 * NG, window - 1)
                        if window % (2 * CHUNKS) == 0:
                            wait(pe, taken["v"], b, NG, G + 2)
                cols = slice(piece * HALF // 2, (piece + 1) * HALF // 2)
                for h in range(GH):
                    last = pe.matmul(ps[32 * h:32 * h + 32, 4 + window % 2, cols], v_ones[:, G % NG, kt, h, :],
                                     probs[:, quad % NQ, h, cols], start=(kt == 0 and piece == 0), stop=(kt == TT - 1),
                                     skip_group_check=True)
                if piece == 1:
                    last.then_inc(pv_done, 1)

            pe.wait_ge(w_qk_ready, 2 * KT * NG)
            pe.wait_ge(weights_loaded, 16 * (4 + 2 * NG))
            for v in range(AHEAD):
                for at, kind, n in opening:
                    if at == v:
                        small(0, 0, kind, n)
                max_tile(0, 0, v)
            pe.wait_ge(ones_ready, 2)
            pe.wait_ge(v_filled, 1)

            def body(b, b0):
                todo = body_jobs(b0)
                for u in range(BU):
                    for at, kind, n in todo:
                        if at == u:
                            small(b, b0, kind, n)
                    if BU * b0 + u + AHEAD < BU * B:
                        max_tile(b, b0, BU * b0 + u + AHEAD)
                    score_tile(b, b0, BU * b0 + u)
                    quad = (BU * b0 + u) // 4 - 1
                    if u % 2 == 1 and quad >= 0:
                        pv(b, b0, quad, u % 4 // 2)
            over_batches(pe, body)
            for piece in range(2):
                pv(B - 1, B - 1, BU * B // 4 - 1, piece)
            for _, kind, n in closing:
                small(B - 1, B - 1, kind, n)

        @block.scalar
        def _(act):
            def turned_x(b, b0, n):
                f = n % 4
                wait(act, ready["turn_x"], b, 4, n + 1)
                act.activation(xn_t[:, :, :].rearrange("p k t -> p (k t)")[:, f * HALF:(f + 1) * HALF],
                               ps[:, bank_of["turn_x", f], :], ACT.Identity).then_inc(taken["turn_x"], 1)

            def take_qk(b, b0, n):
                G, half = divmod(n, 2)
                g = G % NG
                cols = slice(half * HALF, (half + 1) * HALF)
                bank = ps[:, bank_of["qk", n % RATE["qk"]], :]
                wait(act, ready["qk"], b, 2 * NG, n + 1)
                wait(act, rest_ready, b, NG, G)
                act.activation(qk[:, cols], bank, ACT.Identity, bias=b_qk[:, g:g + 1]).then_inc(qk_whole, 1)
                if G > 0:
                    wait(act, rows_loaded[(G - 1) % NG], b, 192, 192 * ((G - 1) // NG + 1))
                act.activation(parts[:, 0, cols], bank, ACT.Identity, bias=b_qk[:, g:g + 1]).then_inc(part1_ready, 1)

            def second_part(b, b0, G):
                wait(act, rest_ready, b, NG, G + 1)
                act.activation(parts[:, 1, :], qk_rest[:, :], ACT.Identity).then_inc(part2_ready, 1)

            def take_ctx(b, b0, n):
                qt = n % TT
                wait(act, ready["turn_ctx"], b, TT, n + 1)
                act.activation(ctx_t[:, qt % 2, :, :], ps[:, bank_of["turn_ctx", qt], 0:D].rearrange("p (k q) -> p k q", k=KT),
                               ACT.Identity, scale=float(D) ** -0.5).then_inc(taken["turn_ctx"], 1)

            def take_o(b, b0, window):
                wait(act, pv_done, b, BU // 4, TT * (window + 1))
                g, half = window // CHUNKS % NG, window % CHUNKS
                if g == 0 and window >= 2 * NG:
                    wait(act, ready["turn_o"], b, TT, window // (2 * NG) * TT - TT // 2 * (1 - half))
                act.activation(o_sb[:, g, half * HALF:(half + 1) * HALF], ps[:, 4 + window % 2, :],
                               ACT.Identity).then_inc(o_taken, 1)

            uses = {"turn_x": turned_x, "qk": take_qk, "turn_ctx": take_ctx}
            act.wait_ge(weights_loaded, 16 * (4 + 2 * NG))
            for _, kind, n in opening:
                if kind in uses:
                    uses[kind](0, 0, n)
                if kind == "qk" and n % 2:
                    second_part(0, 0, n // 2)

            def body(b, b0):
                todo = body_jobs(b0)
                for u in range(BU):
                    U = BU * b0 + u
                    if u % GH == 0:
                        wait(act, pv_done, b, BU // 4, U // GH - NQ + 1)
                    wait(act, scores_ready, b, BU, U + 1)
                    act.activation(probs[:, U // GH % NQ, u % GH, :], ps[:, 2 + u % 2, :], ACT.Exp).then_inc(exp_done, 1)
                    if u % (TT * GH) == 5 and U >= TT * GH:
                        take_o(b, b0, U // (TT * GH) - 1)
                    for at, kind, n in todo:
                        if at == u - 1 and kind in uses:
                            uses[kind](b, b0, n)
                    for g in range(NG):
                        if u == QK_AT[g] + 9 and NG * b0 + g + PREP < NG * B:
                            second_part(b, b0, NG * b0 + g + PREP)
            over_batches(act, body)
            take_o(B - 1, B - 1, 2 * NG * B - 1)
            for _, kind, n in closing:
                if kind in uses:
                    uses[kind](B - 1, B - 1, n)

        blocks.close()
        clear(nc, sems)


def build_program(nc, d, out):
    x = d["L0_attn_x"]
    x1 = nc.dram_tensor("after_first_ffn", x.shape, F32, kind="Internal").ap()
    x2 = nc.dram_tensor("after_attention", x.shape, F32, kind="Internal").ap()
    with ExitStack() as ctx:
        ctx.enter_context(nc.allow_non_contiguous_dma(reason="bias vectors, a few hundred elements each, loaded once"))
        c = build_setup(nc, ctx, d)
        build_ffn(nc, c, "ffn1", x, x1, d["L0_ffn_bo"])
        nc.disable_value_cache = True
        build_attention(nc, c, x1, x2, d["L0_attn_W_qkv"], d["L0_attn_b_qkv"], d["L0_attn_W_out"], d["L0_attn_b_out"])
        build_ffn(nc, c, "ffn2", x2, out, d["L0_ffn_bo"])


_INS = ["L0_attn_x", "L0_attn_W_qkv", "L0_attn_b_qkv", "L0_attn_W_out", "L0_attn_b_out", "L0_ffn_slot_init", "L0_ffn_w1",
        "L0_ffn_b1", "L0_ffn_w2", "L0_ffn_b2", "L0_ffn_tau", "L0_ffn_Wih", "L0_ffn_Whh", "L0_ffn_bih", "L0_ffn_bhh",
        "L0_ffn_wq", "L0_ffn_bq", "L0_ffn_wk", "L0_ffn_bk", "L0_ffn_wv", "L0_ffn_bv", "L0_ffn_ln_g", "L0_ffn_ln_b",
        "L0_ffn_wvp", "L0_ffn_bvp", "L0_ffn_wo", "L0_ffn_bo"]


def kernel(**inputs):
    import numpy as np
    import concourse.bacc as bacc
    from concourse.bass_utils import run_bass_kernel_spmd

    nc = bacc.Bacc("TRN2", target_bir_lowering=False, num_devices=1)
    arrays, d = {}, {}
    for name in _INS:
        a = np.ascontiguousarray(inputs[name])
        arrays[f"in_{name}"] = a
        d[name] = nc.dram_tensor(f"in_{name}", a.shape, mybir.dt.from_np(a.dtype), kind="ExternalInput").ap()
    out = nc.dram_tensor("out", inputs["L0_attn_x"].shape, F32, kind="ExternalOutput").ap()
    build_program(nc, d, out)
    r = run_bass_kernel_spmd(nc, [arrays], core_ids=[0])
    return r.results[0]["out"]
```

```python
from contextlib import ExitStack

import concourse.bass as bass
from concourse import mybir

F32 = mybir.dt.float32
BF16 = mybir.dt.bfloat16
ALU = mybir.AluOpType
ACT = mybir.ActivationFunctionType
AX = mybir.AxisListType

P = 128
HALF = 512
EPS = 1e-5
NEG = -3.0e38


class Consts:
    pass


def clear(nc, sems):
    nums = sorted(s.num for s in sems)
    starts = [n for n in nums if n - 1 not in nums]
    with nc.Block() as block:
        @block.sync
        def _(sp):
            for n in starts:
                end = n
                while end in nums:
                    end += 1
                sp.sem_clear(range(n, end))


def build_setup(nc, ctx, d):
    D, F = d["L0_ffn_w1"].shape[0] // 2, d["L0_ffn_w1"].shape[1]
    S = d["L0_ffn_slot_init"].shape[0]
    G3 = d["L0_ffn_Wih"].shape[0]
    KT, MT = D // P, G3 // P
    c = Consts()
    c.D, c.F, c.S, c.G3, c.KT, c.MT = D, F, S, G3, KT, MT

    def sb(name, shape, dt=F32):
        return ctx.enter_context(nc.sbuf_tensor(name, shape, dt))

    c.ident = sb("ident", [P, P])
    c.ones = sb("ones", [P, P])
    c.neg_half = sb("neg_half", [P, 8])
    c.w1 = sb("w1", [P, KT, F])
    c.hid_bias = sb("hid_bias", [P, 1])
    c.w2 = sb("w2", [P, S])
    c.b2 = sb("b2", [P, S])
    c.wih_t = sb("wih_t", [P, KT, G3])
    c.gate_bias = sb("gate_bias", [P, MT])
    c.gh_t = sb("gh_t", [P, MT, S])
    c.slots_t = sb("slots_t", [P, KT, S])
    c.wq = sb("wq", [P, KT, S])
    c.wk = sb("wk", [P, KT, S])
    c.bq = sb("bq", [S, 1])
    c.bk = sb("bk", [S, 1])
    c.wv = sb("wv", [P, KT, D])
    c.bv = sb("bv", [P, D])
    c.ln_g = sb("ln_g", [P, KT])
    c.ln_b = sb("ln_b", [P, KT])
    c.wvp = sb("wvp", [P, KT, D])
    c.bvp = sb("bvp", [P, KT])
    c.wo = sb("wo", [P, KT, D])

    with ExitStack() as own:
        def tmp(name, shape, dt=F32):
            return own.enter_context(nc.sbuf_tensor(name, shape, dt))

        def sem(name):
            return ctx.enter_context(nc.semaphore(name))

        w1_mean = tmp("w1_mean", [P, KT, F])
        wih = tmp("wih", [P, MT, D])
        whh = tmp("whh", [P, MT, D])
        whh_t = tmp("whh_t", [P, KT, G3])
        hh_bias = tmp("hh_bias", [P, MT])
        both_bias = tmp("both_bias", [P, MT])
        slots = tmp("slots", [S, D])
        slot_sum = tmp("slot_sum", [P, KT])
        slot_mean = tmp("slot_mean", [P, KT])
        b1 = tmp("b1", [P, 1])
        tau = tmp("tau", [P, 1])
        tau_neg = tmp("tau_neg", [P, 1])
        tau_abs = tmp("tau_abs", [P, 1])
        tau_den = tmp("tau_den", [P, 1])
        tau_inv = tmp("tau_inv", [P, 1])
        w2_raw = tmp("w2_raw", [P, S])
        b2_raw = tmp("b2_raw", [P, S])
        ps = own.enter_context(nc.psum_tensor("ps_setup", [P, 8, HALF], F32))

        gates_loaded = [sem("wih_loaded"), sem("whh_loaded")]
        slots_loaded = sem("slots_loaded")
        loaded = sem("setup_loaded")
        loaded_act = sem("setup_loaded_act")
        filled = sem("setup_filled")
        ident_ready = sem("ident_ready")
        turned = sem("setup_turned")
        copied = sem("setup_copied")
        slots_taken = sem("setup_slots_taken")
        mean_ready = sem("slot_mean_ready")
        product_ready = sem("setup_product_ready")
        tau_step = sem("tau_step")
        bias_step = sem("bias_step")

        block = own.enter_context(nc.Block())
        n_sync, n_act = [], []

        @block.sync
        def _(sp):
            def load(dst, src):
                sp.dma_start(dst, src).then_inc(loaded, 16)
                n_sync.append(1)
            sp.dma_start(wih[:, :, :], d["L0_ffn_Wih"].rearrange("(m p) d -> p m d", p=P)).then_inc(gates_loaded[0], 16)
            sp.dma_start(whh[:, :, :], d["L0_ffn_Whh"].rearrange("(m p) d -> p m d", p=P)).then_inc(gates_loaded[1], 16)
            sp.dma_start(slots[:, :], d["L0_ffn_slot_init"]).then_inc(slots_loaded, 16)
            load(c.w1[:, :, :], d["L0_ffn_w1"][0:D, :].rearrange("(k p) f -> p k f", p=P))
            load(w1_mean[:, :, :], d["L0_ffn_w1"][D:2 * D, :].rearrange("(k p) f -> p k f", p=P))
            load(w2_raw[:, :], d["L0_ffn_w2"])
            load(b2_raw[:, :], d["L0_ffn_b2"].partition_broadcast(P))
            load(tau[:, :], d["L0_ffn_tau"].partition_broadcast(P))
            load(b1[:, :], d["L0_ffn_b1"].rearrange("(p o) -> p o", o=1))
            load(c.gate_bias[:, :], d["L0_ffn_bih"].rearrange("(m p o) -> p m o", p=P, o=1))
            load(hh_bias[:, :], d["L0_ffn_bhh"].rearrange("(m p o) -> p m o", p=P, o=1))

        @block.scalar
        def _(act):
            def load(dst, src):
                act.dma_start(dst, src).then_inc(loaded_act, 16)
                n_act.append(1)
            load(c.wq[:, :, :], d["L0_ffn_wq"].rearrange("(k p) f -> p k f", p=P))
            load(c.wk[:, :, :], d["L0_ffn_wk"].rearrange("(k p) f -> p k f", p=P))
            load(c.wv[:, :, :], d["L0_ffn_wv"].rearrange("(k p) f -> p k f", p=P))
            load(c.wvp[:, :, :], d["L0_ffn_wvp"].rearrange("(k p) f -> p k f", p=P))
            load(c.wo[:, :, :], d["L0_ffn_wo"].rearrange("(k p) f -> p k f", p=P))
            load(c.bv[:, :], d["L0_ffn_bv"].partition_broadcast(P))
            load(c.bq[:, :], d["L0_ffn_bq"].rearrange("(p o) -> p o", o=1))
            load(c.bk[:, :], d["L0_ffn_bk"].rearrange("(p o) -> p o", o=1))
            load(c.ln_g[:, :], d["L0_ffn_ln_g"].rearrange("(m p o) -> p m o", p=P, o=1))
            load(c.ln_b[:, :], d["L0_ffn_ln_b"].rearrange("(m p o) -> p m o", p=P, o=1))
            load(c.bvp[:, :], d["L0_ffn_bvp"].rearrange("(m p o) -> p m o", p=P, o=1))
            act.wait_ge(loaded_act, 16 * len(n_act))

        @block.gpsimd
        def _(pool):
            nc.gpsimd.memset(c.ident[:, :], 0.0).then_inc(filled, 1)
            pool.wait_ge(filled, 1)
            nc.gpsimd.affine_select(out=c.ident[:, :], in_=c.ident[:, :], compare_op=ALU.not_equal, fill=1.0,
                                    base=0, pattern=[[-1, P]], channel_multiplier=1).then_inc(ident_ready, 1)
            nc.gpsimd.memset(c.ones[:, :], 1.0).then_inc(filled, 1)
            nc.gpsimd.memset(c.neg_half[:, :], -0.5).then_inc(filled, 1)
            pool.wait_ge(filled, 3)

        groups = KT * MT * P // HALF

        @block.tensor
        def _(pe):
            pe.wait_ge(ident_ready, 1)
            for n, w in enumerate((wih, whh)):
                pe.wait_ge(gates_loaded[n], 16)
                for g in range(groups):
                    for j in range(4):
                        k, m = divmod(4 * g + j, MT)
                        last = pe.transpose(ps[:, 3 * n + g, j * P:(j + 1) * P], w[:, m, k * P:(k + 1) * P],
                                            c.ident[:, :])
                    last.then_inc(turned, 1)
            pe.wait_ge(slots_loaded, 16)
            for k in range(KT):
                last = pe.transpose(ps[:, 6, k * S:(k + 1) * S], slots[:, k * P:(k + 1) * P], c.ident[0:S, 0:S])
            last.then_inc(turned, 1)
            pe.wait_ge(copied, 2 * groups)
            pe.wait_ge(slots_taken, 1)
            for m in range(MT):
                for k in range(KT):
                    last = pe.matmul(ps[:, 0, m * S:(m + 1) * S], whh_t[:, k, m * P:(m + 1) * P],
                                     c.slots_t[:, k, :], start=(k == 0), stop=(k == KT - 1))
            last.then_inc(product_ready, 1)
            pe.wait_ge(mean_ready, 1)
            pe.wait_ge(loaded, 16 * len(n_sync))
            for k in range(KT):
                last = pe.matmul(ps[:, 7, 0:1], w1_mean[:, k, :], slot_mean[:, k:k + 1],
                                 start=(k == 0), stop=(k == KT - 1))
            last.then_inc(product_ready, 1)

        @block.vector
        def _(dve):
            for n, w_t in enumerate((c.wih_t, whh_t)):
                flat = w_t[:, :, :].rearrange("p k g -> p (k g)")
                for g in range(groups):
                    dve.wait_ge(turned, 3 * n + g + 1)
                    dve.tensor_copy(flat[:, g * HALF:(g + 1) * HALF], ps[:, 3 * n + g, :]).then_inc(copied, 1)
            dve.wait_ge(turned, 2 * groups + 1)
            src = ps[:, 6, 0:KT * S].rearrange("p (k s) -> p k s", k=KT)
            dve.tensor_copy(c.slots_t[:, :, :], src).then_inc(slots_taken, 1)
            dve.wait_ge(slots_taken, 1)
            dve.tensor_reduce(slot_sum[:, :], c.slots_t[:, :, :], AX.X, ALU.add).then_inc(slots_taken, 1)
            dve.wait_ge(slots_taken, 2)
            dve.tensor_scalar(slot_mean[:, :], slot_sum[:, :], 1.0 / S, None, ALU.mult).then_inc(mean_ready, 1)
            dve.wait_ge(loaded, 16 * len(n_sync))
            dve.tensor_scalar(tau_neg[:, :], tau[:, :], -1.0, None, ALU.mult).then_inc(tau_step, 1)
            dve.wait_ge(tau_step, 1)
            dve.tensor_tensor(tau_abs[:, :], tau[:, :], tau_neg[:, :], ALU.max).then_inc(tau_step, 1)
            dve.wait_ge(tau_step, 2)
            dve.tensor_scalar(tau_den[:, :], tau_abs[:, :], 0.1, None, ALU.add).then_inc(tau_step, 1)
            dve.wait_ge(tau_step, 3)
            dve.reciprocal(tau_inv[:, :], tau_den[:, :]).then_inc(tau_step, 1)
            dve.wait_ge(tau_step, 4)
            dve.tensor_scalar(c.w2[:, :], w2_raw[:, :], tau_inv[:, 0:1], None, ALU.mult).then_inc(tau_step, 1)
            dve.tensor_scalar(c.b2[:, :], b2_raw[:, :], tau_inv[:, 0:1], None, ALU.mult).then_inc(tau_step, 1)
            dve.tensor_tensor(both_bias[:, :], c.gate_bias[:, :], hh_bias[:, :], ALU.add).then_inc(bias_step, 1)
            dve.wait_ge(product_ready, 1)
            dve.wait_ge(bias_step, 1)
            for m in range(MT):
                bias = both_bias if m < 2 * KT else hh_bias
                dve.tensor_scalar(c.gh_t[:, m, :], ps[:, 0, m * S:(m + 1) * S], bias[:, m:m + 1], None,
                                  ALU.add).then_inc(bias_step, 1)
            dve.wait_ge(product_ready, 2)
            dve.tensor_tensor(c.hid_bias[:, :], ps[:, 7, 0:1], b1[:, :], ALU.add).then_inc(bias_step, 1)
            dve.wait_ge(bias_step, 2 + MT)
            dve.wait_ge(tau_step, 6)
    return c


def build_ffn(nc, c, tag, x_in, x_out, bo):
    B, T, D = x_in.shape
    S, KT, MT, F = c.S, c.KT, c.MT, c.F
    TT = T // P
    NS = B * S
    PAIRS = B // 2
    R = 4

    def rows(t, b):
        return t[bass.ds(b, 1)].rearrange("a (p t) d -> (a p) t d", t=TT)

    with ExitStack() as ctx:
        def sb(name, shape, dt=F32, on=ctx):
            return on.enter_context(nc.sbuf_tensor(f"{tag}_{name}", shape, dt))

        def sem(name):
            sems.append(ctx.enter_context(nc.semaphore(f"{tag}_{name}")))
            return sems[-1]

        sems = []
        alpha_t = sb("alpha_t", [P, PAIRS, T])
        si_t = sb("si_t", [P, KT, NS])
        slot_out = sb("slot_out", [P, PAIRS, 2, D])

        with ExitStack() as own:
            x_ring = sb("x_ring", [P, R, TT, D + 1], F32, own)
            stats = sb("stats", [P, TT, 6], F32, own)
            mean_var = sb("mean_var", [P, TT, 2], F32, own)
            waited = sb("waited", [P, 1], F32, own)
            var_eps = sb("var_eps", [P, TT], F32, own)
            rstd = sb("rstd", [P, TT], F32, own)
            shift = sb("shift", [P, TT], F32, own)
            xn_t = sb("xn_t", [P, KT, T], F32, own)
            hid = sb("hid", [P, T], F32, own)
            logit = sb("logit", [P, TT, S], F32, own)
            top8 = sb("top8", [P, TT, 8], F32, own)
            rest = sb("rest", [P, TT, S], F32, own)
            shifted = sb("shifted", [P, TT, S], F32, own)
            expd = sb("expd", [P, TT, S], F32, own)
            picked = sb("picked", [P, TT, S], F32, own)
            total = sb("total", [P, TT], F32, own)
            inv_total = sb("inv_total", [P, TT], F32, own)
            alpha = sb("alpha", [P, 2, TT, 2, S], F32, own)
            den_eps = sb("den_eps", [P, 1], F32, own)
            den_inv = sb("den_inv", [P, 1], F32, own)
            si_rows = sb("si_rows", [P, D], F32, own)
            ps_turn = own.enter_context(nc.psum_tensor(f"{tag}_ps_turn", [P, 2, HALF], F32))
            ps_hid = own.enter_context(nc.psum_tensor(f"{tag}_ps_hid", [P, 2, HALF], F32))
            ps_logit = own.enter_context(nc.psum_tensor(f"{tag}_ps_logit", [P, TT, S], F32))
            ps_si = own.enter_context(nc.psum_tensor(f"{tag}_ps_si", [P, HALF], F32))
            ps_at = own.enter_context(nc.psum_tensor(f"{tag}_ps_at", [P, 2, HALF], F32))

            x_loaded = [sem(f"x_loaded{r}") for r in range(R)]
            ones_set = sem("ones_set")
            stat_step = sem("stat_step")
            var_ready = sem("var_ready")
            rstd_ready = sem("rstd_ready")
            shift_set = sem("shift_set")
            xn_low, xn_high = sem("xn_low"), sem("xn_high")
            turned = sem("turned")
            turn_taken = sem("turn_taken")
            hid_ready = sem("hid_ready")
            gelu_done = sem("gelu_done")
            logit_ready = sem("logit_ready")
            logit_taken = sem("logit_taken")
            top_step = sem("top_step")
            shift_ready = sem("shift_ready")
            exp_done = sem("exp_done")
            pick_step = sem("pick_step")
            alpha_ready = sem("alpha_ready")
            si_ready = sem("si_ready")
            den_step = sem("den_step")
            si_taken = sem("si_taken")
            at_ready, at_taken = sem("at_ready"), sem("at_taken")
            si_turned, si_t_ready = sem("si_turned"), sem("si_t_ready")

            block = own.enter_context(nc.Block())
            FILLS = KT * T // HALF
            assert FILLS == 4 and TT == 8
            LOW = TT // 2

            def over_batches(eng, step):
                for b in range(R):
                    step(b, 0, b, b)
                with eng.Fori(1, B // R - 1, 1) as q:
                    for r in range(R):
                        step(q * R + r, q, r, R + r)
                for b in range(B - R, B + 3):
                    step(b, b // R, b % R, b)

            def pairs_of(q, r):
                return q * (R // 2) + r // 2

            @block.sync
            def _(sp):
                for r in range(R):
                    sp.dma_start(x_ring[:, r, :, 0:D], rows(x_in, r)).then_inc(x_loaded[r], 16)

                def load(b, q, r, n):
                    if 2 <= n < B - 2:
                        sp.wait_ge(si_ready, b - 1)
                        sp.dma_start(x_ring[:, (r + 2) % R, :, 0:D], rows(x_in, b + 2)).then_inc(x_loaded[(r + 2) % R], 16)
                over_batches(sp, load)

            @block.gpsimd
            def _(pool):
                pool.memset(x_ring[:, :, :, D:D + 1], 1.0).then_inc(ones_set, 1)

                def rsqrt(b):
                    pool.wait_ge(var_ready, b + 1)
                    pool.tensor_tensor(rstd[:, :], var_eps[:, :], c.neg_half[:, 0:TT], ALU.pow).then_inc(rstd_ready, 1)

                def less_largest(b):
                    pool.wait_ge(top_step, b * (2 * TT) + TT)
                    pool.tensor_tensor(shifted[:, :, :], logit[:, :, :], top8[:, :, 0:1].to_broadcast([P, TT, S]),
                                       ALU.subtract).then_inc(shift_ready, 1)

                def scale(b, pair, r, n):
                    pool.wait_ge(pick_step, b * 3 + 3)
                    if n >= R:
                        pool.wait_ge(at_ready, pair - 1)
                    pool.tensor_tensor(alpha[:, r // 2, :, r % 2, :], picked[:, :, :],
                                       inv_total[:, :].unsqueeze(2).to_broadcast([P, TT, S]),
                                       ALU.mult).then_inc(alpha_ready, 1)

                rsqrt(0)

                def step(b, q, r, n):
                    if 1 <= n <= B:
                        less_largest(b - 1)
                    if n + 1 < B:
                        pool.wait_ge(xn_high, b + 1)
                        rsqrt(b + 1)
                    if 1 <= n <= B:
                        scale(b - 1, q * (R // 2) + (r - 1) // 2, (r - 1) % R, n - 1)
                over_batches(pool, step)

            @block.vector
            def _(dve):
                def statistics(b, r):
                    base = b * (2 * TT)
                    dve.wait_ge(x_loaded[r], b * (16 // R) + (16 - r * (16 // R)))
                    for t in range(TT):
                        dve.bn_stats(stats[:, t, :], x_ring[:, r, t, 0:D]).then_inc(stat_step, 1)
                    dve.wait_ge(stat_step, base + TT)
                    dve.memset(waited[:, :], 0.0)
                    for t in range(TT):
                        dve.bn_aggr(mean_var[:, t, :], stats[:, t, :]).then_inc(stat_step, 1)
                    dve.wait_ge(stat_step, base + 2 * TT)
                    dve.tensor_scalar(var_eps[:, :], mean_var[:, :, 1], EPS, None, ALU.add).then_inc(var_ready, 1)

                def normalise(b, r):
                    dve.wait_ge(rstd_ready, b + 1)
                    dve.scalar_tensor_tensor(shift[:, :], mean_var[:, :, 0], -1.0, rstd[:, :], ALU.mult,
                                             ALU.mult).then_inc(shift_set, 1)
                    for t in range(LOW):
                        last = dve.tensor_scalar(x_ring[:, r, t, 0:D], x_ring[:, r, t, 0:D], mean_var[:, t, 0:1],
                                                 rstd[:, t:t + 1], ALU.subtract, ALU.mult)
                    last.then_inc(xn_low, 1)

                def find_top(b):
                    dve.wait_ge(logit_ready, b + 1)
                    dve.tensor_tensor(logit[:, :, :], ps_logit[:, :, :], c.b2[:, :].unsqueeze(1).to_broadcast([P, TT, S]),
                                      ALU.add).then_inc(logit_taken, 1)
                    dve.wait_ge(logit_taken, b + 1)
                    dve.memset(waited[:, :], 0.0)
                    for t in range(TT):
                        dve.max(top8[:, t, :], logit[:, t, :]).then_inc(top_step, 1)
                    dve.wait_ge(top_step, b * (2 * TT) + TT)
                    dve.memset(waited[:, :], 0.0)
                    for t in range(TT):
                        dve.match_replace(out=rest[:, t, :], in_to_replace=top8[:, t, :], in_values=logit[:, t, :],
                                          imm_value=NEG).then_inc(top_step, 1)

                def weigh(b, n):
                    if n >= 1:
                        dve.wait_ge(alpha_ready, b)
                    dve.wait_ge(top_step, b * (2 * TT) + 2 * TT)
                    dve.wait_ge(exp_done, b + 1)
                    dve.scalar_tensor_tensor(picked[:, :, :], rest[:, :, :], NEG, expd[:, :, :], ALU.is_equal,
                                             ALU.mult).then_inc(pick_step, 1)
                    dve.wait_ge(pick_step, b * 3 + 1)
                    dve.tensor_reduce(total[:, :], picked[:, :, :], AX.X, ALU.add).then_inc(pick_step, 1)
                    dve.wait_ge(pick_step, b * 3 + 2)
                    dve.reciprocal(inv_total[:, :], total[:, :]).then_inc(pick_step, 1)

                def divide(pairs, n):
                    dve.wait_ge(si_ready, pairs * 2)
                    dve.tensor_scalar(den_eps[:, :], ps_si[:, D:D + 1], 1e-8, None, ALU.add).then_inc(den_step, 1)
                    dve.wait_ge(den_step, pairs * 2 - 1)
                    dve.reciprocal(den_inv[:, :], den_eps[:, :]).then_inc(den_step, 1)
                    dve.wait_ge(den_step, pairs * 2)
                    if n >= 5:
                        dve.wait_ge(si_turned, pairs - 1)
                    dve.tensor_scalar(si_rows[:, :], ps_si[:, 0:D], den_inv[:, 0:1], None, ALU.mult).then_inc(si_taken, 1)

                statistics(0, 0)
                normalise(0, 0)

                def step(b, q, r, n):
                    if 1 <= n <= B:
                        find_top(b - 1)
                    if n + 1 < B:
                        statistics(b + 1, (r + 1) % R)
                    if 1 <= n <= B:
                        weigh(b - 1, n - 1)
                    if n + 1 < B:
                        normalise(b + 1, (r + 1) % R)
                    if n % 2 and 3 <= n <= B + 1:
                        divide(pairs_of(q, r), n)
                over_batches(dve, step)

            @block.tensor
            def _(pe):
                def turn_rows(b, r, n, fills):
                    for f in fills:
                        if f < 2:
                            pe.wait_ge((xn_low, xn_high)[f], b + 1)
                        if n * FILLS + f >= 2:
                            pe.wait_ge(turn_taken, b * FILLS + (f - 1))
                        for j in range(4):
                            k, t = divmod(4 * f + j, TT)
                            last = pe.transpose(ps_turn[:, f % 2, j * P:(j + 1) * P],
                                                x_ring[:, r, t, k * P:(k + 1) * P], c.ident[:, :])
                        last.then_inc(turned, 1)

                def hidden(b, n):
                    pe.wait_ge(turn_taken, b * FILLS + FILLS)
                    if n >= 1:
                        pe.wait_ge(gelu_done, b)
                    for h in range(T // HALF):
                        for k in range(KT):
                            last = pe.matmul(ps_hid[:, h, :], c.w1[:, k, :], xn_t[:, k, h * HALF:(h + 1) * HALF],
                                             start=(k == 0), stop=(k == KT - 1))
                    last.then_inc(hid_ready, 1)

                def logits(b, n):
                    pe.wait_ge(gelu_done, b + 1)
                    if n >= 1:
                        pe.wait_ge(logit_taken, b)
                    for t in range(TT):
                        last = pe.matmul(ps_logit[:, t, :], hid[:, t * P:(t + 1) * P], c.w2[:, :], start=True, stop=True)
                    last.then_inc(logit_ready, 1)

                def sum_tokens(b, pair, r, n, tiles):
                    e = r % 2
                    if tiles[0] == 0:
                        pe.wait_ge(alpha_ready, b + 1)
                        if n >= 2 and e == 0:
                            pe.wait_ge(si_taken, pair)
                    for t in tiles:
                        last = pe.matmul(ps_si[e * S:(e + 1) * S, 0:D + 1], alpha[:, r // 2, t, e, :], x_ring[:, r, t, :],
                                         start=(t == 0), stop=(t == TT - 1), skip_group_check=True)
                    if t == TT - 1:
                        last.then_inc(si_ready, 1)

                def turn_weights(pairs, r, n):
                    if n >= 5:
                        pe.wait_ge(si_t_ready, pairs - 1)
                    for t in range(TT):
                        last = pe.transpose(ps_at[:, t // 4, (t % 4) * P:(t % 4 + 1) * P],
                                            alpha[:, (r - 3) % R // 2, t].rearrange("p e s -> p (e s)"), c.ident[:, :])
                    last.then_inc(at_ready, 1)

                def turn_sums(pairs):
                    pe.wait_ge(at_taken, pairs - 1)
                    pe.wait_ge(si_taken, pairs - 1)
                    for k in range(KT):
                        last = pe.transpose(ps_at[:, 0, k * P:(k + 1) * P], si_rows[:, k * P:(k + 1) * P], c.ident[:, :])
                    last.then_inc(si_turned, 1)

                pe.wait_ge(ones_set, 1)

                def step(b, q, r, n):
                    def sums(*tiles):
                        if 2 <= n <= B + 1:
                            sum_tokens(b - 2, q * (R // 2) + (r - 2) // 2, (r - 2) % R, n - 2, tiles)
                    if n < B:
                        turn_rows(b, r, n, (0, 1))
                    sums(0)
                    if n < B:
                        turn_rows(b, r, n, (2, 3))
                    sums(1, 2, 3)
                    if n < B:
                        hidden(b, n)
                    if n % 2 == 0 and n >= 4:
                        turn_sums(pairs_of(q, r))
                    sums(4, 5, 6, 7)
                    if n % 2 and 3 <= n <= B + 1:
                        turn_weights(pairs_of(q, r), r, n)
                    if n < B:
                        logits(b, n)
                over_batches(pe, step)

            @block.scalar
            def _(act):
                def normalise(b, r):
                    act.wait_ge(shift_set, b + 1)
                    for t in range(LOW, TT):
                        last = act.activation(x_ring[:, r, t, 0:D], x_ring[:, r, t, 0:D], ACT.Identity,
                                              bias=shift[:, t:t + 1], scale=rstd[:, t:t + 1])
                    last.then_inc(xn_high, 1)

                normalise(0, 0)

                def step(b, q, r, n):
                    flat = xn_t[:, :, :].rearrange("p k t -> p (k t)")
                    if n < B:
                        for f in range(FILLS):
                            act.wait_ge(turned, b * FILLS + (f + 1))
                            act.activation(flat[:, f * HALF:(f + 1) * HALF], ps_turn[:, f % 2, :],
                                           ACT.Identity).then_inc(turn_taken, 1)
                    if 1 <= n <= B:
                        act.wait_ge(shift_ready, b)
                        act.activation(expd[:, :, :], shifted[:, :, :], ACT.Exp).then_inc(exp_done, 1)
                    if n < B:
                        act.wait_ge(hid_ready, b + 1)
                        if n >= 1:
                            act.wait_ge(logit_ready, b)
                        act.activation(hid[:, :].rearrange("p (n h) -> p n h", n=2), ps_hid[:, :, :], ACT.Gelu,
                                       bias=c.hid_bias[:, 0:1]).then_inc(gelu_done, 1)
                    if n + 1 < B:
                        normalise(b + 1, (r + 1) % R)
                    pairs = pairs_of(q, r)
                    if n % 2 and 3 <= n <= B + 1:
                        act.wait_ge(at_ready, pairs)
                        act.activation(alpha_t[:, bass.ds(pairs - 1, 1), :].rearrange("p a (n h) -> p (a n) h", n=2),
                                       ps_at[:, :, :], ACT.Identity).then_inc(at_taken, 1)
                    if n % 2 == 0 and n >= 4:
                        act.wait_ge(si_turned, pairs - 1)
                        act.activation(si_t[:, :, bass.ds((pairs - 2) * P, P)],
                                       ps_at[:, 0, 0:D].rearrange("p (k s) -> p k s", k=KT),
                                       ACT.Identity).then_inc(si_t_ready, 1)
                over_batches(act, step)

        RP = 4
        EARLY = 3
        x_early = sb("x_early", [P, EARLY, 2, TT, D])
        back_loaded = [sem(f"back_loaded{r}") for r in range(RP)]

        with ExitStack() as own:
            gates = slot_out[:, :, :, :].rearrange("p a e d -> p (a e d)").rearrange("p (m n) -> p m n", m=2 * KT)
            pre = sb("pre", [P, KT, NS], F32, own)
            cand = sb("cand", [P, KT, NS], F32, own)
            mix = sb("mix", [P, KT, NS], F32, own)
            mix_z = sb("mix_z", [P, KT, NS], F32, own)
            new_t = sb("new_t", [P, KT, NS], F32, own)
            q_t = sb("q_t", [S, NS], F32, own)
            k_t = sb("k_t", [S, NS], F32, own)
            s_max = sb("s_max", [P, PAIRS], F32, own)
            s_shift = sb("s_shift", [P, PAIRS, S], F32, own)
            s_exp = sb("s_exp", [P, PAIRS, S], F32, own)
            s_sum = sb("s_sum", [P, PAIRS], F32, own)
            s_inv = sb("s_inv", [P, PAIRS], F32, own)
            attn = sb("attn", [P, PAIRS, P], F32, own)
            attn_t = sb("attn_t", [P, PAIRS, P], F32, own)
            stats = sb("y_stats", [P, PAIRS, 6], F32, own)
            mean_var = sb("y_mean_var", [P, PAIRS, 2], F32, own)
            var_eps = sb("y_var_eps", [P, PAIRS], F32, own)
            rstd = sb("y_rstd", [P, PAIRS], F32, own)
            b_out = sb("b_out", [P, D], F32, own)
            y_t, val_t = pre, mix
            v_sb = mix_z[:, :, :].rearrange("p k n -> p (k n)").rearrange("p (a d) -> p a d", d=D)
            y_hat = cand[:, :, :].rearrange("p k n -> p (k n)").rearrange("p (a d) -> p a d", d=D)
            ps = own.enter_context(nc.psum_tensor(f"{tag}_ps_slot", [P, 8, HALF], F32))

            gi_ready, gate_taken = sem("gi_ready"), sem("gate_taken")
            tanh_done, gate_ready = sem("tanh_done"), sem("gate_ready")
            cand_step, cand_ready, mix_step = sem("cand_step"), sem("cand_ready"), sem("mix_step")
            qk_ready, qk_taken = sem("qk_ready"), sem("qk_taken")
            v_ready, v_taken = sem("v_ready"), sem("v_taken")
            score_ready, soft_step, soft_exp = sem("score_ready"), sem("soft_step"), sem("soft_exp")
            attn_zero, attn_ready = sem("attn_zero"), sem("attn_ready")
            attn_turned, attn_taken = sem("attn_turned"), sem("attn_taken")
            y_ready, y_step = sem("y_ready"), sem("y_step")
            y_var, y_rstd, yhat_ready = sem("y_var"), sem("y_rstd"), sem("yhat_ready")
            y_turned, yt_ready = sem("y_turned"), sem("yt_ready")
            val_ready, val_taken = sem("val_ready"), sem("val_taken")
            out_ready, out_taken = sem("out_ready"), sem("out_taken")
            b_out_loaded, out_zero = sem("b_out_loaded"), sem("out_zero")

            block = own.enter_context(nc.Block())
            NH = NS // HALF
            QP = PAIRS // 2
            GATES = [m for k in range(KT) for m in (k, 2 * KT + k, KT + k)]

            def pair_banks(n):
                return ps[:, 2 * (n % 4):2 * (n % 4) + NH, :]

            def cols(ap):
                return ap.rearrange("p (n h) -> p n h", h=HALF)

            @block.tensor
            def _(pe):
                def project(n, weights, moving, rows_out=P):
                    for h in range(NH):
                        for k in range(KT):
                            last = pe.matmul(ps[0:rows_out, 2 * (n % 4) + h, :], weights(k),
                                             moving[:, k, h * HALF:(h + 1) * HALF], start=(k == 0), stop=(k == KT - 1))
                    return last
                for n, m in enumerate(GATES):
                    if n >= 4:
                        pe.wait_ge(gate_taken, n - 3)
                    project(n, lambda k: c.wih_t[:, k, m * P:(m + 1) * P], si_t).then_inc(gi_ready, 1)
                pe.wait_ge(gate_taken, MT)
                for k in range(KT):
                    pe.wait_ge(mix_step, 3 * k + 3)
                    for n, weights in enumerate((c.wq, c.wk)):
                        for h in range(NH):
                            last = pe.matmul(ps[0:S, 4 + 2 * n + h, :], weights[:, k, :],
                                             new_t[:, k, h * HALF:(h + 1) * HALF], start=(k == 0), stop=(k == KT - 1))
                        if k == KT - 1:
                            last.then_inc(qk_ready, 1)

                def values(g):
                    for pair in (2 * g, 2 * g + 1):
                        for k in range(KT):
                            last = pe.matmul(ps[:, g, (pair % 2) * D:(pair % 2 + 1) * D],
                                             new_t[:, k, pair * P:(pair + 1) * P], c.wv[:, k, :],
                                             start=(k == 0), stop=(k == KT - 1))
                    last.then_inc(v_ready, 1)
                values(0)
                values(1)
                pe.wait_ge(qk_taken, 2)
                for b in range(B):
                    half = b % 2 * S
                    last = pe.matmul(ps[half:half + S, 4, b // 2 * S:(b // 2 + 1) * S], q_t[:, b * S:(b + 1) * S],
                                     k_t[:, b * S:(b + 1) * S], start=True, stop=True)
                last.then_inc(score_ready, 1)
                values(2)
                values(3)
                y = [ps[:, pair // 2, (pair % 2) * D:(pair % 2 + 1) * D] for pair in range(PAIRS)]
                for pair in range(PAIRS):
                    if pair % 2 == 0:
                        pe.wait_ge(v_taken, pair // 2 + 1)
                    for k in range(KT):
                        pe.matmul(y[pair][:, k * P:(k + 1) * P], new_t[:, k, pair * P:(pair + 1) * P], c.ident[:, :],
                                  start=(pair % 2 == 0 and k == 0), stop=False, skip_group_check=True)
                pe.wait_ge(attn_ready, 2)
                for pair in range(PAIRS):
                    last = pe.transpose(ps[:, 6 + pair // 4, (pair % 4) * P:(pair % 4 + 1) * P], attn[:, pair, :],
                                        c.ident[:, :])
                    if pair % 4 == 3:
                        last.then_inc(attn_turned, 1)
                for pair in range(PAIRS):
                    if pair % 4 == 0:
                        pe.wait_ge(attn_taken, pair // 4 + 1)
                    pe.matmul(y[pair], attn_t[:, pair, :], v_sb[:, pair, :], start=False, stop=True,
                              skip_group_check=True).then_inc(y_ready, 1)
                pe.wait_ge(attn_taken, 2)
                for half in range(2):
                    pe.wait_ge(yhat_ready, half + 1)
                    for k in range(KT):
                        for i in range(QP):
                            last = pe.transpose(ps[:, 4 + 2 * half + k, i * P:(i + 1) * P],
                                                y_hat[:, QP * half + i, k * P:(k + 1) * P], c.ident[:, :])
                        last.then_inc(y_turned, 1)
                for half in range(2):
                    pe.wait_ge(yt_ready, KT * (half + 1))
                    for m in range(KT):
                        for k in range(KT):
                            last = pe.matmul(ps[:, 2 * half + m, :], c.wvp[:, k, m * P:(m + 1) * P],
                                             y_t[:, k, half * HALF:(half + 1) * HALF], start=(k == 0), stop=(k == KT - 1))
                        last.then_inc(val_ready, 1)
                for pair in range(PAIRS):
                    if pair % QP == 0:
                        pe.wait_ge(val_taken, KT * (pair // QP + 1))
                    for k in range(KT):
                        last = pe.matmul(ps[:, 4 + pair // 2, (pair % 2) * D:(pair % 2 + 1) * D],
                                         val_t[:, k, pair * P:(pair + 1) * P], c.wo[:, k, :],
                                         start=(k == 0), stop=(k == KT - 1))
                    if pair % 2:
                        last.then_inc(out_ready, 1)

            @block.vector
            def _(dve):
                def per_batch(ap):
                    return ap.unsqueeze(1).to_broadcast([P, B, S])

                def by_batch(ap):
                    return ap.rearrange("p (b s) -> p b s", s=S)

                def banks_by_batch(n):
                    return pair_banks(n).rearrange("p n (b s) -> p (n b) s", s=S)

                dve.memset(attn[:, :, :], 0.0).then_inc(attn_zero, 1)
                def gate(n, m):
                    dve.wait_ge(gi_ready, n + 1)
                    dve.tensor_tensor(by_batch(gates[:, m, :]), banks_by_batch(n), per_batch(c.gh_t[:, m, :]),
                                      ALU.add).then_inc(gate_taken, 1)

                def squash(m, count):
                    dve.wait_ge(tanh_done, count)
                    dve.tensor_scalar(gates[:, m, :], gates[:, m, :], 0.5, 0.5, ALU.mult, ALU.add).then_inc(gate_ready, 1)

                for k in range(KT):
                    m = 2 * KT + k
                    gate(3 * k, k)
                    squash(k, 2 * k + 1)
                    dve.wait_ge(gate_ready, 2 * k + 1)
                    dve.tensor_tensor(by_batch(pre[:, k, :]), by_batch(gates[:, k, :]), per_batch(c.gh_t[:, m, :]),
                                      ALU.mult).then_inc(cand_step, 1)
                    dve.wait_ge(gi_ready, 3 * k + 2)
                    dve.wait_ge(cand_step, k + 1)
                    dve.scalar_tensor_tensor(cols(pre[:, k, :]), pair_banks(3 * k + 1), c.gate_bias[:, m:m + 1],
                                             cols(pre[:, k, :]), ALU.add, ALU.add).then_inc(gate_taken, 1)
                    gate(3 * k + 2, KT + k)
                    old = per_batch(c.slots_t[:, k, :])
                    dve.wait_ge(cand_ready, k + 1)
                    dve.tensor_tensor(by_batch(mix[:, k, :]), old, by_batch(cand[:, k, :]), ALU.subtract).then_inc(mix_step, 1)
                    squash(KT + k, 2 * k + 2)
                    dve.wait_ge(gate_ready, 2 * k + 2)
                    dve.wait_ge(mix_step, 3 * k + 1)
                    dve.tensor_tensor(mix_z[:, k, :], mix[:, k, :], gates[:, KT + k, :], ALU.mult).then_inc(mix_step, 1)
                    dve.wait_ge(mix_step, 3 * k + 2)
                    dve.tensor_tensor(new_t[:, k, :], mix_z[:, k, :], cand[:, k, :], ALU.add).then_inc(mix_step, 1)
                def take_values(g):
                    dve.wait_ge(v_ready, g + 1)
                    dve.tensor_tensor(v_sb[:, 2 * g:2 * g + 2, :], ps[:, g, :].rearrange("p (a d) -> p a d", d=D),
                                      c.bv[:, :].unsqueeze(1).to_broadcast([P, 2, D]), ALU.add).then_inc(v_taken, 1)
                take_values(0)
                take_values(1)
                scores = ps[:, 4, :].rearrange("p (a s) -> p a s", s=S)
                dve.wait_ge(score_ready, 1)
                dve.tensor_reduce(s_max[:, :], scores, AX.X, ALU.max).then_inc(soft_step, 1)
                dve.wait_ge(soft_step, 1)
                dve.tensor_tensor(s_shift[:, :, :], scores, s_max[:, :].unsqueeze(2).to_broadcast([P, PAIRS, S]),
                                  ALU.subtract).then_inc(soft_step, 1)
                take_values(2)
                dve.wait_ge(soft_exp, 1)
                dve.tensor_reduce(s_sum[:, :], s_exp[:, :, :], AX.X, ALU.add).then_inc(soft_step, 1)
                dve.wait_ge(soft_step, 3)
                dve.reciprocal(s_inv[:, :], s_sum[:, :]).then_inc(soft_step, 1)
                take_values(3)
                dve.wait_ge(soft_step, 4)
                dve.wait_ge(attn_zero, 1)
                for h in range(2):
                    rows_h = slice(h * S, (h + 1) * S)
                    dve.tensor_tensor(attn[rows_h, :, rows_h], s_exp[rows_h, :, :],
                                      s_inv[rows_h, :].unsqueeze(2).to_broadcast([S, PAIRS, S]),
                                      ALU.mult).then_inc(attn_ready, 1)
                for half in range(2):
                    dve.wait_ge(attn_turned, half + 1)
                    dve.tensor_copy(attn_t[:, QP * half:QP * (half + 1), :].rearrange("p a s -> p (a s)"),
                                    ps[:, 6 + half, :]).then_inc(attn_taken, 1)
                y_rows = ps[:, 0:PAIRS // 2, :].rearrange("p n (a d) -> p (n a) d", d=D)
                for half in range(2):
                    mine = range(QP * half, QP * (half + 1))
                    for a in mine:
                        dve.wait_ge(y_ready, a // 2 * 2 + 2)
                        dve.bn_stats(stats[:, a, :], y_rows[:, a, :]).then_inc(y_step, 1)
                    dve.wait_ge(y_step, (2 * half + 1) * QP)
                    for a in mine:
                        dve.bn_aggr(mean_var[:, a, :], stats[:, a, :]).then_inc(y_step, 1)
                    dve.wait_ge(y_step, (2 * half + 2) * QP)
                    part = slice(QP * half, QP * (half + 1))
                    dve.tensor_scalar(var_eps[:, part], mean_var[:, part, 1], EPS, None, ALU.add).then_inc(y_var, 1)
                for half in range(2):
                    dve.wait_ge(y_rstd, half + 1)
                    for a in range(QP * half, QP * (half + 1)):
                        last = dve.tensor_scalar(y_hat[:, a, :], y_rows[:, a, :], mean_var[:, a, 0:1], rstd[:, a:a + 1],
                                                 ALU.subtract, ALU.mult)
                    last.then_inc(yhat_ready, 1)
                dve.wait_ge(b_out_loaded, 16)
                dve.wait_ge(out_zero, 1)
                for g in range(PAIRS // 2):
                    dve.wait_ge(out_ready, g + 1)
                    for h in range(2):
                        rows_h = slice(h * S, (h + 1) * S)
                        dve.tensor_tensor(slot_out[rows_h, 2 * g:2 * g + 2, h, :],
                                          ps[rows_h, 4 + g, :].rearrange("p (a d) -> p a d", d=D),
                                          b_out[rows_h, :].unsqueeze(1).to_broadcast([S, 2, D]),
                                          ALU.add).then_inc(out_taken, 1)
                dve.wait_ge(out_taken, PAIRS)

            @block.sync
            def _(sp):
                sp.dma_start(b_out[:, :], bo.partition_broadcast(P)).then_inc(b_out_loaded, 16)
                for r in range(EARLY):
                    for e in range(2):
                        sp.dma_start(x_early[:, r, e], rows(x_in, 2 * r + e)).then_inc(back_loaded[r], 16)
                for r in range(EARLY):
                    sp.wait_ge(back_loaded[r], 32)

            @block.gpsimd
            def _(pool):
                pool.wait_ge(mix_step, 3 * KT)
                pool.memset(slot_out[:, :, :, :], 0.0).then_inc(out_zero, 1)
                for half in range(2):
                    part = slice(QP * half, QP * (half + 1))
                    pool.wait_ge(y_var, half + 1)
                    pool.tensor_tensor(rstd[:, part], var_eps[:, part], c.neg_half[:, 0:QP], ALU.pow).then_inc(y_rstd, 1)

            @block.scalar
            def _(act):
                for k in range(KT):
                    act.wait_ge(gate_taken, 3 * k + 1)
                    act.activation(gates[:, k, :], gates[:, k, :], ACT.Tanh, scale=0.5).then_inc(tanh_done, 1)
                    act.wait_ge(gate_taken, 3 * k + 2)
                    act.activation(cand[:, k, :], pre[:, k, :], ACT.Tanh).then_inc(cand_ready, 1)
                    act.wait_ge(gate_taken, 3 * k + 3)
                    act.activation(gates[:, KT + k, :], gates[:, KT + k, :], ACT.Tanh, scale=0.5).then_inc(tanh_done, 1)
                for n, (dst, bias) in enumerate(((q_t, c.bq), (k_t, c.bk))):
                    act.wait_ge(qk_ready, n + 1)
                    act.activation(cols(dst[:, :]), ps[0:S, 4 + 2 * n:6 + 2 * n, :], ACT.Identity,
                                   bias=bias[:, 0:1]).then_inc(qk_taken, 1)
                act.wait_ge(soft_step, 2)
                act.activation(s_exp[:, :, :], s_shift[:, :, :], ACT.Exp, scale=float(S) ** -0.5).then_inc(soft_exp, 1)
                for half in range(2):
                    here = slice(half * HALF, (half + 1) * HALF)
                    for k in range(KT):
                        act.wait_ge(y_turned, KT * half + k + 1)
                        act.activation(y_t[:, k, here], ps[:, 4 + 2 * half + k, :], ACT.Identity,
                                       bias=c.ln_b[:, k:k + 1], scale=c.ln_g[:, k:k + 1]).then_inc(yt_ready, 1)
                for half in range(2):
                    here = slice(half * HALF, (half + 1) * HALF)
                    for m in range(KT):
                        act.wait_ge(val_ready, KT * half + m + 1)
                        act.activation(val_t[:, m, here], ps[:, 2 * half + m, :], ACT.Identity,
                                       bias=c.bvp[:, m:m + 1]).then_inc(val_taken, 1)

        with ExitStack() as own:
            x_late = sb("x_late", [P, RP - EARLY, 2, TT, D], F32, own)
            xc = [x_early[:, i] for i in range(EARLY)] + [x_late[:, i] for i in range(RP - EARLY)]
            ps = own.enter_context(nc.psum_tensor(f"{tag}_ps_back", [P, TT, 2, D], F32))
            stored = [sem(f"stored{r}") for r in range(RP)]
            mixed, added = sem("mixed"), sem("added")
            block = own.enter_context(nc.Block())

            def over_pairs(eng, step):
                step(0, True)
                with eng.Fori(1, PAIRS // RP, 1) as q:
                    step(q, False)

            @block.sync
            def _(sp):
                def step(q, first):
                    for r in range(RP):
                        if first and r < EARLY:
                            continue
                        if not first:
                            sp.wait_ge(stored[r], q * 32)
                        for e in range(2):
                            sp.dma_start(xc[r][:, e], rows(x_in, q * (2 * RP) + (2 * r + e))).then_inc(back_loaded[r], 16)
                over_pairs(sp, step)

            @block.tensor
            def _(pe):
                def step(q, first):
                    for r in range(RP):
                        for t in range(TT):
                            if not (first and r == 0):
                                pe.wait_ge(added, q * (RP * TT) + ((r - 1) * TT + t + 1))
                            pe.matmul(ps[:, t].rearrange("p e d -> p (e d)"),
                                      alpha_t[:, bass.ds(q * RP + r, 1), t * P:(t + 1) * P].rearrange("p a n -> p (a n)"),
                                      slot_out[:, bass.ds(q * RP + r, 1), :, :].rearrange("p a e d -> p (a e d)"),
                                      start=True, stop=True).then_inc(mixed, 1)
                over_pairs(pe, step)

            @block.vector
            def _(dve):
                def step(q, first):
                    for r in range(RP):
                        dve.wait_ge(back_loaded[r], q * 32 + 32)
                        for t in range(TT):
                            dve.wait_ge(mixed, q * (RP * TT) + (r * TT + t + 1))
                            dve.scalar_tensor_tensor(xc[r][:, :, t, :], ps[:, t], 0.5, xc[r][:, :, t, :], ALU.mult,
                                                     ALU.add).then_inc(added, 1)
                over_pairs(dve, step)

            @block.scalar
            def _(act):
                def step(q, first):
                    for r in range(RP):
                        act.wait_ge(added, q * (RP * TT) + (r + 1) * TT)
                        for e in range(2):
                            act.dma_start(rows(x_out, q * (2 * RP) + (2 * r + e)), xc[r][:, e]).then_inc(stored[r], 16)
                over_pairs(act, step)
                for r in range(RP):
                    act.wait_ge(stored[r], PAIRS // RP * 32)

        clear(nc, sems)


def build_attention(nc, c, x_in, x_out, w_qkv, b_qkv, w_out, b_out):
    B, T, D = x_in.shape
    KT, TT = D // P, T // P
    H, DH = 16, D // 16
    GH = 4
    NG = H // GH
    CHUNKS = T // HALF
    GU = GH * TT * CHUNKS
    BU = NG * GU
    AHEAD = GU + 16
    NQ = 4
    Q_PARTS, K_PARTS = (0, 0, 1, 0, 2, 1), (0, 1, 0, 2, 0, 1)
    SR = len(Q_PARTS) * DH
    PREP = 3
    LAST_EARLY = 3
    B0 = 2

    QK_AT = [76, GU + 58, 2 * GU + 33, 3 * GU + 33]
    X_AT = 106
    V_AT = [70, 87, 2 * GU + 8, 2 * GU + 14]
    RATE = {"turn_x": 4, "qk": 2 * NG, "v": NG, "turn_max": NG, "turn_o": TT, "turn_ctx": TT, "project": TT}

    def jobs(b):
        out = []
        for qt in range(TT):
            out += [(7 + 8 * qt, "turn_o", TT * (b - 1) + qt), (12 + 8 * qt, "turn_ctx", TT * (b - 1) + qt),
                    (17 + 8 * qt, "project", TT * (b - 1) + qt)]
        for g in range(NG):
            u, G = g * GU, NG * b + g
            out += [(u + 52, "turn_max", G + 1)] + [(QK_AT[g] + 5 * i, "qk", 2 * (G + PREP) + i) for i in range(2)]
        out += [(X_AT + 3 * f, "turn_x", 4 * (b + 1) + f) for f in range(4)]
        out += [(at, "v", NG * b + 2 + i) for i, at in enumerate(V_AT)]
        if b == B - 1:
            for qt in range(LAST_EARLY):
                out += [(231 + 7 * qt, "turn_o", TT * b + qt), (235 + 7 * qt, "turn_ctx", TT * b + qt),
                        (240 + 7 * qt, "project", TT * b + qt)]
        return sorted(out)

    WINDOW = TT * GH
    PIECES = {2 * k + 5 if k > 1 else 7 + k: k for k in range(2 * TT)}

    def score_bank(u):
        return 2 + (u % 3 if u < BU - 1 else 1)

    def since(u):
        return next(n for n in range(1, BU) if score_bank((u - n) % BU) == score_bank(u))

    LIMIT = {k: r * B for k, r in RATE.items()}

    def body_jobs(b):
        return [j for j in jobs(b) if 0 <= j[2] < LIMIT[j[1]]]

    bank_of = {(kind, n % RATE[kind]): 6 + i % 2 for i, (_, kind, n) in enumerate(jobs(B0))}
    opening = [(0, "turn_x", f) for f in range(4)] + [(0, "qk", 0), (0, "qk", 1), (0, "v", 0), (1, "v", 1),
               (3, "qk", 2), (6, "qk", 3), (30, "qk", 4), (33, "qk", 5), (68, "turn_max", 0)]
    assert PREP == 3 and AHEAD > 68
    closing = []
    for s in range(LAST_EARLY, TT + 2):
        closing += [(s, kind, TT * (B - 1) + s - lag) for lag, kind in enumerate(("turn_o", "turn_ctx", "project"))
                    if LAST_EARLY <= s - lag < TT]
    before = {}
    holder = {}
    for _, kind, n in opening + [j for b in range(B) for j in body_jobs(b)] + closing:
        bank = bank_of[kind, n % RATE[kind]]
        before[kind, n] = holder.get(bank)
        holder[bank] = (kind, n)

    with ExitStack() as ctx:
        def sb(name, shape, dt=F32):
            return ctx.enter_context(nc.sbuf_tensor(f"attn_{name}", shape, dt))

        def sem(name):
            sems.append(ctx.enter_context(nc.semaphore(f"attn_{name}")))
            return sems[-1]

        sems = []
        blocks = ExitStack()
        w_qk = sb("w_qk", [P, KT, NG, P])
        b_qk = sb("b_qk", [P, NG])
        w_v = sb("w_v", [P, KT, D])
        b_v = sb("b_v", [P, D])
        w_o = sb("w_o", [P, KT, D])
        b_o = sb("b_o", [P, D])
        x_ln = sb("x_ln", [P, TT, D])
        x_res = sb("x_res", [P, TT, D])
        stats = sb("stats", [P, TT, 6])
        mean_var = sb("mean_var", [P, TT, 2])
        waited, pool_waited = sb("waited", [P, 1]), sb("pool_waited", [P, 1])
        var_eps = sb("var_eps", [P, TT])
        rstd = sb("rstd", [P, TT])
        xn_t = sb("xn_t", [P, KT, T])
        qk = sb("qk", [P, T])
        qk_rest = sb("qk_rest", [P, T])
        parts = sb("parts", [P, 3, T], BF16)
        q_rows = sb("q_rows", [SR + 3, NG, GH, T], BF16)
        k_rows = sb("k_rows", [SR + 3, NG, GH, T], BF16)
        v_ones = sb("v_ones", [P, NG, TT, GH, 2 * DH])
        probs = sb("probs", [P, NQ, GH, HALF])
        o_sb = sb("o_sb", [P, NG, T])
        part_max = sb("part_max", [P, 2, GU])
        neg_max = sb("neg_max", [P, 2, GU // 2])
        max_whole = sb("max_whole", [GU // 2, P])
        max_rest = sb("max_rest", [GU // 2, P])
        max_parts = sb("max_parts", [GU // 2, 3, P], BF16)
        sum_inv = sb("sum_inv", [P, 2, H])
        ctx_rows = sb("ctx_rows", [P, 2, D])
        ctx_t = sb("ctx_t", [P, 2, KT, P])
        w_raw = o_sb[:, 0, :].rearrange("p (k n) -> p k n", k=KT)
        ps = ctx.enter_context(nc.psum_tensor("attn_ps", [P, 8, HALF], F32))

        weights_loaded, w_raw_loaded = sem("weights_loaded"), sem("w_raw_loaded")
        w_qk_ready, ones_ready, v_filled = sem("w_qk_ready"), sem("ones_ready"), sem("v_filled")
        x_loaded, res_loaded, res_ready = sem("x_loaded"), sem("res_loaded"), sem("res_ready")
        stat_step, var_ready, rstd_ready, xn_ready = sem("stat_step"), sem("var_ready"), sem("rstd_ready"), sem("xn_ready")
        ready = {k: sem(f"{k}_ready") for k in RATE}
        taken = {k: sem(f"{k}_taken") for k in RATE if k != "qk"}
        qk_whole, part1_ready = sem("qk_whole"), sem("part1_ready")
        taken["qk"] = part1_ready
        rest_ready, part2_ready, part3_ready = sem("rest_ready"), sem("part2_ready"), sem("part3_ready")
        rows_loaded = [sem(f"rows_loaded{g}") for g in range(NG)]
        max_tile_ready, max_tile_taken = sem("max_tile_ready"), sem("max_tile_taken")
        neg_max_ready, max_split, max_parts_ready = sem("neg_max_ready"), sem("max_split"), sem("max_parts_ready")
        max_loaded = [sem(f"max_loaded{g}") for g in range(NG)]
        scores_ready, exp_done, pv_done, o_taken = sem("scores_ready"), sem("exp_done"), sem("pv_done"), sem("o_taken")
        inv_ready = sem("inv_ready")
        stored = sem("stored")

        block = blocks.enter_context(nc.Block())

        def over_batches(eng, body):
            body(0, 0)
            with eng.Fori(1, B - 1, 1) as b:
                body({1: b, "eng": eng}, B0)
            body(B - 1, B - 1)

        def value(b, rate, n):
            if isinstance(b, int):
                return n
            if rate not in b:
                b[rate] = b["eng"].snap(b[1] * rate)
            return b[rate] + (n - B0 * rate)

        def wait(eng, sem_, b, rate, n):
            if n <= 0:
                assert isinstance(b, int)
                return
            assert isinstance(b, int) or n > rate, (rate, n)
            eng.wait_ge(sem_, value(b, rate, n))

        def rows(t, b, b0, ahead=0):
            at = b if isinstance(b, int) else b[1]
            return t[bass.ds(at + ahead, 1)].rearrange("a (p t) d -> (a p) t d", t=TT)

        @block.sync
        def _(sp):
            sp.dma_start(x_ln[:, :, :], rows(x_in, 0, 0)).then_inc(x_loaded, 16)
            sp.dma_start(w_raw, w_qkv[:, 0:2 * D].rearrange("(k p) n -> p k n", p=P)).then_inc(w_raw_loaded, 16)
            sp.dma_start(w_v[:, :, :], w_qkv[:, 2 * D:3 * D].rearrange("(k p) n -> p k n", p=P)).then_inc(weights_loaded, 16)
            sp.dma_start(w_o[:, :, :], w_out.rearrange("(k p) n -> p k n", p=P)).then_inc(weights_loaded, 16)
            sp.dma_start(b_v[:, :], b_qkv[2 * D:3 * D].partition_broadcast(P)).then_inc(weights_loaded, 16)
            sp.dma_start(b_o[:, :], b_out.partition_broadcast(P)).then_inc(weights_loaded, 16)
            for i in range(2):
                for g in range(NG):
                    src = b_qkv[i * D + g * GH * DH:i * D + (g + 1) * GH * DH].rearrange("(h d o) -> d h o", h=GH, o=1)
                    sp.dma_start(b_qk[i * 64:i * 64 + 64, g:g + 1], src).then_inc(weights_loaded, 16)

            def lay_out(b, b0, G):
                g = G % NG
                for part in range(3):
                    if part < 2:
                        wait(sp, (part1_ready, part2_ready)[part], b, 2 * NG, 2 * G + 2)
                    else:
                        wait(sp, part3_ready, b, NG, G + 1)
                    for dst, order, half in ((q_rows, Q_PARTS, 0), (k_rows, K_PARTS, 1)):
                        for i in range(len(order)):
                            if order[i] == part:
                                sp.dma_start(dst[i * DH:(i + 1) * DH, g, :, :],
                                             parts[half * 64:half * 64 + 64, part, :]).then_inc(rows_loaded[g], 16)

            def max_rows(b, b0, G):
                wait(sp, max_parts_ready, b, NG, G + 1)
                for i in range(3):
                    sp.dma_start(q_rows[SR + i:SR + i + 1, G % NG, :, :],
                                 max_parts[:, i, :]).then_inc(max_loaded[G % NG], 16)

            for G in range(PREP):
                lay_out(0, 0, G)
            max_rows(0, 0, 0)

            def body(b, b0):
                if b0 < B - 1:
                    wait(sp, ready["turn_x"], b, 4, 4 * (b0 + 1))
                    sp.dma_start(x_ln[:, :, :], rows(x_in, b, b0, 1)).then_inc(x_loaded, 16)
                for g in range(NG):
                    G = NG * b0 + g
                    if G + 1 < NG * B:
                        max_rows(b, b0, G + 1)
                    if g == 0:
                        if b0 > 0:
                            wait(sp, taken["project"], b, TT, TT * b0)
                            sp.dma_start(rows(x_out, b, b0, -1), x_res[:, :, :]).then_inc(stored, 16)
                            wait(sp, stored, b, 16, 16 * b0)
                        sp.dma_start(x_res[:, :, :], rows(x_in, b, b0)).then_inc(res_loaded, 16)
                    if G + PREP < NG * B:
                        lay_out(b, b0, G + PREP)
            over_batches(sp, body)
            sp.wait_ge(taken["project"], TT * B)
            sp.dma_start(rows(x_out, B - 1, B - 1), x_res[:, :, :]).then_inc(stored, 16)
            sp.wait_ge(stored, 16 * B)

        @block.gpsimd
        def _(pool):
            pool.memset(v_ones[:, :, :, :, :], 1.0).then_inc(v_filled, 1)

            def split(b, b0, G):
                wait(pool, qk_whole, b, 2 * NG, 2 * G + 2)
                wait(pool, part1_ready, b, 2 * NG, 2 * G + 2)
                pool.tensor_tensor(qk_rest[:, :], qk[:, :], parts[:, 0, :], ALU.subtract).then_inc(rest_ready, 1)
                wait(pool, part2_ready, b, 2 * NG, 2 * G + 2)
                pool.tensor_tensor(parts[:, 2, :], qk_rest[:, :], parts[:, 1, :], ALU.subtract).then_inc(part3_ready, 1)

            def rsqrt(b, b0, n):
                wait(pool, var_ready, b, 1, n + 1)
                pool.tensor_tensor(rstd[:, :], var_eps[:, :], c.neg_half[:, 0:TT], ALU.pow).then_inc(rstd_ready, 1)

            def split_max(b, b0, G):
                wait(pool, taken["turn_max"], b, NG, G + 1)
                if G > 0:
                    wait(pool, max_loaded[(G - 1) % NG], b, 48, 48 * ((G - 1) // NG + 1))
                pool.tensor_tensor(pool_waited[:, :], c.ones[:, 0:1], c.ones[:, 0:1], ALU.mult)
                pool.tensor_copy(max_parts[:, 0, :], max_whole[:, :]).then_inc(max_split, 1)
                wait(pool, max_split, b, 3 * NG, 3 * G + 1)
                pool.tensor_tensor(max_rest[:, :], max_whole[:, :], max_parts[:, 0, :], ALU.subtract).then_inc(max_split, 1)
                wait(pool, max_split, b, 3 * NG, 3 * G + 2)
                pool.tensor_tensor(pool_waited[:, :], c.ones[:, 0:1], c.ones[:, 0:1], ALU.mult)
                pool.tensor_copy(max_parts[:, 1, :], max_rest[:, :]).then_inc(max_split, 1)
                wait(pool, max_split, b, 3 * NG, 3 * G + 3)
                pool.tensor_tensor(max_parts[:, 2, :], max_rest[:, :], max_parts[:, 1, :],
                                   ALU.subtract).then_inc(max_parts_ready, 1)

            rsqrt(0, 0, 0)
            for G in range(PREP):
                split(0, 0, G)
            split_max(0, 0, 0)
            pool.wait_ge(weights_loaded, 16 * (4 + 2 * NG))

            def body(b, b0):
                def operands(g):
                    if NG * b0 + g + PREP < NG * B:
                        split(b, b0, NG * b0 + g + PREP)

                def maxima(g):
                    if NG * b0 + g + 1 < NG * B:
                        split_max(b, b0, NG * b0 + g + 1)
                maxima(0)
                if b0 < B - 1:
                    rsqrt(b, b0, b0 + 1)
                operands(0)
                maxima(1)
                operands(1)
                wait(pool, res_loaded, b, 16, 16 * (b0 + 1))
                pool.tensor_tensor(x_res[:, :, :], x_res[:, :, :],
                                   b_o[:, :].unsqueeze(1).to_broadcast([P, TT, D]), ALU.add).then_inc(res_ready, 1)
                operands(2)
                maxima(2)
                operands(3)
                maxima(3)
            over_batches(pool, body)

        @block.vector
        def _(dve):
            def stat(b, b0, n, t):
                if t == 0:
                    wait(dve, x_loaded, b, 16, 16 * (n + 1))
                dve.bn_stats(stats[:, t, :], x_ln[:, t, :]).then_inc(stat_step, 1)

            def moments(b, b0, n, half):
                if half == 0:
                    wait(dve, stat_step, b, 2 * TT, 2 * TT * n + TT)
                    dve.memset(waited[:, :], 0.0)
                for t in range(half * TT // 2, (half + 1) * TT // 2):
                    dve.bn_aggr(mean_var[:, t, :], stats[:, t, :]).then_inc(stat_step, 1)
                if half == 0:
                    return
                wait(dve, stat_step, b, 2 * TT, 2 * TT * (n + 1))
                dve.tensor_scalar(var_eps[:, :], mean_var[:, :, 1], EPS, None, ALU.add).then_inc(var_ready, 1)

            def normalise(b, b0, n, t):
                if t == 0:
                    wait(dve, rstd_ready, b, 1, n + 1)
                ins = dve.tensor_scalar(x_ln[:, t, :], x_ln[:, t, :], mean_var[:, t, 0:1], rstd[:, t:t + 1],
                                        ALU.subtract, ALU.mult)
                if t == TT - 1:
                    ins.then_inc(xn_ready, 1)

            def values(b, b0, n, i):
                pair, half = n % NG // 2, n % 2
                bank = ps[:, bank_of["v", n % NG], :].rearrange("p (t g h d) -> p t g h d", t=TT // 2, g=2, h=GH)
                if i == 0:
                    wait(dve, ready["v"], b, NG, n + 1)
                g = 2 * pair + i
                bias = b_v[:, g * 64:(g + 1) * 64].rearrange("p (h d) -> p h d", h=GH)
                last = dve.tensor_tensor(v_ones[:, g, half * (TT // 2):(half + 1) * (TT // 2), :, 0:DH], bank[:, :, i],
                                         bias.unsqueeze(1).to_broadcast([P, TT // 2, GH, DH]), ALU.add)
                if i == 1:
                    last.then_inc(taken["v"], 1)

            def reduce_tile(b, b0, v):
                G, w = divmod(v, GU)
                wait(dve, max_tile_ready, b, BU, v + 1)
                dve.tensor_reduce(part_max[:, G % 2, w:w + 1], ps[:, v % 2, :], AX.X, ALU.max).then_inc(max_tile_taken, 1)
                if w == GU - 1:
                    wait(dve, max_tile_taken, b, BU, v + 1)
                    dve.tensor_reduce(neg_max[:, G % 2, :], part_max[:, G % 2, :].rearrange("p (n h) -> p n h", h=CHUNKS),
                                      AX.X, ALU.max, negate=True).then_inc(neg_max_ready, 1)

            def invert_sums(b, b0, n):
                bank = ps[:, bank_of["turn_o", n % TT], :].rearrange("p (h d) -> p h d", h=H)
                wait(dve, ready["turn_o"], b, TT, n + 1)
                dve.reciprocal(sum_inv[:, n % TT % 2, :], bank[:, :, DH]).then_inc(inv_ready, 1)

            def divide_out(b, b0, n):
                qt = n % TT
                bank = ps[:, bank_of["turn_o", qt], :].rearrange("p (h d) -> p h d", h=H)
                wait(dve, inv_ready, b, TT, n + 1)
                dve.tensor_tensor(ctx_rows[:, qt % 2, :].rearrange("p (h d) -> p h d", h=H), bank[:, :, 0:DH],
                                  sum_inv[:, qt % 2, :].unsqueeze(2).to_broadcast([P, H, DH]), ALU.mult).then_inc(taken["turn_o"], 1)

            def add_out(b, b0, n):
                qt = n % TT
                wait(dve, ready["project"], b, TT, n + 1)
                if qt == 0:
                    wait(dve, res_ready, b, 1, n // TT + 1)
                dve.tensor_tensor(x_res[:, qt, :], ps[:, bank_of["project", qt], 0:D], x_res[:, qt, :],
                                  ALU.add).then_inc(taken["project"], 1)

            uses = {"v": [(1, lambda b, b0, n: values(b, b0, n, 0)), (3, lambda b, b0, n: values(b, b0, n, 1))],
                    "turn_o": [(1, invert_sums), (2, divide_out)], "project": [(1, add_out)]}
            for t in range(TT):
                stat(0, 0, 0, t)
            for half in range(2):
                moments(0, 0, 0, half)
            dve.wait_ge(w_raw_loaded, 16)
            for k in range(KT):
                for i in range(2):
                    for g in range(NG):
                        src = w_raw[:, k, i * D + g * 64:i * D + (g + 1) * 64].rearrange("p (h d) -> p d h", h=GH)
                        dst = w_qk[:, k, g, i * 64:(i + 1) * 64].rearrange("p (d h) -> p d h", h=GH)
                        dve.tensor_copy(dst, src).then_inc(w_qk_ready, 1)
            for t in range(TT):
                normalise(0, 0, 0, t)
            dve.memset(k_rows[SR:SR + 3, 0:2, :, :], 1.0).then_inc(ones_ready, 1)
            dve.wait_ge(weights_loaded, 16 * (4 + 2 * NG))
            dve.wait_ge(v_filled, 1)
            for i in range(2):
                values(0, 0, 0, i)
            dve.memset(k_rows[SR:SR + 3, 2:NG, :, :], 1.0).then_inc(ones_ready, 1)
            for v in range(AHEAD):
                reduce_tile(0, 0, v)
                if v in (2, 3):
                    values(0, 0, 1, v - 2)

            def body(b, b0):
                todo = body_jobs(b0)
                for u in range(BU):
                    v = BU * b0 + u + AHEAD
                    if v < BU * B:
                        reduce_tile(b, b0, v)
                    for at, kind, n in todo:
                        for delay, use in uses.get(kind, ()):
                            if at + delay == u:
                                use(b, b0, n)
                    if b0 < B - 1:
                        for t in range(TT):
                            if u == 19 + 8 * t:
                                stat(b, b0, b0 + 1, t)
                            if u == 81 + 3 * t:
                                normalise(b, b0, b0 + 1, t)
                        if u in (77, 78):
                            moments(b, b0, b0 + 1, u - 77)
            over_batches(dve, body)
            for _, kind, n in closing:
                for _, use in uses.get(kind, ()):
                    use(B - 1, B - 1, n)

        @block.tensor
        def _(pe):
            def small(b, b0, kind, n):
                key = n % RATE[kind]
                bank = bank_of[kind, key]
                if before[kind, n]:
                    prev, m = before[kind, n]
                    wait(pe, taken[prev], b, RATE[prev], m + 1)
                if kind == "turn_x":
                    if key == 0:
                        wait(pe, xn_ready, b, 1, n // 4 + 1)
                    for j in range(4):
                        k, t = divmod(4 * key + j, TT)
                        last = pe.transpose(ps[:, bank, j * P:(j + 1) * P], x_ln[:, t, k * P:(k + 1) * P], c.ident[:, :])
                elif kind == "qk":
                    G, half = divmod(n, 2)
                    wait(pe, taken["turn_x"], b, 4, 4 * (G // NG + 1))
                    for k in range(KT):
                        last = pe.matmul(ps[:, bank, :], w_qk[:, k, G % NG, :], xn_t[:, k, half * HALF:(half + 1) * HALF],
                                         start=(k == 0), stop=(k == KT - 1))
                elif kind == "v":
                    pair, half = n % NG // 2, n % 2
                    wait(pe, taken["turn_x"], b, 4, 4 * (n // NG + 1))
                    for t in range(TT // 2):
                        for k in range(KT):
                            last = pe.matmul(ps[:, bank, t * P:(t + 1) * P],
                                             xn_t[:, k, (half * (TT // 2) + t) * P:(half * (TT // 2) + t + 1) * P],
                                             w_v[:, k, pair * P:(pair + 1) * P], start=(k == 0), stop=(k == KT - 1))
                elif kind == "turn_max":
                    wait(pe, neg_max_ready, b, NG, n + 1)
                    last = pe.transpose(ps[0:GU // 2, bank, 0:P], neg_max[:, n % 2, :], c.ident[:, :])
                elif kind == "turn_o":
                    if key in (0, TT // 2):
                        wait(pe, o_taken, b, 2 * NG, 2 * NG * (n // TT + 1) - (key == 0))
                    for g in range(NG):
                        last = pe.transpose(ps[:, bank, g * P:(g + 1) * P], o_sb[:, g, key * P:(key + 1) * P], c.ident[:, :])
                elif kind == "turn_ctx":
                    wait(pe, taken["turn_o"], b, TT, n + 1)
                    for k in range(KT):
                        last = pe.transpose(ps[:, bank, k * P:(k + 1) * P], ctx_rows[:, key % 2, k * P:(k + 1) * P], c.ident[:, :])
                else:
                    wait(pe, taken["turn_ctx"], b, TT, n + 1)
                    for k in range(KT):
                        last = pe.matmul(ps[:, bank, 0:D], ctx_t[:, key % 2, k, :], w_o[:, k, :],
                                         start=(k == 0), stop=(k == KT - 1))
                last.then_inc(ready[kind], 1)

            def max_tile(b, b0, v):
                G, w = divmod(v, GU)
                h, t, half = w // (TT * CHUNKS), w // CHUNKS % TT, w % CHUNKS
                g = G % NG
                if w == 0:
                    wait(pe, rows_loaded[g], b, 192, 192 * (G // NG + 1))
                wait(pe, max_tile_taken, b, BU, v - 1)
                pe.matmul(ps[:, v % 2, :], q_rows[0:SR, g, h, t * P:(t + 1) * P],
                          k_rows[0:SR, g, h, half * HALF:(half + 1) * HALF], start=True, stop=True).then_inc(max_tile_ready, 1)

            def score_tile(b, b0, u):
                G, w = divmod(u, GU)
                half, kt, h = w // (TT * GH), w // GH % TT, w % GH
                g = G % NG
                if w == 0:
                    wait(pe, max_loaded[g], b, 48, 48 * (G // NG + 1))
                wait(pe, exp_done, b, BU, u - since(u % BU) + 1)
                pe.matmul(ps[:, score_bank(u % BU), :], k_rows[:, g, h, kt * P:(kt + 1) * P],
                          q_rows[:, g, h, half * HALF:(half + 1) * HALF], start=True, stop=True).then_inc(scores_ready, 1)

            def pv(b, b0, quad, piece):
                window, kt = divmod(quad, TT)
                G = window // CHUNKS
                if piece == 0:
                    wait(pe, exp_done, b, BU, 4 * (quad + 1))
                    if kt == 0:
                        wait(pe, o_taken, b, 2 * NG, window)
                        if window % (2 * CHUNKS) == 0:
                            wait(pe, taken["v"], b, NG, G + 2)
                cols = slice(piece * HALF // 2, (piece + 1) * HALF // 2)
                for h in range(GH):
                    last = pe.matmul(ps[32 * h:32 * h + 32, 5, cols], v_ones[:, G % NG, kt, h, :],
                                     probs[:, quad % NQ, h, cols], start=(kt == 0 and piece == 0), stop=(kt == TT - 1),
                                     skip_group_check=True)
                if piece == 1:
                    last.then_inc(pv_done, 1)

            pe.wait_ge(w_qk_ready, 2 * KT * NG)
            pe.wait_ge(weights_loaded, 16 * (4 + 2 * NG))
            for v in range(AHEAD):
                for at, kind, n in opening:
                    if at == v:
                        small(0, 0, kind, n)
                max_tile(0, 0, v)
            pe.wait_ge(ones_ready, 2)
            pe.wait_ge(v_filled, 1)

            def body(b, b0):
                todo = body_jobs(b0)
                for u in range(BU):
                    for at, kind, n in todo:
                        if at == u:
                            small(b, b0, kind, n)
                    if BU * b0 + u + AHEAD < BU * B:
                        max_tile(b, b0, BU * b0 + u + AHEAD)
                    score_tile(b, b0, BU * b0 + u)
                    for lag in range(2):
                        k = PIECES.get(u % WINDOW + lag * WINDOW)
                        window = (BU * b0 + u) // WINDOW - lag
                        if k is not None and window >= 0:
                            pv(b, b0, TT * window + k // 2, k % 2)
            over_batches(pe, body)
            for at, k in PIECES.items():
                if at >= WINDOW:
                    pv(B - 1, B - 1, TT * (BU * B // WINDOW - 1) + k // 2, k % 2)
            for _, kind, n in closing:
                small(B - 1, B - 1, kind, n)

        @block.scalar
        def _(act):
            def turned_x(b, b0, n):
                f = n % 4
                wait(act, ready["turn_x"], b, 4, n + 1)
                act.activation(xn_t[:, :, :].rearrange("p k t -> p (k t)")[:, f * HALF:(f + 1) * HALF],
                               ps[:, bank_of["turn_x", f], :], ACT.Identity).then_inc(taken["turn_x"], 1)

            def take_qk(b, b0, n):
                G, half = divmod(n, 2)
                g = G % NG
                cols = slice(half * HALF, (half + 1) * HALF)
                bank = ps[:, bank_of["qk", n % RATE["qk"]], :]
                wait(act, ready["qk"], b, 2 * NG, n + 1)
                wait(act, rest_ready, b, NG, G)
                act.activation(qk[:, cols], bank, ACT.Identity, bias=b_qk[:, g:g + 1]).then_inc(qk_whole, 1)

            def first_part(b, b0, n):
                G, half = divmod(n, 2)
                g = G % NG
                cols = slice(half * HALF, (half + 1) * HALF)
                bank = ps[:, bank_of["qk", n % RATE["qk"]], :]
                if G > 0:
                    wait(act, rows_loaded[(G - 1) % NG], b, 192, 192 * ((G - 1) // NG + 1))
                act.activation(parts[:, 0, cols], bank, ACT.Identity, bias=b_qk[:, g:g + 1]).then_inc(part1_ready, 1)

            def second_part(b, b0, G, half):
                cols = slice(half * HALF, (half + 1) * HALF)
                wait(act, rest_ready, b, NG, G + 1)
                act.activation(parts[:, 1, cols], qk_rest[:, cols], ACT.Identity).then_inc(part2_ready, 1)

            def take_max(b, b0, G):
                wait(act, ready["turn_max"], b, NG, G + 1)
                wait(act, max_parts_ready, b, NG, G)
                act.activation(max_whole[:, :], ps[0:GU // 2, bank_of["turn_max", G % NG], 0:P],
                               ACT.Identity).then_inc(taken["turn_max"], 1)

            def take_ctx(b, b0, n):
                qt = n % TT
                wait(act, ready["turn_ctx"], b, TT, n + 1)
                act.activation(ctx_t[:, qt % 2, :, :], ps[:, bank_of["turn_ctx", qt], 0:D].rearrange("p (k q) -> p k q", k=KT),
                               ACT.Identity, scale=float(D) ** -0.5).then_inc(taken["turn_ctx"], 1)

            def take_o(b, b0, window):
                wait(act, pv_done, b, BU // 4, TT * (window + 1))
                g, half = window // CHUNKS % NG, window % CHUNKS
                if g == 0 and window >= 2 * NG:
                    wait(act, ready["turn_o"], b, TT, window // (2 * NG) * TT - TT // 2 * (1 - half))
                act.activation(o_sb[:, g, half * HALF:(half + 1) * HALF], ps[:, 5, :],
                               ACT.Identity).then_inc(o_taken, 1)

            uses = {"turn_x": [(1, turned_x)], "qk": [(1, take_qk), (3, first_part)], "turn_ctx": [(1, take_ctx)],
                    "turn_max": [(1, take_max)]}
            act.wait_ge(weights_loaded, 16 * (4 + 2 * NG))
            for _, kind, n in opening:
                for _, use in uses.get(kind, ()):
                    use(0, 0, n)
                if kind == "qk" and n % 2:
                    for half in range(2):
                        second_part(0, 0, n // 2, half)

            def body(b, b0):
                todo = body_jobs(b0)
                for u in range(BU):
                    U = BU * b0 + u
                    if u % GH == 0:
                        wait(act, pv_done, b, BU // 4, U // GH - NQ + 1)
                    wait(act, scores_ready, b, BU, U + 1)
                    act.activation(probs[:, U // GH % NQ, u % GH, :], ps[:, score_bank(u), :], ACT.Exp).then_inc(exp_done, 1)
                    if u % (TT * GH) == 4 and U >= TT * GH:
                        take_o(b, b0, U // (TT * GH) - 1)
                    for at, kind, n in todo:
                        for delay, use in uses.get(kind, ()):
                            if at + delay == u:
                                use(b, b0, n)
                    for g in range(NG):
                        if u in (QK_AT[g] + 12, QK_AT[g] + 14) and NG * b0 + g + PREP < NG * B:
                            second_part(b, b0, NG * b0 + g + PREP, (u - QK_AT[g] - 12) // 2)
            over_batches(act, body)
            take_o(B - 1, B - 1, 2 * NG * B - 1)
            for _, kind, n in closing:
                for _, use in uses.get(kind, ()):
                    use(B - 1, B - 1, n)

        blocks.close()
        clear(nc, sems)


def build_program(nc, d, out):
    x = d["L0_attn_x"]
    x1 = nc.dram_tensor("after_first_ffn", x.shape, F32, kind="Internal").ap()
    x2 = nc.dram_tensor("after_attention", x.shape, F32, kind="Internal").ap()
    with ExitStack() as ctx:
        ctx.enter_context(nc.allow_non_contiguous_dma(reason="bias vectors, a few hundred elements each, loaded once"))
        c = build_setup(nc, ctx, d)
        build_ffn(nc, c, "ffn1", x, x1, d["L0_ffn_bo"])
        nc.disable_value_cache = True
        build_attention(nc, c, x1, x2, d["L0_attn_W_qkv"], d["L0_attn_b_qkv"], d["L0_attn_W_out"], d["L0_attn_b_out"])
        build_ffn(nc, c, "ffn2", x2, out, d["L0_ffn_bo"])


_INS = ["L0_attn_x", "L0_attn_W_qkv", "L0_attn_b_qkv", "L0_attn_W_out", "L0_attn_b_out", "L0_ffn_slot_init", "L0_ffn_w1",
        "L0_ffn_b1", "L0_ffn_w2", "L0_ffn_b2", "L0_ffn_tau", "L0_ffn_Wih", "L0_ffn_Whh", "L0_ffn_bih", "L0_ffn_bhh",
        "L0_ffn_wq", "L0_ffn_bq", "L0_ffn_wk", "L0_ffn_bk", "L0_ffn_wv", "L0_ffn_bv", "L0_ffn_ln_g", "L0_ffn_ln_b",
        "L0_ffn_wvp", "L0_ffn_bvp", "L0_ffn_wo", "L0_ffn_bo"]


def kernel(**inputs):
    import numpy as np
    import concourse.bacc as bacc
    from concourse.bass_utils import run_bass_kernel_spmd

    nc = bacc.Bacc("TRN2", target_bir_lowering=False, num_devices=1)
    arrays, d = {}, {}
    for name in _INS:
        a = np.ascontiguousarray(inputs[name])
        arrays[f"in_{name}"] = a
        d[name] = nc.dram_tensor(f"in_{name}", a.shape, mybir.dt.from_np(a.dtype), kind="ExternalInput").ap()
    out = nc.dram_tensor("out", inputs["L0_attn_x"].shape, F32, kind="ExternalOutput").ap()
    build_program(nc, d, out)
    r = run_bass_kernel_spmd(nc, [arrays], core_ids=[0])
    return r.results[0]["out"]
```
